# Optimizing a Trainium2 kernel written in Bass

```python
import numpy as np
import jax
import jax.numpy as jnp

def _softmax(x, axis=-1):
    return jax.nn.softmax(x, axis=axis)

def _gelu(x):
    return jax.nn.gelu(x, approximate=True)

def _silu(x):
    return jax.nn.silu(x)

def _sigmoid(x):
    return jax.nn.sigmoid(x)

def _layernorm(x, axis=-1, eps=1e-05):
    m = jnp.mean(x, axis=axis, keepdims=True)
    v = jnp.var(x, axis=axis, keepdims=True)
    return (x - m) / jnp.sqrt(v + eps)

def _scatter_add(tgt, idx, src, axis=0):
    return tgt.at[idx].add(src)

def _segment_sum(src, seg, n):
    return jax.ops.segment_sum(src, seg, n)
kernel_name = 'mk_seq_preln_d1_jaxref_r8_ca4903'

def setup_inputs(seed: int=0):
    np.random.seed(seed)
    _w = jnp.asarray

    def _L0_attn_setup():
        import jax, jax.numpy as jnp
        import numpy as np
        NUM_HEADS = 16
        key = jax.random.key(seed)
        k1, k2, k3 = jax.random.split(key, 3)
        B, T, D = (4, 256, 128)
        x = jax.random.normal(k1, (B, T, D), dtype=jnp.float32)
        w = jax.random.normal(k2, (3 * D, D), dtype=jnp.float32) * (1.0 / np.sqrt(D))
        w_out = jax.random.normal(k3, (D, D), dtype=jnp.float32) * (1.0 / np.sqrt(D))
        return {'x': x, 'w': w, 'w_out': w_out}
    _L0_attn_in = _L0_attn_setup()

    def _L0_ffn_setup():
        import jax, jax.numpy as jnp
        import numpy as np
        DIM = 128
        DEPTH = 6
        HEADS = 16
        DIM_HEAD = 64
        WINDOW = 32
        INNER = HEADS * DIM_HEAD
        DIM_INNER = int(DIM * 4 * 2 / 3)
        QK_SCALE = 8.0

        def shift_tokens(t):
            a, s = jnp.split(t, 2, -1)
            s = jnp.pad(s, ((0, 0), (1, 0), (0, 0)))[:, :-1]
            return jnp.concatenate([a, s], -1)

        def l2norm(t):
            return t / jnp.maximum(jnp.linalg.norm(t, axis=-1, keepdims=True), 1e-12)

        def rotate_half(x):
            x1, x2 = jnp.split(x, 2, -1)
            return jnp.concatenate([-x2, x1], -1)

        def rotary_tables(n):
            half = jnp.arange(0, DIM_HEAD, 2, dtype=jnp.float32)
            inv_freq = 1.0 / 10000.0 ** (half / DIM_HEAD)
            t = jnp.arange(n, dtype=jnp.float32)
            freqs = t[:, None] * inv_freq[None, :]
            freqs = jnp.concatenate([freqs, freqs], -1)
            base_scale = (half + 0.4 * DIM_HEAD) / (1.4 * DIM_HEAD)
            power = (t - n // 2) / (WINDOW // 2)
            scale = base_scale[None, :] ** power[:, None]
            scale = jnp.concatenate([scale, scale], -1)
            return (freqs, scale)

        def local_attention(q, k, v):
            b, h, n, d = q.shape
            w = WINDOW
            nw = n // w
            bq = q.reshape(b, h, nw, w, d)
            bk = k.reshape(b, h, nw, w, d)
            bv = v.reshape(b, h, nw, w, d)

            def look(t):
                p = jnp.pad(t, ((0, 0), (0, 0), (1, 0), (0, 0), (0, 0)))
                return jnp.concatenate([p[:, :, :nw], p[:, :, 1:]], axis=3)
            bk2, bv2 = (look(bk), look(bv))
            seq = jnp.arange(n).reshape(nw, w)
            seq_p = jnp.pad(seq, ((1, 0), (0, 0)), constant_values=-1)
            jt = jnp.concatenate([seq_p[:nw], seq_p[1:]], axis=1)
            it = seq[:, :, None]
            jb = jt[:, None, :]
            mask = (it < jb) | (it > jb + w) | (jb == -1)
            sim = jnp.einsum('bhwie,bhwje->bhwij', bq, bk2) * QK_SCALE
            sim = jnp.where(mask, -jnp.finfo(sim.dtype).max, sim)
            attn = jax.nn.softmax(sim, -1)
            out = jnp.einsum('bhwij,bhwje->bhwie', attn, bv2)
            return out.reshape(b, h, n, d)

        def attn_layer(x, Wqkv, qs, ksc, Wo):
            b, n, _ = x.shape
            qkv = x @ Wqkv
            q, k, v = jnp.split(qkv, 3, -1)
            sh = lambda t: t.reshape(b, n, HEADS, DIM_HEAD).transpose(0, 2, 1, 3)
            q, k, v = (sh(q), sh(k), sh(v))
            q = l2norm(q) * qs
            k = l2norm(k) * ksc
            freqs, scale = rotary_tables(n)
            cos, sin = (jnp.cos(freqs), jnp.sin(freqs))
            q = q * cos * scale + rotate_half(q) * sin * scale
            inv = 1.0 / scale
            k = k * cos * inv + rotate_half(k) * sin * inv
            out = local_attention(q, k, v)
            out = out.transpose(0, 2, 1, 3).reshape(b, n, INNER)
            return out @ Wo

        def ffn_layer(x, g, bln, W1, b1, W2, b2):
            mu = x.mean(-1, keepdims=True)
            var = ((x - mu) ** 2).mean(-1, keepdims=True)
            xn = (x - mu) / jnp.sqrt(var + 1e-05) * g + bln
            hg = xn @ W1 + b1
            a, gate = jnp.split(hg, 2, -1)
            return a * jax.nn.gelu(gate, approximate=False) @ W2 + b2
        key = jax.random.key(seed)
        ks = jax.random.split(key, 8)
        B, N = (2, 256)
        init = lambda k, shape: jax.random.normal(k, shape, jnp.float32) * 0.02
        return {'x': jax.random.normal(ks[0], (B, N, DIM), jnp.float32), 'Wqkv': init(ks[1], (DEPTH, DIM, 3 * INNER)), 'q_scale': jnp.ones((DEPTH, DIM_HEAD), jnp.float32), 'k_scale': jnp.ones((DEPTH, DIM_HEAD), jnp.float32), 'Wo': init(ks[2], (DEPTH, INNER, DIM)), 'ln_g': jnp.ones((DEPTH, DIM), jnp.float32), 'ln_b': jnp.zeros((DEPTH, DIM), jnp.float32), 'W1': init(ks[3], (DEPTH, DIM, 2 * DIM_INNER)), 'b1': jnp.zeros((DEPTH, 2 * DIM_INNER), jnp.float32), 'W2': init(ks[4], (DEPTH, DIM_INNER, DIM)), 'b2': jnp.zeros((DEPTH, DIM), jnp.float32)}
    _L0_ffn_in = _L0_ffn_setup()
    _d = {'L0_attn_x': _L0_attn_in['x'], 'L0_attn_w': _L0_attn_in['w'], 'L0_attn_w_out': _L0_attn_in['w_out'], 'L0_ffn_Wqkv': _L0_ffn_in['Wqkv'], 'L0_ffn_q_scale': _L0_ffn_in['q_scale'], 'L0_ffn_k_scale': _L0_ffn_in['k_scale'], 'L0_ffn_Wo': _L0_ffn_in['Wo'], 'L0_ffn_ln_g': _L0_ffn_in['ln_g'], 'L0_ffn_ln_b': _L0_ffn_in['ln_b'], 'L0_ffn_W1': _L0_ffn_in['W1'], 'L0_ffn_b1': _L0_ffn_in['b1'], 'L0_ffn_W2': _L0_ffn_in['W2'], 'L0_ffn_b2': _L0_ffn_in['b2']}
    _x0 = _d['L0_attn_x']
    _d['L0_attn_x'] = jax.random.normal(jax.random.fold_in(jax.random.key(seed), 1), (16, 256, 128), dtype=_x0.dtype)
    del _x0
    return _d

def reference(L0_attn_x, L0_attn_w, L0_attn_w_out, L0_ffn_Wqkv, L0_ffn_q_scale, L0_ffn_k_scale, L0_ffn_Wo, L0_ffn_ln_g, L0_ffn_ln_b, L0_ffn_W1, L0_ffn_b1, L0_ffn_W2, L0_ffn_b2):

    def _L0_attn_ref(x, w, w_out):
        import jax, jax.numpy as jnp
        import numpy as np
        NUM_HEADS = 16
        B, T, D = x.shape
        H = NUM_HEADS
        L = D // H
        q, k, v = jnp.split(jnp.matmul(x, w.T), 3, axis=2)
        q = q.reshape(B, T, H, L).transpose(1, 0, 2, 3)
        k = k.reshape(B, T, H, L).transpose(1, 0, 2, 3)
        v = v.reshape(B, T, H, L).transpose(1, 0, 2, 3)
        scale = jax.lax.rsqrt(jnp.float32(L))
        k_exp = jnp.exp(k * scale) + 1e-06
        k_norm = jnp.cumsum(k_exp, axis=0)
        qs = jax.nn.softmax(q * scale, axis=-1) / k_norm

        def step(carry, args):
            qs_t, k_t, v_t = args
            carry = carry + k_t[..., :, None] * v_t[..., None, :]
            y_t = jnp.einsum('bhl,bhlm->bhm', qs_t, carry)
            return (carry, y_t)
        init = jnp.zeros((B, H, L, L), dtype=x.dtype)
        _, y = jax.lax.scan(step, init, (qs, k_exp, v))
        y = y.reshape(T, B, D).transpose(1, 0, 2)
        return jnp.matmul(y, w_out)

    def _L0_ffn_ref(x, Wqkv, q_scale, k_scale, Wo, ln_g, ln_b, W1, b1, W2, b2):
        import jax, jax.numpy as jnp
        import numpy as np
        DIM = 128
        DEPTH = 6
        HEADS = 16
        DIM_HEAD = 64
        WINDOW = 32
        INNER = HEADS * DIM_HEAD
        DIM_INNER = int(DIM * 4 * 2 / 3)
        QK_SCALE = 8.0

        def shift_tokens(t):
            a, s = jnp.split(t, 2, -1)
            s = jnp.pad(s, ((0, 0), (1, 0), (0, 0)))[:, :-1]
            return jnp.concatenate([a, s], -1)

        def l2norm(t):
            return t / jnp.maximum(jnp.linalg.norm(t, axis=-1, keepdims=True), 1e-12)

        def rotate_half(x):
            x1, x2 = jnp.split(x, 2, -1)
            return jnp.concatenate([-x2, x1], -1)

        def rotary_tables(n):
            half = jnp.arange(0, DIM_HEAD, 2, dtype=jnp.float32)
            inv_freq = 1.0 / 10000.0 ** (half / DIM_HEAD)
            t = jnp.arange(n, dtype=jnp.float32)
            freqs = t[:, None] * inv_freq[None, :]
            freqs = jnp.concatenate([freqs, freqs], -1)
            base_scale = (half + 0.4 * DIM_HEAD) / (1.4 * DIM_HEAD)
            power = (t - n // 2) / (WINDOW // 2)
            scale = base_scale[None, :] ** power[:, None]
            scale = jnp.concatenate([scale, scale], -1)
            return (freqs, scale)

        def local_attention(q, k, v):
            b, h, n, d = q.shape
            w = WINDOW
            nw = n // w
            bq = q.reshape(b, h, nw, w, d)
            bk = k.reshape(b, h, nw, w, d)
            bv = v.reshape(b, h, nw, w, d)

            def look(t):
                p = jnp.pad(t, ((0, 0), (0, 0), (1, 0), (0, 0), (0, 0)))
                return jnp.concatenate([p[:, :, :nw], p[:, :, 1:]], axis=3)
            bk2, bv2 = (look(bk), look(bv))
            seq = jnp.arange(n).reshape(nw, w)
            seq_p = jnp.pad(seq, ((1, 0), (0, 0)), constant_values=-1)
            jt = jnp.concatenate([seq_p[:nw], seq_p[1:]], axis=1)
            it = seq[:, :, None]
            jb = jt[:, None, :]
            mask = (it < jb) | (it > jb + w) | (jb == -1)
            sim = jnp.einsum('bhwie,bhwje->bhwij', bq, bk2) * QK_SCALE
            sim = jnp.where(mask, -jnp.finfo(sim.dtype).max, sim)
            attn = jax.nn.softmax(sim, -1)
            out = jnp.einsum('bhwij,bhwje->bhwie', attn, bv2)
            return out.reshape(b, h, n, d)

        def attn_layer(x, Wqkv, qs, ksc, Wo):
            b, n, _ = x.shape
            qkv = x @ Wqkv
            q, k, v = jnp.split(qkv, 3, -1)
            sh = lambda t: t.reshape(b, n, HEADS, DIM_HEAD).transpose(0, 2, 1, 3)
            q, k, v = (sh(q), sh(k), sh(v))
            q = l2norm(q) * qs
            k = l2norm(k) * ksc
            freqs, scale = rotary_tables(n)
            cos, sin = (jnp.cos(freqs), jnp.sin(freqs))
            q = q * cos * scale + rotate_half(q) * sin * scale
            inv = 1.0 / scale
            k = k * cos * inv + rotate_half(k) * sin * inv
            out = local_attention(q, k, v)
            out = out.transpose(0, 2, 1, 3).reshape(b, n, INNER)
            return out @ Wo

        def ffn_layer(x, g, bln, W1, b1, W2, b2):
            mu = x.mean(-1, keepdims=True)
            var = ((x - mu) ** 2).mean(-1, keepdims=True)
            xn = (x - mu) / jnp.sqrt(var + 1e-05) * g + bln
            hg = xn @ W1 + b1
            a, gate = jnp.split(hg, 2, -1)
            return a * jax.nn.gelu(gate, approximate=False) @ W2 + b2
        for i in range(DEPTH):
            x = attn_layer(shift_tokens(x), Wqkv[i], q_scale[i], k_scale[i], Wo[i]) + x
            x = ffn_layer(shift_tokens(x), ln_g[i], ln_b[i], W1[i], b1[i], W2[i], b2[i]) + x
        return x
    x = L0_attn_x
    x = x + _L0_attn_ref(_layernorm(x, axis=-1), L0_attn_w, L0_attn_w_out)
    x = x + _L0_ffn_ref(_layernorm(x, axis=-1), L0_ffn_Wqkv, L0_ffn_q_scale, L0_ffn_k_scale, L0_ffn_Wo, L0_ffn_ln_g, L0_ffn_ln_b, L0_ffn_W1, L0_ffn_b1, L0_ffn_W2, L0_ffn_b2)
    return x

_drawn_inputs = setup_inputs


def setup_inputs(seed=0):
    import zlib

    import numpy as np

    out = dict(_drawn_inputs(seed))
    spreads = {'L0_ffn_q_scale': (1.0, 0.6),
     'L0_ffn_k_scale': (1.0, 0.6),
     'L0_ffn_ln_g': (1.0, 0.6),
     'L0_ffn_ln_b': (0.0, 0.8),
     'L0_ffn_b1': (0.0, 0.8),
     'L0_ffn_b2': (0.0, 0.1)}
    factors = {'L0_ffn_W1': 3.661, 'L0_ffn_W2': 3.595}
    for name, (base, spread) in spreads.items():
        noise = np.random.default_rng([zlib.crc32(name.encode()), seed]).standard_normal(out[name].shape)
        drawn = base * np.exp(spread * noise) if base else spread * noise
        out[name] = jnp.asarray(drawn.astype(out[name].dtype))
    for name, factor in factors.items():
        out[name] = (out[name] * factor).astype(out[name].dtype)
    return out
```

```python
from contextlib import ExitStack

import numpy as np

import concourse.bass as bass
from concourse import mybir
from concourse.alu_op_type import AluOpType as ALU

F32 = mybir.dt.float32
F32R = mybir.dt.float32r
BF16 = mybir.dt.bfloat16
I32 = mybir.dt.int32
ACT = mybir.ActivationFunctionType
AX = mybir.AxisListType

P = 128
NB, T, D = 16, 256, 128
NT = T // P
DEPTH, HEADS, DH, WIN = 6, 16, 64, 32
INNER = HEADS * DH
FF = int(D * 4 * 2 / 3)
FFB = [(0, 128), (128, 128), (256, FF - 256)]
LH = 8
NP8 = HEADS // 2
EPS_LN, EPS_L2SQ, EPS_K = 1e-5, 1e-24, 1e-6
RSQRT_SEED = float(0x5F3759DF)
NEWTON = 3
RSQ_STEPS = 3 + 3 * NEWTON
GRP = 2 * T

SLOTS = [
    ("A", "xs", 0), ("C", "wo", 0), ("C", "x1", 0), ("B", "qk", 0), ("A", "proj", 0), ("C", "mean", 0),
    ("A", "proj", 1), ("B", "qk", 1), ("B", "pt", 0), ("A", "proj", 2), ("C", "var", 0), ("B", "qk", 2),
    ("B", "pv", 0), ("A", "proj", 3), ("C", "ln", 0), ("B", "pt", 1), ("A", "proj", 4), ("C", "w1", 0),
    ("B", "qk", 3), ("B", "pv", 1), ("B", "ot", 0), ("A", "proj", 5), ("B", "pt", 2), ("C", "w1", 1),
    ("A", "proj", 6), ("B", "pv", 2), ("B", "ot", 1), ("A", "proj", 7), ("C", "w1", 2), ("A", "norm", 0),
    ("B", "pt", 3), ("A", "v", 0), ("A", "v", 1), ("A", "v", 2), ("A", "v", 3), ("B", "pv", 3),
    ("B", "ot", 2), ("C", "w2", 0), ("A", "tr", 0), ("A", "v", 4), ("A", "tr", 1), ("A", "v", 5),
    ("A", "tr", 2), ("A", "v", 6), ("A", "tr", 3), ("A", "v", 7), ("B", "ot", 3),
    ("A", "tr", 4), ("A", "tr", 5), ("A", "tr", 6), ("A", "tr", 7),
]
PROJ_ORDER = [(k, n) for s, k, n in SLOTS if s == "A" and k in ("proj", "v")]

TRB_ORDER = [(k, n) for s, k, n in SLOTS if s == "B" and k in ("pt", "ot")]


class Count:

    def __init__(self, sem, per):
        self.sem, self.per = sem, per

    def at(self, batch, n):
        return batch * self.per + n


def build(nc, x_in, w_in, w_out_in, Wqkv, q_scale, k_scale, Wo, ln_g, ln_b, W1, b1, W2, b2,
          rotary, masks, ident_in, pick_in, gather_in, seg_in, out):
    ctx = ExitStack()
    with ctx:
        def sb(name, shape, dt=F32):
            return ctx.enter_context(nc.sbuf_tensor(name, shape, dt))

        def ps(name, shape, dt=F32):
            return ctx.enter_context(nc.psum_tensor(name, shape, dt))

        def sem(name):
            return ctx.enter_context(nc.semaphore(name))

        counts = []

        def per_batch(name, per):
            counts.append(Count(sem(name), per))
            return counts[-1]

        X = sb("X", [P, NB * T])
        wqkv_raw = sb("wqkv_raw", [P, 3 * INNER])
        wo_raw = sb("wo_raw", [P, 2 * 4, D])
        w1_raw = sb("w1_raw", [P, 2 * FF])
        w2_raw = sb("w2_raw", [P, 3, D])
        vec_raw = sb("vec_raw", [P, 9])
        qks_raw = sb("qks_raw", [P, 2, DH])
        wqkv_hi = sb("wqkv_hi", [P, 3 * INNER], F32R)
        wqkv_lo = sb("wqkv_lo", [P, 3 * INNER], F32R)
        wo_hi = sb("wo_hi", [P, 8, D], F32R)
        wo_lo = sb("wo_lo", [P, 8, D], F32R)
        w1_hi = sb("w1_hi", [P, 2 * FF], F32R)
        w1_lo = sb("w1_lo", [P, 2 * FF], F32R)
        w2_hi = sb("w2_hi", [P, 3, D], F32R)
        w2_lo = sb("w2_lo", [P, 3, D], F32R)
        vec = sb("vec", [P, 9])
        rot = sb("rot", [P, NT, 4, DH])
        rots = sb("rots", [P, NT, 4, DH])
        ident = sb("ident", [P, P])
        identb = sb("identb", [P, P], BF16)
        mask_f = sb("mask_f", [P, 2, 2 * WIN])
        maskb = sb("maskb", [P, 2, 2 * WIN], BF16)
        mean_w = sb("mean_w", [P, P])
        xraw = sb("xraw", [P, WIN + T])
        xs_hi = sb("xs_hi", [P, T], F32R)
        xs_lo = sb("xs_lo", [P, T], F32R)
        xw_hi = sb("xw_hi", [P, 4, 3 * DH], F32R)
        xw_lo = sb("xw_lo", [P, 4, 3 * DH], F32R)
        sq = sb("sq", [P, 2, 512])
        ropec = sb("ropec", [P, 2, 512])
        ropes = sb("ropes", [P, 2, 512])
        qn = sb("qn", [P, 8, 512])
        ss = sb("ss", [P, 64])
        rsq_i = sb("rsq_i", [P, 64], I32)
        rsq_t = sb("rsq_t", [P, 64])
        rinv = sb("rinv", [P, 64])
        qT = sb("qT", [P, 8, T])
        kT = sb("kT", [P, 8, WIN + T])
        V = sb("V", [P, 4, 2, 4, 2, DH + 1])
        mx = sb("mx", [P, 2, 8])
        Pr = sb("Pr", [P, 2, 512])
        PT = sb("PT", [P, 2, 512])
        rs = sb("rs", [P, 2, 4])
        On = sb("On", [P, 2, 512])
        OT_hi = sb("OT_hi", [P, 8, T], F32R)
        OT_lo = sb("OT_lo", [P, 8, T], F32R)
        xres = sb("xres", [P, T])
        x1 = sb("x1", [P, T])
        xsf = sb("xsf", [P, T])
        dlt = sb("dlt", [P, T])
        dsq = sb("dsq", [P, T])
        lnv = sb("lnv", [P, T])
        lni = sb("lni", [P, T], I32)
        lnt = sb("lnt", [P, T])
        lnr = sb("lnr", [P, T])
        xn = lnv
        xn_hi = sb("xn_hi", [P, T], F32R)
        xn_lo = sb("xn_lo", [P, T], F32R)
        gel, hm = dsq, lnt
        h_hi = sb("h_hi", [P, 3, T], F32R)
        h_lo = sb("h_lo", [P, 3, T], F32R)
        x2 = sb("x2", [P, T])

        bank = [ps(f"bank{i}", [P, 512]) for i in range(6)]
        obank = ps("obank", [P, 2, 512])
        b_proj, b_trA, b_trB, b_sim, b_c = bank[0:2], bank[2], bank[3], bank[4], bank[5]

        qTf = qT[:].rearrange("p a b -> p (a b)")
        kTf = kT[:].rearrange("p a b -> p (a b)")
        Vf = V[:].rearrange("p a b c d e -> p (a b c d e)")
        pick = Vf[:, 0:1024].rearrange("p (m n) -> p m n", m=LH)
        gather = Vf[:, 1024:2048].rearrange("p (m n) -> p m n", m=LH)
        la_w = Vf[:, 2048:2048 + 4 * P].rearrange("p (m n) -> p m n", m=4)
        la_x, la_q, la_k, la_kn = (qTf[:, i * 512:(i + 1) * 512] for i in range(4))
        la_qn, la_v, la_y, la_seg = (kTf[:, i * 512:(i + 1) * 512] for i in range(4))
        la_w_rows = Vf[:, 2560:2560 + 3 * P].rearrange("p (m n) -> p m n", m=3)
        X1 = qn[:].rearrange("p a b -> p (a b)").rearrange("p (t c) -> p t c", c=D)
        ln_tmp = Vf[:, 0:NB * NT * D].rearrange("p (t c) -> p t c", c=D)
        ln_sq = [b[:].rearrange("p a b -> p (a b)").rearrange("p (t c) -> p t c", c=D) for b in (sq, ropec)]
        st = sb("st", [P, 4, 64])

        start = sem("start")
        const_in = sem("const_in")
        x_in_sem = sem("x_in_sem")
        setup = sem("setup")
        ln_step = sem("ln_step")
        ln_sqd = sem("ln_sqd")
        ln_tr = sem("ln_tr")
        ln_cp = sem("ln_cp")
        la_wt = sem("la_wt")
        la_wc = sem("la_wc")
        la_step = per_batch("la_step", 8)
        la_pe = per_batch("la_pe", 6)
        la_act = per_batch("la_act", 4)
        la_xin = per_batch("la_xin", 16)
        la_vb = per_batch("la_vb", 8)
        la_kv = per_batch("la_kv", 8)
        la_sc = per_batch("la_sc", 8)
        la_z = per_batch("la_z", 8)
        la_ym = per_batch("la_ym", 8)
        la_out = per_batch("la_out", 1)
        la_const_in = sem("la_const_in")
        x1_saved = sem("x1_saved")
        x1_back = sem("x1_back")
        fin_tr = sem("fin_tr")
        fin_add = sem("fin_add")
        fin_dma = sem("fin_dma")

        w_in_sem = sem("w_in")
        w_split = sem("w_split")
        sp_held, pe_held = sem("sp_held"), sem("pe_held")
        w_hi_sem = sem("w_hi")
        x_loaded = per_batch("x_loaded", 32)
        xres_loaded = per_batch("xres_loaded", 16)
        x_stored = per_batch("x_stored", 16)
        xs_hi_done = per_batch("xs_hi_done", 1)
        xs_lo_done = per_batch("xs_lo_done", 1)
        proj_full = per_batch("proj_full", 16)
        squared = per_batch("squared", 8)
        roped = per_batch("roped", 8)
        ss_done = per_batch("ss_done", 8)
        rope_sum = per_batch("rope_sum", 8)
        rsq_step = per_batch("rsq_step", RSQ_STEPS)
        normed = per_batch("normed", 8)
        v_copied = per_batch("v_copied", 8)
        trA_full = per_batch("trA_full", 8)
        trA_copied = per_batch("trA_copied", 8)
        sim_full = per_batch("sim_full", 4)
        max_done = per_batch("max_done", 4)
        sim_shift = per_batch("sim_shift", 4)
        p_ready = per_batch("p_ready", 4)
        trB_full = per_batch("trB_full", 8)
        pt_copied = per_batch("pt_copied", 4)
        o_full = per_batch("o_full", 4)
        rs_done = per_batch("rs_done", 4)
        on_done = per_batch("on_done", 4)
        ot_hi_done = per_batch("ot_hi_done", 4)
        ot_lo_done = per_batch("ot_lo_done", 4)
        c_full = per_batch("c_full", 7)
        c_x1 = per_batch("c_x1", 1)
        c_xs = per_batch("c_xs", 1)
        c_d = per_batch("c_d", 1)
        c_dsq = per_batch("c_dsq", 1)
        ln_rsq = per_batch("ln_rsq", 2 + RSQ_STEPS)
        c_xhi = per_batch("c_xhi", 1)
        c_xlo = per_batch("c_xlo", 1)
        c_gelu = per_batch("c_gelu", 3)
        c_h = per_batch("c_h", 3)
        c_hhi = per_batch("c_hhi", 3)
        c_hlo = per_batch("c_hlo", 3)
        c_x2 = per_batch("c_x2", 1)

        out_rows = out.rearrange("b (t p) c -> p (b t) c", p=P)
        block = ctx.enter_context(nc.Block())

        def layer_batches(eng, layer, body):
            first = layer * NB + 1
            body(first, None, None, 0)
            body(first + 1, first, None, 1)
            with eng.Fori(2, NB) as g:
                body(first + g, first + g - 1, first + g - 2, g)
            body(None, first + NB - 1, first + NB - 2, NB)
            body(None, None, first + NB - 1, NB + 1)

        def run_slots(a, b, c, steps):
            for stage, kind, n in SLOTS:
                batch = {"A": a, "B": b, "C": c}[stage]
                step = steps.get((stage, kind))
                if batch is not None and step is not None:
                    step(batch, n)

        def chunk(c):
            return (c // 2) % 2, c % 2, c // 4

        def heads8(ap):
            return ap.rearrange("p (h d) -> p h d", h=8)

        def halves(ap):
            return ap.rearrange("p (h a d) -> p h a d", h=8, a=2)

        UNIT = [(u // 2, u % 2) for u in range(4)]

        def even_odd(ap, e):
            return ap.rearrange("p j (w e q) -> p j w e q", w=2, e=2)[:, :, :, e, :]

        def hold(eng, held, s, value):
            eng.wait_ge(s, value)
            eng.sem_inc(held, 1)

        def bank_free(eng, a, n):
            kind, i = PROJ_ORDER[n - 2]
            batch = a if n >= 2 else a - 1
            s = roped if kind == "proj" else v_copied
            order = i + 1
            eng.wait_ge(s.sem, s.at(batch, order))

        def window_view(n):
            a = xraw[:, 0:T].rearrange("p (w c) -> p w c", w=4)
            return bass.AP(a.tensor, a.offset, [list(a.ap[0]), [2 * WIN, 4], [WIN, n], [1, DH]])

        W_DMAS = 20
        W_SPLIT = 2

        @block.sync
        def _(sp):
            for s in counts:
                sp.sem_inc(s.sem, s.per)
            sp.sem_inc(start, 1)
            for k in range(4):
                rows = slice(8 * k, 8 * k + 8)
                sp.dma_start(X1[:, rows, :], x_in.rearrange("b (t p) c -> p (b t) c", p=P)[:, rows, :]).then_inc(x_in_sem, 16)
            sp.dma_start(ident[:], ident_in).then_inc(const_in, 16)
            sp.dma_start(rot[:], rotary).then_inc(const_in, 16)
            sp.dma_start(mask_f[:], masks).then_inc(const_in, 16)

            def load_weights(layer):
                def col(name, i, src, n=P):
                    sp.dma_start(vec_raw[0:n, i:i + 1], src).then_inc(w_in_sem, 16)
                one = slice(layer, layer + 1) if isinstance(layer, int) else bass.ds(layer, 1)
                sp.dma_start(wqkv_raw[:], Wqkv[one].rearrange("l p n -> p (l n)")).then_inc(w_in_sem, 16)
                for slot in range(2):
                    for par in range(2):
                        src = Wo[one].rearrange("l (j s r p) n -> s r p (l j) n", j=4, s=2, r=2)[slot, par]
                        sp.dma_start(wo_raw[slot * 64:slot * 64 + 64, 4 * par:4 * par + 4, :], src).then_inc(w_in_sem, 16)
                sp.dma_start(w1_raw[:], W1[one].rearrange("l p n -> p (l n)")).then_inc(w_in_sem, 16)
                for j, (f0, n) in enumerate(FFB):
                    sp.dma_start(w2_raw[0:n, j, :], W2[one, f0:f0 + n].rearrange("l p n -> p (l n)")).then_inc(w_in_sem, 16)
                col("g", 0, ln_g[one].rearrange("l p -> p l"))
                col("b", 1, ln_b[one].rearrange("l p -> p l"))
                col("b2", 2, b2[one].rearrange("l p -> p l"))
                for j, (f0, n) in enumerate(FFB):
                    col("b1a", 3 + j, b1[one, f0:f0 + n].rearrange("l p -> p l"), n)
                    col("b1g", 6 + j, b1[one, FF + f0:FF + f0 + n].rearrange("l p -> p l"), n)
                sp.dma_start(qks_raw[:, 0, :], q_scale[one].broadcast_to([P, DH])).then_inc(w_in_sem, 16)
                sp.dma_start(qks_raw[:, 1, :], k_scale[one].broadcast_to([P, DH])).then_inc(w_in_sem, 16)

            load_weights(0)
            sp.wait_ge(ln_cp, 8)
            sp.dma_start(la_w_rows, w_in.rearrange("(m p) c -> p m c", p=P)).then_inc(la_const_in, 16)
            sp.dma_start(la_w[:, 3, :], w_out_in).then_inc(la_const_in, 16)
            sp.dma_start(pick, pick_in).then_inc(la_const_in, 16)
            sp.dma_start(gather, gather_in).then_inc(la_const_in, 16)
            sp.dma_start(la_seg, seg_in).then_inc(la_const_in, 16)
            with sp.Fori(0, NB * T // GRP) as i:
                sp.wait_ge(la_pe.sem, la_pe.at(i, 3))
                sp.dma_start(la_x, X[:, bass.ds(i * GRP, GRP)]).then_inc(la_xin.sem, 16)

            sp.wait_ge(la_out.sem, la_out.at(NB * T // GRP, 1))
            sp.dma_start(out_rows, X1).then_inc(x1_saved, 16)
            sp.wait_ge(ln_cp, 16)

            def body(a, b, c, g):
                if a is not None:
                    sp.wait_ge(xs_lo_done.sem, xs_lo_done.at(a - 1, 1))
                    sp.wait_ge(xs_hi_done.sem, xs_hi_done.at(a - 1, 1))
                    sp.dma_start(xraw[0:64, WIN:WIN + T], X[0:64, bass.ds(g * T, T)]).then_inc(x_loaded.sem, 16)
                    sp.dma_start(xraw[64:P, WIN + 1:WIN + T], X[64:P, bass.ds(g * T, T - 1)]).then_inc(x_loaded.sem, 16)
                if c is not None:
                    sp.wait_ge(c_x1.sem, c_x1.at(c - 1, 1))
                    sp.dma_start(xres[:], X[:, bass.ds((g - 2) * T, T)]).then_inc(xres_loaded.sem, 16)
                    sp.wait_ge(c_x2.sem, c_x2.at(c, 1))
                    sp.dma_start(X[:, bass.ds((g - 2) * T, T)], x2[:]).then_inc(x_stored.sem, 16)

            def layer(layer, prefetch):
                if prefetch:
                    hold(sp, sp_held, w_split, (layer + 1) * W_SPLIT)
                    load_weights(layer + 1)
                layer_batches(sp, layer, body)
                hold(sp, sp_held, x_stored.sem, x_stored.at(layer * NB + NB, 16))

            with sp.Fori(0, DEPTH - 1) as l:
                layer(l, True)
            layer(DEPTH - 1, False)
            sp.wait_ge(trA_full.sem, trA_full.at(DEPTH * NB, 8))
            sp.wait_ge(x1_saved, 16)
            sp.dma_start(X1, out_rows).then_inc(x1_back, 16)
            for k in range(8):
                sp.wait_ge(fin_add, k + 1)
                rows = slice(4 * k, 4 * k + 4)
                sp.dma_start(out_rows[:, rows, :], X1[:, rows, :]).then_inc(fin_dma, 16)
            sp.wait_ge(fin_dma, 8 * 16)

        @block.tensor
        def _(pe):
            pe.wait_ge(start, 1)
            pe.wait_ge(const_in, 3 * 16)

            def rows_to_X(first, norm_steps):
                for k in range(8):
                    pe.wait_ge(ln_step, first + norm_steps[k // 2])
                    if first or k >= 2:
                        pe.wait_ge(ln_cp, (8 if first else 0) + k - 1 if not (first and k < 2) else 8)
                    for t in range(4):
                        mm = pe.transpose(b_proj[k % 2][:, t * P:(t + 1) * P], ln_tmp[:, 4 * k + t, :], ident[:])
                    mm.then_inc(ln_tr, 1)

            rows_to_X(0, LN_DONE)
            pe.wait_ge(la_const_in, 5 * 16)
            for m in range(3):
                mm = pe.transpose(b_sim[:, m * P:(m + 1) * P], la_w_rows[:, m, :], ident[:])
            mm.then_inc(la_wt, 1)
            pe.wait_ge(la_wc, 1)
            with pe.Fori(1, NB * T // GRP + 1) as i:
                pe.wait_ge(la_xin.sem, la_xin.at(i, 16))
                pe.wait_ge(la_step.sem, la_step.at(i - 1, 2))
                for t in range(4):
                    mm = pe.matmul(bank[0][:, t * P:(t + 1) * P], la_x[:, t * P:(t + 1) * P], la_w[:, 0, :], start=True, stop=True)
                mm.then_inc(la_pe.sem, 1)
                pe.wait_ge(la_act.sem, la_act.at(i - 1, 3))
                pe.matmul(bank[1][:], la_w[:, 1, :], la_x, start=True, stop=True).then_inc(la_pe.sem, 1)
                pe.matmul(bank[2][:], la_w[:, 2, :], la_x, start=True, stop=True).then_inc(la_pe.sem, 1)
                pe.wait_ge(la_step.sem, la_step.at(i, 5))
                for t in range(4):
                    mm = pe.transpose(bank[3][:, t * P:(t + 1) * P], la_q[:, t * P:(t + 1) * P], ident[:])
                mm.then_inc(la_pe.sem, 1)

                def vb(m):
                    if m == 0:
                        pe.wait_ge(la_act.sem, la_act.at(i, 3))
                    pe.wait_ge(la_kv.sem, la_kv.at(i - 1, m + 7) if m < 2 else la_kv.at(i, m - 1))
                    pe.matmul(bank[4 + m % 2][:], pick[:, m, :], la_v, start=True, stop=True).then_inc(la_vb.sem, 1)

                vb(0)
                for m in range(LH):
                    if m + 1 < LH:
                        vb(m + 1)
                    pe.wait_ge(la_z.sem, la_z.at(i, m + 1))
                    if m == 0:
                        pe.wait_ge(la_act.sem, la_act.at(i - 1, 4))
                    pe.matmul(obank[:, 0, :], gather[:, m, :], Pr[:, m % 2, :], start=m == 0, stop=m == LH - 1).then_inc(la_ym.sem, 1)
                pe.wait_ge(la_act.sem, la_act.at(i, 4))
                pe.wait_ge(la_out.sem, la_out.at(i - 1, 1))
                for t in range(4):
                    mm = pe.matmul(obank[:, 1, t * P:(t + 1) * P], la_y[:, t * P:(t + 1) * P], la_w[:, 3, :], start=True, stop=True)
                mm.then_inc(la_pe.sem, 2)
            rows_to_X(LN_ALL, LN_DONE)

            def a_proj(a, c):
                kind, hh, t = chunk(c)
                n = PROJ_ORDER.index(("proj", c))
                if c == 0:
                    pe.wait_ge(xs_lo_done.sem, xs_lo_done.at(a, 1))
                bank_free(pe, a, n)
                cols = slice(kind * INNER + hh * 512, kind * INNER + hh * 512 + 512)
                rows = slice(t * P, t * P + P)
                o = b_proj[n % 2][:]
                pe.matmul(o, xs_hi[:, rows], wqkv_hi[:, cols], start=True, stop=False)
                pe.matmul(o, xs_hi[:, rows], wqkv_lo[:, cols], start=False, stop=False)
                pe.matmul(o, xs_lo[:, rows], wqkv_hi[:, cols], start=False, stop=True).then_inc(proj_full.sem, 1)

            def a_v(a, n8):
                wp, mo = n8 // 2, n8 % 2
                n = PROJ_ORDER.index(("v", n8))
                bank_free(pe, a, n)
                keys = slice(DH * mo, DH * mo + P)
                def wv(w):
                    return w[:, 2 * INNER:3 * INNER].rearrange("p (i m c) -> p i m c", i=4, m=2)[:, :, mo, :]
                o = b_proj[n % 2][:].rearrange("p (i c) -> p i c", i=4)
                pe.matmul(o, xw_hi[:, wp, keys], wv(wqkv_hi), start=True, stop=False)
                pe.matmul(o, xw_hi[:, wp, keys], wv(wqkv_lo), start=False, stop=False)
                pe.matmul(o, xw_lo[:, wp, keys], wv(wqkv_hi), start=False, stop=True).then_inc(proj_full.sem, 1)

            def a_tr(a, c):
                pe.wait_ge(normed.sem, normed.at(a, c + 1))
                pe.wait_ge(trA_copied.sem, trA_copied.at(a, c) if c else trA_copied.at(a - 1, 8))
                for j in range(4):
                    mm = pe.transpose(b_trA[:, j * P:(j + 1) * P], qn[:, c, j * P:(j + 1) * P], ident[:])
                mm.then_inc(trA_full.sem, 1)

            def b_qk(b, u):
                t, par = UNIT[u]
                if u == 0:
                    pe.wait_ge(trA_copied.sem, trA_copied.at(b, 8))
                pe.wait_ge(sim_shift.sem, sim_shift.at(b, u) if u else sim_shift.at(b - 1, 4))
                pe.matmul(b_sim[:], identb[:], maskb[:, 1 if t else 0, :].unsqueeze(1).broadcast_to([P, 8, 2 * WIN]),
                          start=True, stop=False, skip_group_check=True)
                for w in range(4):
                    for m in range(8):
                        slot = (m + w) % 2
                        col = (2 * (m // 2) + slot) * 2 * WIN
                        q0 = t * P + w * WIN
                        mm = pe.matmul(b_sim[w * WIN:(w + 1) * WIN, col:col + 2 * WIN],
                                       qT[64 * par:64 * par + 64, m, q0:q0 + WIN],
                                       kT[64 * par:64 * par + 64, m, q0:q0 + 2 * WIN],
                                       start=False, stop=w == 3 and m == 7, skip_group_check=True)
                mm.then_inc(sim_full.sem, 1)

            def b_pt(b, u):
                pe.wait_ge(p_ready.sem, p_ready.at(b, u + 1))
                trB_free(b, "pt", u)
                for j in range(4):
                    mm = pe.transpose(b_trB[:, j * P:(j + 1) * P], Pr[:, u % 2, j * P:(j + 1) * P], ident[:])
                mm.then_inc(trB_full.sem, 1)

            def trB_free(b, kind, u):
                at = TRB_ORDER.index((kind, u))
                k, n = TRB_ORDER[at - 1]
                batch = b if at else b - 1
                if k == "pt":
                    pe.wait_ge(pt_copied.sem, pt_copied.at(batch, n + 1))
                else:
                    pe.wait_ge(ot_lo_done.sem, ot_lo_done.at(batch, n + 1))

            def b_pv(b, u):
                t, par = UNIT[u]
                if u == 0:
                    hold(pe, pe_held, v_copied.sem, v_copied.at(b, 8))
                hold(pe, pe_held, on_done.sem, on_done.at(b, u) if u else on_done.at(b - 1, 4))
                hold(pe, pe_held, pt_copied.sem, pt_copied.at(b, u + 1))
                for w in range(4):
                    for slot in range(2):
                        for j in range(4):
                            rows = slice(64 * slot, 64 * slot + 64)
                            wg = 4 * t + w
                            mm = pe.matmul(obank[w * WIN:(w + 1) * WIN, slot, j * 65:j * 65 + 65],
                                           PT[rows, u % 2, j * P + w * WIN:j * P + (w + 1) * WIN],
                                           V[rows, wg // 2, (slot + w) % 2, j, par, :],
                                           start=True, stop=True, skip_group_check=True)
                mm.then_inc(o_full.sem, 1)

            def b_ot(b, u):
                pe.wait_ge(on_done.sem, on_done.at(b, u + 1))
                trB_free(b, "ot", u)
                for j in range(4):
                    mm = pe.transpose(b_trB[:, j * P:(j + 1) * P], On[:, u % 2, j * P:(j + 1) * P], ident[:])
                mm.then_inc(trB_full.sem, 1)

            def c_wo(c, _):
                pe.wait_ge(ot_lo_done.sem, ot_lo_done.at(c, 4))
                pe.wait_ge(c_x2.sem, c_x2.at(c - 1, 1))
                o = b_c[:, 0:T]
                for i in range(8):
                    pe.matmul(o, wo_hi[:, i, :], OT_hi[:, i, :], start=i == 0, stop=False)
                    pe.matmul(o, wo_hi[:, i, :], OT_lo[:, i, :], start=False, stop=False)
                    mm = pe.matmul(o, wo_lo[:, i, :], OT_hi[:, i, :], start=False, stop=i == 7)
                mm.then_inc(c_full.sem, 1)

            def c_mean(c, _):
                pe.wait_ge(c_x1.sem, c_x1.at(c, 1))
                pe.wait_ge(c_xs.sem, c_xs.at(c, 1))
                pe.matmul(b_c[:, 0:T], mean_w[:], xsf[:], start=True, stop=True).then_inc(c_full.sem, 1)

            def c_var(c, _):
                pe.wait_ge(c_d.sem, c_d.at(c, 1))
                pe.wait_ge(c_dsq.sem, c_dsq.at(c, 1))
                pe.matmul(b_c[:, 0:T], mean_w[:], dsq[:], start=True, stop=True).then_inc(c_full.sem, 1)

            def c_w1(c, j):
                f0, n = FFB[j]
                if j == 0:
                    pe.wait_ge(c_xlo.sem, c_xlo.at(c, 1))
                else:
                    pe.wait_ge(c_h.sem, c_h.at(c, j))
                for part in range(2):
                    o = b_c[0:n, part * T:(part + 1) * T]
                    cols = slice(part * FF + f0, part * FF + f0 + n)
                    pe.matmul(o, w1_hi[:, cols], xn_hi[:], start=True, stop=False)
                    pe.matmul(o, w1_hi[:, cols], xn_lo[:], start=False, stop=False)
                    mm = pe.matmul(o, w1_lo[:, cols], xn_hi[:], start=False, stop=True)
                mm.then_inc(c_full.sem, 1)

            def c_w2(c, _):
                pe.wait_ge(c_hlo.sem, c_hlo.at(c, 3))
                o = b_c[:, 0:T]
                for j, (f0, n) in enumerate(FFB):
                    pe.matmul(o, w2_hi[0:n, j, :], h_hi[0:n, j, :], start=j == 0, stop=False)
                    pe.matmul(o, w2_hi[0:n, j, :], h_lo[0:n, j, :], start=False, stop=False)
                    mm = pe.matmul(o, w2_lo[0:n, j, :], h_hi[0:n, j, :], start=False, stop=j == 2)
                mm.then_inc(c_full.sem, 1)

            steps = {("A", "proj"): a_proj, ("A", "v"): a_v, ("A", "tr"): a_tr, ("B", "qk"): b_qk,
                     ("B", "pt"): b_pt, ("B", "pv"): b_pv, ("B", "ot"): b_ot, ("C", "wo"): c_wo,
                     ("C", "mean"): c_mean, ("C", "var"): c_var, ("C", "w1"): c_w1, ("C", "w2"): c_w2}
            with pe.Fori(0, DEPTH) as l:
                pe.wait_ge(w_split, (l + 1) * W_SPLIT)
                layer_batches(pe, l, lambda a, b, c, g: run_slots(a, b, c, steps))
            pe.wait_ge(x_stored.sem, x_stored.at(DEPTH * NB, 16))
            for k in range(8):
                if k >= 2:
                    pe.wait_ge(fin_add, k - 1)
                for t in range(4):
                    i = 4 * k + t
                    mm = pe.transpose(b_proj[k % 2][:, t * P:(t + 1) * P], X[:, i * P:(i + 1) * P], ident[:])
                mm.then_inc(fin_tr, 1)

        @block.scalar
        def _(act):
            act.wait_ge(start, 1)

            def row_norm(first, marks):
                for k in range(4):
                    act.wait_ge(ln_step, first + LN_SUB[k])
                    act.activation(ln_sq[k % 2], ln_tmp[:, 8 * k:8 * k + 8, :], ACT.Square).then_inc(ln_sqd, 1)
                for k in range(8):
                    act.wait_ge(ln_tr, (8 if first else 0) + k + 1)
                    act.activation(X[:, k * 512:(k + 1) * 512], b_proj[k % 2][:], ACT.Copy).then_inc(ln_cp, 1)

            row_norm(0, None)
            act.wait_ge(la_wt, 1)
            act.activation(la_w[:, 0:3, :], b_sim[:, 0:3 * P].rearrange("p (m n) -> p m n", m=3), ACT.Copy).then_inc(la_wc, 1)
            with act.Fori(1, NB * T // GRP + 1) as i:
                act.wait_ge(la_step.sem, la_step.at(i, 2))
                act.activation(la_q, la_q, ACT.Exp, scale=LH ** -0.5).then_inc(la_act.sem, 1)
                act.wait_ge(la_pe.sem, la_pe.at(i, 2))
                act.wait_ge(la_sc.sem, la_sc.at(i - 1, 8))
                act.activation(la_k, bank[1][:], ACT.Exp, scale=LH ** -0.5).then_inc(la_act.sem, 1)
                act.wait_ge(la_pe.sem, la_pe.at(i, 3))
                act.wait_ge(la_vb.sem, la_vb.at(i - 1, 8))
                act.activation(la_v, bank[2][:], ACT.Copy).then_inc(la_act.sem, 1)
                act.wait_ge(la_ym.sem, la_ym.at(i, 8))
                act.wait_ge(la_pe.sem, la_pe.at(i - 1, 6))
                act.activation(la_y, obank[:, 0, :], ACT.Copy).then_inc(la_act.sem, 1)
            row_norm(LN_ALL, None)

            def a_xs(a, _):
                act.wait_ge(x_loaded.sem, x_loaded.at(a, 32))
                act.wait_ge(proj_full.sem, proj_full.at(a - 1, 16))
                act.activation(xs_hi[:], xraw[:, WIN:WIN + T], ACT.Copy)
                act.activation(xw_hi[:, :, 0:P].rearrange("p w (a c) -> p w a c", a=2), window_view(2), ACT.Copy)
                act.activation(xw_hi[:, :, P:3 * DH], xraw[:, 0:T].rearrange("p (w c) -> p w c", w=4), ACT.Copy).then_inc(xs_hi_done.sem, 1)

            def a_proj(a, c):
                act.wait_ge(proj_full.sem, proj_full.at(a, PROJ_ORDER.index(("proj", c)) + 1))
                act.wait_ge(ss_done.sem, ss_done.at(a, c - 1) if c >= 2 else ss_done.at(a - 1, c + 7))
                act.activation(sq[:, c % 2, :], b_proj[PROJ_ORDER.index(("proj", c)) % 2][:], ACT.Square).then_inc(squared.sem, 1)

            def a_v(a, n8):
                wp, mo = n8 // 2, n8 % 2
                n = PROJ_ORDER.index(("v", n8))
                act.wait_ge(proj_full.sem, proj_full.at(a, n + 1))
                act.wait_ge(o_full.sem, o_full.at(a - 1, 2 if wp < 2 else 4))
                act.activation(V[:, wp, mo, :, :, 0:DH], b_proj[n % 2][:].rearrange("p (i r c) -> p i r c", i=4, r=2),
                               ACT.Copy).then_inc(v_copied.sem, 1)

            def a_tr(a, c):
                kind, hh, t = chunk(c)
                act.wait_ge(trA_full.sem, trA_full.at(a, c + 1))
                if c == 0:
                    act.wait_ge(sim_full.sem, sim_full.at(a - 1, 4))
                pad = WIN if kind else 0
                dst = (kT if kind else qT)[:, 4 * hh:4 * hh + 4, pad + t * P:pad + (t + 1) * P]
                act.activation(dst, b_trA[:].rearrange("p (j q) -> p j q", j=4), ACT.Copy).then_inc(trA_copied.sem, 1)

            def b_qk(b, u):
                act.wait_ge(sim_shift.sem, sim_shift.at(b, u + 1))
                act.activation(Pr[:, u % 2, :], Pr[:, u % 2, :], ACT.Exp, scale=8.0).then_inc(p_ready.sem, 1)

            def b_pt(b, u):
                act.wait_ge(trB_full.sem, trB_full.at(b, TRB_ORDER.index(("pt", u)) + 1))
                act.wait_ge(o_full.sem, o_full.at(b, u - 1) if u >= 2 else o_full.at(b - 1, u + 3))
                act.activation(PT[:, u % 2, :], b_trB[:], ACT.Copy).then_inc(pt_copied.sem, 1)

            def b_ot(b, u):
                t, par = UNIT[u]
                act.wait_ge(trB_full.sem, trB_full.at(b, TRB_ORDER.index(("ot", u)) + 1))
                if u == 0:
                    act.wait_ge(c_full.sem, c_full.at(b - 1, 1))
                src = b_trB[:].rearrange("p (j q) -> p j q", j=4)
                dst = OT_hi[:, 4 * par:4 * par + 4, t * P:(t + 1) * P]
                act.activation(even_odd(dst, 0), even_odd(src, 0), ACT.Copy)
                act.activation(even_odd(dst, 1)[0:64], even_odd(src, 1)[64:P], ACT.Copy)
                act.activation(even_odd(dst, 1)[64:P], even_odd(src, 1)[0:64], ACT.Copy).then_inc(ot_hi_done.sem, 1)

            def c_x1_(c, _):
                act.wait_ge(c_x1.sem, c_x1.at(c, 1))
                act.activation(xsf[0:64, :], x1[0:64, :], ACT.Copy)
                act.activation(xsf[64:P, 1:T], x1[64:P, 0:T - 1], ACT.Copy).then_inc(c_xs.sem, 1)

            def c_mean(c, _):
                act.wait_ge(c_d.sem, c_d.at(c, 1))
                act.activation(dsq[:], dlt[:], ACT.Square).then_inc(c_dsq.sem, 1)

            def c_ln(c, _):
                act.wait_ge(ln_rsq.sem, ln_rsq.at(c, 2 + RSQ_STEPS))
                act.activation(xn_hi[:], xn[:], ACT.Copy).then_inc(c_xhi.sem, 1)

            def c_w1(c, j):
                f0, n = FFB[j]
                act.wait_ge(c_full.sem, c_full.at(c, 4 + j))
                act.activation(gel[0:n, :], b_c[0:n, T:2 * T], ACT.Gelu, bias=vec[0:n, 6 + j:7 + j]).then_inc(c_gelu.sem, 1)
                act.wait_ge(c_h.sem, c_h.at(c, j + 1))
                act.activation(h_hi[0:n, j, :], hm[0:n, :], ACT.Copy).then_inc(c_hhi.sem, 1)

            steps = {("A", "xs"): a_xs, ("A", "proj"): a_proj, ("A", "v"): a_v, ("A", "tr"): a_tr, ("B", "qk"): b_qk,
                     ("B", "pt"): b_pt, ("B", "ot"): b_ot, ("C", "x1"): c_x1_, ("C", "mean"): c_mean,
                     ("C", "ln"): c_ln, ("C", "w1"): c_w1}
            with act.Fori(0, DEPTH) as l:
                act.wait_ge(w_in_sem, (l + 1) * (W_DMAS * 16))
                act.wait_ge(x_stored.sem, x_stored.at(l * NB, 16))
                act.activation(wqkv_hi[:], wqkv_raw[:], ACT.Copy).then_inc(w_hi_sem, 1)
                act.activation(w1_hi[:], w1_raw[:], ACT.Copy).then_inc(w_hi_sem, 1)
                act.activation(wo_hi[:], wo_raw[:], ACT.Copy).then_inc(w_hi_sem, 1)
                act.activation(w2_hi[:, 0:2, :], w2_raw[:, 0:2, :], ACT.Copy)
                act.activation(w2_hi[0:FFB[2][1], 2, :], w2_raw[0:FFB[2][1], 2, :], ACT.Copy).then_inc(w_hi_sem, 1)
                layer_batches(act, l, lambda a, b, c, g: run_slots(a, b, c, steps))

        @block.gpsimd
        def _(pool):
            pool.wait_ge(start, 1)
            with pool.Fori(1, NB * T // GRP + 1) as i:
                for m in range(LH):
                    pool.wait_ge(la_sc.sem, la_sc.at(i, m + 1))
                    pool.wait_ge(la_ym.sem, la_ym.at(i, m - 1) if m >= 2 else la_ym.at(i - 1, m + 7))
                    pool.tensor_tensor(Pr[:, m % 2, :], PT[:, m % 2, :], la_qn, ALU.mult).then_inc(la_z.sem, 1)

            def a_proj(a, c):
                pool.wait_ge(roped.sem, roped.at(a, c + 1))
                pool.wait_ge(trA_full.sem, trA_full.at(a - 1, c + 1))
                pool.tensor_tensor(qn[:, c, :], ropec[:, c % 2, :], ropes[:, c % 2, :], ALU.add).then_inc(rope_sum.sem, 1)

            def a_norm(a, _):
                pool.wait_ge(rsq_step.sem, rsq_step.at(a, RSQ_STEPS))
                pool.wait_ge(rope_sum.sem, rope_sum.at(a, 8))
                for c in range(8):
                    pool.tensor_tensor(heads8(qn[:, c, :]), heads8(qn[:, c, :]),
                                       rinv[:, 8 * c:8 * c + 8].unsqueeze(2).broadcast_to([P, 8, DH]),
                                       ALU.mult).then_inc(normed.sem, 1)

            steps = {("A", "proj"): a_proj, ("A", "norm"): a_norm}
            pool.wait_ge(x1_saved, 16)
            with pool.Fori(0, DEPTH) as l:
                layer_batches(pool, l, lambda a, b, c, g: run_slots(a, b, c, steps))

        @block.vector
        def _(dve):
            dve.wait_ge(start, 1)
            dve.wait_ge(const_in, 3 * 16)
            dve.tensor_copy(identb[:], ident[:])
            dve.tensor_copy(maskb[:], mask_f[:])
            dve.memset(mean_w[:], 1.0 / D)
            dve.memset(xraw[:, 0:WIN + 1], 0.0)
            dve.memset(xsf[64:P, 0:1], 0.0).then_inc(setup, 1)

            n_ln = [0]

            def link(ins):
                n_ln[0] += 1
                ins.then_inc(ln_step, 1)
                dve.wait_ge(ln_step, n_ln[0])

            def rsqrt(step, wait, src, seed, tmp, dst):
                step(dve.tensor_scalar(seed, src.bitcast(I32), 1, None, ALU.logical_shift_right))
                wait()
                step(dve.tensor_scalar(dst.bitcast(I32), seed, -1.0, RSQRT_SEED, ALU.mult, ALU.add))
                for _ in range(NEWTON):
                    wait()
                    step(dve.scalar_tensor_tensor(tmp, dst, -0.5, dst, ALU.mult, ALU.mult))
                    wait()
                    step(dve.tensor_tensor(tmp, tmp, src, ALU.mult))
                    wait()
                    step(dve.scalar_tensor_tensor(dst, tmp, 1.5, dst, ALU.add, ALU.mult))

            def row_norm(first):
                for k in range(4):
                    t8 = slice(8 * k, 8 * k + 8)
                    s, v, r = (st[:, j, 0:8] for j in range(3))
                    i_ = rsq_i[:, 0:8]
                    if not first:
                        dve.wait_ge(x_in_sem, 16 * (k + 1))
                    elif k == 0:
                        dve.wait_ge(la_out.sem, la_out.at(NB * T // GRP, 1))
                    link(dve.tensor_reduce(s, X1[:, t8, :], AX.X, ALU.add))
                    link(dve.tensor_scalar(s, s, -1.0 / D, None, ALU.mult))
                    link(dve.tensor_tensor(ln_tmp[:, t8, :], X1[:, t8, :], s.unsqueeze(2).broadcast_to([P, 8, D]), ALU.add))
                    dve.wait_ge(ln_sqd, (4 if first else 0) + k + 1)
                    link(dve.tensor_reduce(v, ln_sq[k % 2], AX.X, ALU.add))
                    link(dve.tensor_scalar(v, v, 1.0 / D, EPS_LN, ALU.mult, ALU.add))
                    rsqrt(link, lambda: None, v, i_, s, r)
                    link(dve.tensor_tensor(ln_tmp[:, t8, :], ln_tmp[:, t8, :], r.unsqueeze(2).broadcast_to([P, 8, D]), ALU.mult))

            row_norm(0)
            assert n_ln[0] == LN_ALL
            dve.wait_ge(la_wc, 1)
            with dve.Fori(1, NB * T // GRP + 1) as i:
                q3 = la_q.rearrange("p (h l) -> p h l", l=LH)
                m64, s64 = st[:, 0, :], st[:, 1, :]

                def own(n):
                    dve.wait_ge(la_step.sem, la_step.at(i, n))
                dve.wait_ge(la_pe.sem, la_pe.at(i, 1))
                b3 = bank[0][:].rearrange("p (h l) -> p h l", l=LH)
                dve.tensor_reduce(m64, b3, AX.X, ALU.max).then_inc(la_step.sem, 1)
                own(1)
                dve.wait_ge(la_pe.sem, la_pe.at(i - 1, 4))
                dve.tensor_tensor(q3, b3, m64.unsqueeze(2).broadcast_to([P, 64, LH]), ALU.subtract).then_inc(la_step.sem, 1)
                dve.wait_ge(la_act.sem, la_act.at(i, 1))
                dve.tensor_reduce(s64, q3, AX.X, ALU.add).then_inc(la_step.sem, 1)
                own(3)
                dve.reciprocal(s64, s64).then_inc(la_step.sem, 1)
                own(4)
                dve.tensor_tensor(q3, q3, s64.unsqueeze(2).broadcast_to([P, 64, LH]), ALU.mult).then_inc(la_step.sem, 1)
                dve.wait_ge(la_act.sem, la_act.at(i, 2))
                dve.tensor_scalar(la_k, la_k, EPS_K, None, ALU.add).then_inc(la_step.sem, 1)
                own(6)
                dve.tensor_tensor_scan(la_kn, la_seg, la_k, 0.0, ALU.mult, ALU.add).then_inc(la_step.sem, 1)
                own(7)
                dve.reciprocal(la_kn, la_kn).then_inc(la_step.sem, 1)
                own(8)
                dve.wait_ge(la_pe.sem, la_pe.at(i, 4))
                dve.wait_ge(la_z.sem, la_z.at(i - 1, 8))
                dve.tensor_tensor(la_qn, bank[3][:], la_kn, ALU.mult)
                for m in range(LH):
                    dve.wait_ge(la_vb.sem, la_vb.at(i, m + 1))
                    dve.tensor_tensor(On[:, m % 2, :], bank[4 + m % 2][:], la_k, ALU.mult).then_inc(la_kv.sem, 1)
                    dve.wait_ge(la_kv.sem, la_kv.at(i, m + 1))
                    dve.wait_ge(la_z.sem, la_z.at(i, m - 1) if m >= 2 else la_z.at(i - 1, m + 7))
                    dve.tensor_tensor_scan(PT[:, m % 2, :], la_seg, On[:, m % 2, :], 0.0, ALU.mult, ALU.add).then_inc(la_sc.sem, 1)
                dve.wait_ge(la_pe.sem, la_pe.at(i, 6))
                rows = X1[:, bass.ds((i - 1) * 4, 4), :]
                dve.tensor_tensor(rows, rows, obank[:, 1, :].rearrange("p (t c) -> p t c", c=D), ALU.add).then_inc(la_out.sem, 1)
            row_norm(1)
            dve.wait_ge(ln_tr, 16)
            dve.memset(kT[:, :, 0:WIN], 0.0)
            dve.memset(V[:, :, :, :, :, DH:DH + 1], 1.0).then_inc(setup, 1)

            def a_xs(a, _):
                dve.wait_ge(xs_hi_done.sem, xs_hi_done.at(a, 1))
                dve.tensor_tensor(xs_lo[:], xraw[:, WIN:WIN + T], xs_hi[:].bitcast(F32), ALU.subtract)
                dve.tensor_tensor(xw_lo[:, :, 0:P].rearrange("p w (a c) -> p w a c", a=2), window_view(2),
                                  xw_hi[:, :, 0:P].bitcast(F32).rearrange("p w (a c) -> p w a c", a=2), ALU.subtract)
                dve.tensor_tensor(xw_lo[:, :, P:3 * DH], xraw[:, 0:T].rearrange("p (w c) -> p w c", w=4),
                                  xw_hi[:, :, P:3 * DH].bitcast(F32), ALU.subtract).then_inc(xs_lo_done.sem, 1)

            def a_proj(a, c):
                kind, hh, t = chunk(c)
                b_ = b_proj[PROJ_ORDER.index(("proj", c)) % 2][:]
                dve.wait_ge(squared.sem, squared.at(a, c + 1))
                dve.wait_ge(rope_sum.sem, rope_sum.at(a, c - 1) if c >= 2 else rope_sum.at(a - 1, c + 7))
                cos = rots[:, t, 2 * kind, :].rearrange("p (a d) -> p a d", a=2).unsqueeze(1).broadcast_to([P, 8, 2, DH // 2])
                sin = rots[:, t, 2 * kind + 1, :].rearrange("p (a d) -> p a d", a=2).unsqueeze(1).broadcast_to([P, 8, 2, DH // 2])
                dve.tensor_tensor(halves(ropec[:, c % 2, :]), halves(b_), cos, ALU.mult)
                dve.tensor_tensor(halves(ropes[:, c % 2, :]), halves(b_)[:, :, ::-1, :], sin, ALU.mult).then_inc(roped.sem, 1)
                if c == 0:
                    dve.wait_ge(rsq_step.sem, rsq_step.at(a - 1, RSQ_STEPS))
                dve.tensor_reduce(ss[:, 8 * c:8 * c + 8], heads8(sq[:, c % 2, :]), AX.X, ALU.add).then_inc(ss_done.sem, 1)

            def a_norm(a, _):
                n = [0]

                def step(ins):
                    n[0] += 1
                    ins.then_inc(rsq_step.sem, 1)

                def wait():
                    dve.wait_ge(rsq_step.sem, rsq_step.at(a, n[0]))
                dve.wait_ge(ss_done.sem, ss_done.at(a, 8))
                step(dve.tensor_scalar(ss[:], ss[:], EPS_L2SQ, None, ALU.max))
                wait()
                dve.wait_ge(normed.sem, normed.at(a - 1, 8))
                rsqrt(step, wait, ss[:], rsq_i[:], rsq_t[:], rinv[:])
                assert n[0] == RSQ_STEPS

            def b_qk(b, u):
                dve.wait_ge(sim_full.sem, sim_full.at(b, u + 1))
                s3 = heads8(b_sim[:])
                dve.tensor_reduce(mx[:, u % 2, :], s3, AX.X, ALU.max).then_inc(max_done.sem, 1)
                dve.wait_ge(max_done.sem, max_done.at(b, u + 1))
                dve.wait_ge(trB_full.sem, trB_full.at(b, TRB_ORDER.index(("pt", u - 2)) + 1) if u >= 2
                            else trB_full.at(b - 1, TRB_ORDER.index(("pt", u + 2)) + 1))
                dve.tensor_tensor(heads8(Pr[:, u % 2, :]), s3, mx[:, u % 2, :].unsqueeze(2).broadcast_to([P, 8, 2 * WIN]),
                                  ALU.subtract).then_inc(sim_shift.sem, 1)

            def b_pv(b, u):
                dve.wait_ge(o_full.sem, o_full.at(b, u + 1))
                o4 = obank[:, :, 0:4 * 65].rearrange("p s (j c) -> p s j c", j=4)
                dve.reciprocal(rs[:], o4[:, :, :, DH]).then_inc(rs_done.sem, 1)
                dve.wait_ge(rs_done.sem, rs_done.at(b, u + 1))
                dve.wait_ge(trB_full.sem, trB_full.at(b, TRB_ORDER.index(("ot", u - 2)) + 1) if u >= 2
                            else trB_full.at(b - 1, TRB_ORDER.index(("ot", u + 2)) + 1))
                dve.tensor_tensor(On[:, u % 2, :].rearrange("p (j s c) -> p s j c", j=4, s=2), o4[:, :, :, 0:DH],
                                  rs[:].unsqueeze(3).broadcast_to([P, 2, 4, DH]), ALU.mult).then_inc(on_done.sem, 1)

            def b_ot(b, u):
                t, par = UNIT[u]
                dve.wait_ge(ot_hi_done.sem, ot_hi_done.at(b, u + 1))
                src = b_trB[:].rearrange("p (j q) -> p j q", j=4)
                hi = OT_hi[:, 4 * par:4 * par + 4, t * P:(t + 1) * P].bitcast(F32)
                lo = OT_lo[:, 4 * par:4 * par + 4, t * P:(t + 1) * P]
                dve.tensor_tensor(even_odd(lo, 0), even_odd(src, 0), even_odd(hi, 0), ALU.subtract)
                dve.tensor_tensor(even_odd(lo, 1)[0:64], even_odd(src, 1)[64:P], even_odd(hi, 1)[0:64], ALU.subtract)
                dve.tensor_tensor(even_odd(lo, 1)[64:P], even_odd(src, 1)[0:64], even_odd(hi, 1)[64:P],
                                  ALU.subtract).then_inc(ot_lo_done.sem, 1)

            def c_x1_(c, _):
                dve.wait_ge(c_full.sem, c_full.at(c, 1))
                dve.wait_ge(xres_loaded.sem, xres_loaded.at(c, 16))
                dve.wait_ge(c_x2.sem, c_x2.at(c - 1, 1))
                dve.tensor_tensor(x1[:], b_c[:, 0:T], xres[:], ALU.add).then_inc(c_x1.sem, 1)

            def c_mean(c, _):
                dve.wait_ge(c_full.sem, c_full.at(c, 2))
                dve.tensor_tensor(dlt[:], xsf[:], b_c[:, 0:T], ALU.subtract).then_inc(c_d.sem, 1)

            def c_var(c, _):
                dve.wait_ge(c_full.sem, c_full.at(c, 3))
                dve.tensor_scalar(lnv[:], b_c[:, 0:T], EPS_LN, None, ALU.add).then_inc(ln_rsq.sem, 1)

            def c_ln(c, _):
                n = [1]

                def step(ins):
                    n[0] += 1
                    ins.then_inc(ln_rsq.sem, 1)

                def wait():
                    dve.wait_ge(ln_rsq.sem, ln_rsq.at(c, n[0]))
                wait()
                rsqrt(step, wait, lnv[:], lni[:], lnt[:], lnr[:])
                wait()
                step(dve.tensor_tensor(lnt[:], dlt[:], lnr[:], ALU.mult))
                wait()
                dve.tensor_scalar(xn[:], lnt[:], vec[:, 0:1], vec[:, 1:2], ALU.mult, ALU.add).then_inc(ln_rsq.sem, 1)
                dve.wait_ge(c_xhi.sem, c_xhi.at(c, 1))
                dve.tensor_tensor(xn_lo[:], xn[:], xn_hi[:].bitcast(F32), ALU.subtract).then_inc(c_xlo.sem, 1)

            def c_w1(c, j):
                f0, n = FFB[j]
                dve.wait_ge(c_gelu.sem, c_gelu.at(c, j + 1))
                if j:
                    dve.wait_ge(c_hlo.sem, c_hlo.at(c, j))
                dve.scalar_tensor_tensor(hm[0:n, :], b_c[0:n, 0:T], vec[0:n, 3 + j:4 + j], gel[0:n, :],
                                         ALU.add, ALU.mult).then_inc(c_h.sem, 1)
                dve.wait_ge(c_hhi.sem, c_hhi.at(c, j + 1))
                dve.tensor_tensor(h_lo[0:n, j, :], hm[0:n, :], h_hi[0:n, j, :].bitcast(F32), ALU.subtract).then_inc(c_hlo.sem, 1)

            def c_w2(c, _):
                dve.wait_ge(c_full.sem, c_full.at(c, 7))
                dve.wait_ge(x_stored.sem, x_stored.at(c - 1, 16))
                dve.scalar_tensor_tensor(x2[:], b_c[:, 0:T], vec[:, 2:3], x1[:], ALU.add, ALU.add).then_inc(c_x2.sem, 1)

            steps = {("A", "xs"): a_xs, ("A", "proj"): a_proj, ("A", "norm"): a_norm, ("B", "qk"): b_qk,
                     ("B", "pv"): b_pv, ("B", "ot"): b_ot, ("C", "x1"): c_x1_, ("C", "mean"): c_mean,
                     ("C", "var"): c_var, ("C", "ln"): c_ln, ("C", "w1"): c_w1, ("C", "w2"): c_w2}
            with dve.Fori(0, DEPTH) as l:
                dve.wait_ge(w_in_sem, (l + 1) * (W_DMAS * 16))
                dve.wait_ge(x_stored.sem, x_stored.at(l * NB, 16))
                for kind, s in enumerate((0, 1)):
                    sc = qks_raw[:, s, :]
                    sw = sc.rearrange("p (a d) -> p a d", a=2)[:, ::-1, :].unsqueeze(1).broadcast_to([P, NT, 2, DH // 2])
                    dve.tensor_tensor(rots[:, :, 2 * kind, :], rot[:, :, 2 * kind, :], sc.unsqueeze(1).broadcast_to([P, NT, DH]), ALU.mult)
                    dve.tensor_tensor(rots[:, :, 2 * kind + 1, :].rearrange("p t (a d) -> p t a d", a=2),
                                      rot[:, :, 2 * kind + 1, :].rearrange("p t (a d) -> p t a d", a=2), sw, ALU.mult)
                dve.tensor_copy(vec[:, 0:5], vec_raw[:, 0:5])
                dve.tensor_copy(vec[0:FFB[2][1], 5:6], vec_raw[0:FFB[2][1], 5:6])
                dve.tensor_copy(vec[:, 6:8], vec_raw[:, 6:8])
                dve.tensor_copy(vec[0:FFB[2][1], 8:9], vec_raw[0:FFB[2][1], 8:9]).then_inc(w_split, 1)
                dve.wait_ge(w_hi_sem, l * 4 + 1)
                dve.tensor_tensor(wqkv_lo[:], wqkv_raw[:], wqkv_hi[:].bitcast(F32), ALU.subtract)
                dve.wait_ge(w_hi_sem, l * 4 + 4)
                dve.tensor_tensor(w1_lo[:], w1_raw[:], w1_hi[:].bitcast(F32), ALU.subtract)
                dve.tensor_tensor(wo_lo[:], wo_raw[:], wo_hi[:].bitcast(F32), ALU.subtract)
                dve.tensor_tensor(w2_lo[:, 0:2, :], w2_raw[:, 0:2, :], w2_hi[:, 0:2, :].bitcast(F32), ALU.subtract)
                dve.tensor_tensor(w2_lo[0:FFB[2][1], 2, :], w2_raw[0:FFB[2][1], 2, :],
                                  w2_hi[0:FFB[2][1], 2, :].bitcast(F32), ALU.subtract).then_inc(w_split, 1)
                layer_batches(dve, l, lambda a, b, c, g: run_slots(a, b, c, steps))
            dve.wait_ge(x1_back, 16)
            for k in range(8):
                dve.wait_ge(fin_tr, k + 1)
                rows = X1[:, 4 * k:4 * k + 4, :]
                dve.tensor_tensor(rows, rows, b_proj[k % 2][:].rearrange("p (t c) -> p t c", c=D), ALU.add).then_inc(fin_add, 1)


LN_PER = 5 + (2 + 3 * NEWTON) + 1
LN_ALL = 4 * LN_PER
LN_SUB = [LN_PER * k + 3 for k in range(4)]
LN_DONE = [LN_PER * (k + 1) for k in range(4)]


def shape_constants():
    f = np.float32
    half = np.arange(0, DH, 2, dtype=f)
    inv_freq = (f(1.0) / f(10000.0) ** (half / f(DH))).astype(f)
    t = np.arange(T, dtype=f)
    freqs = (t[:, None] * inv_freq[None, :]).astype(f)
    freqs = np.concatenate([freqs, freqs], -1).astype(np.float64)
    base = ((half + f(0.4 * DH)) / f(1.4 * DH)).astype(f)
    power = ((t - T // 2) / f(WIN // 2)).astype(f)
    scale = base[None, :].astype(np.float64) ** power[:, None].astype(np.float64)
    scale = np.concatenate([scale, scale], -1)
    sign = np.where(np.arange(DH) < DH // 2, -1.0, 1.0)[None, :]
    cos, sin = np.cos(freqs), np.sin(freqs) * sign
    tab = np.stack([cos * scale, sin * scale, cos / scale, sin / scale], 1)
    rotary = tab.reshape(NT, P, 4, DH).transpose(1, 0, 2, 3).astype(f)
    masks = np.zeros((P, 2, 2 * WIN), f)
    i = np.arange(P) % WIN
    j = np.arange(WIN)
    masks[:, :, WIN:] = np.where(j[None, :] > i[:, None], f(-1e30), f(0))[:, None, :]
    masks[:, :, :WIN] = np.where(j[None, :] < i[:, None], f(-1e30), f(0))[:, None, :]
    masks[0:WIN, 0, 0:WIN] = f(-1e30)
    ident = np.eye(P, dtype=f)
    pick = np.zeros((P, LH, P), f)
    for m in range(LH):
        for h in range(HEADS):
            pick[h * LH + m, m, h * LH:(h + 1) * LH] = 1
    gather = np.ascontiguousarray(pick.transpose(2, 1, 0))
    seg = np.ones((P, GRP), f)
    seg[:, ::T] = 0
    return {"c_rotary": rotary, "c_masks": masks, "c_ident": ident, "c_pick": pick, "c_gather": gather, "c_seg": seg}


_INS = ["L0_attn_x", "L0_attn_w", "L0_attn_w_out", "L0_ffn_Wqkv", "L0_ffn_q_scale", "L0_ffn_k_scale", "L0_ffn_Wo",
        "L0_ffn_ln_g", "L0_ffn_ln_b", "L0_ffn_W1", "L0_ffn_b1", "L0_ffn_W2", "L0_ffn_b2"]


def kernel(**inputs):
    import concourse.bacc as bacc
    from concourse.bass_utils import run_bass_kernel_spmd

    nc = bacc.Bacc("TRN2", target_bir_lowering=False, num_devices=1)
    arrays, args = {}, []
    for name, a in [(n, inputs[n]) for n in _INS] + list(shape_constants().items()):
        a = np.ascontiguousarray(a)
        arrays[name] = a
        args.append(nc.dram_tensor(name, a.shape, mybir.dt.from_np(a.dtype), kind="ExternalInput").ap())
    args.append(nc.dram_tensor("out", (NB, T, D), F32, kind="ExternalOutput").ap())
    build(nc, *args)
    r = run_bass_kernel_spmd(nc, [arrays], core_ids=[0])
    return r.results[0]["out"]
```

```python
from contextlib import ExitStack

import numpy as np

import concourse.bass as bass
from concourse import mybir
from concourse.alu_op_type import AluOpType as ALU

F32 = mybir.dt.float32
F32R = mybir.dt.float32r
BF16 = mybir.dt.bfloat16
I32 = mybir.dt.int32
ACT = mybir.ActivationFunctionType
AX = mybir.AxisListType

P = 128
NB, T, D = 16, 256, 128
NT = T // P
DEPTH, HEADS, DH, WIN = 6, 16, 64, 32
INNER = HEADS * DH
FF = int(D * 4 * 2 / 3)
FFB = [(0, 128), (128, 128), (256, FF - 256)]
LH = 8
NP8 = HEADS // 2
EPS_LN, EPS_L2SQ, EPS_K = 1e-5, 1e-24, 1e-6
RSQRT_SEED = float(0x5F3759DF)
NEWTON = 3
RSQ_STEPS = 3 + 3 * NEWTON
GRP = 2 * T

ORDER = {
    "pe": """
        tr.6' wo.0'' tr.7' proj.0 proj.1 qk.0' proj.2 proj.3 mean.0'' qk.1' pt.0' proj.4 pv.0' qk.2' ot.0'
        var.0'' proj.5 proj.6 pt.1' proj.7 pv.1' v.0 v.1 ot.1' qk.3' pt.2' v.2 pv.2' ln.0'' tr.0 v.3 tr.1 w1.0''
        ot.2' tr.2 w1.1'' tr.3 pt.3' v.4 tr.4 v.5 pv.3' w1.2'' v.6 tr.5 ot.3' v.7 w2.0'' """,
    "act": """
        xs.0 tr.6' tr.7' proj.0 proj.1 x1.0'' qk.0' proj.2 pt.0' proj.3 mean.0'' proj.4 qk.1' ot.0' proj.5 pt.1'
        proj.6 proj.7 qk.2' ot.1' v.0 pt.2' v.1 v.2 tr.0 v.3 qk.3' tr.1 w1.0'' tr.2 ot.2' tr.3 pt.3' w1.1'' tr.4
        v.4 v.5 w1.2'' tr.5 ot.3' v.6 v.7 """,
    "dve": """
        xs.0 x1.0'' proj.0 qk.0' sums.0 sums.1 proj.1 proj.2 qk.1' sums.2 mean.0'' proj.3 pv.0' sums.3 qk.2'
        sums.4 var.0'' proj.4 proj.5 sums.5 sums.6 pv.1' sums.7 rsqrt.0 qk.3' norm.1 ln.0'' proj.6 pv.2' proj.7
        w1.0'' norm.3 w1.1'' norm.5 pv.3' w1.2'' norm.7 w2.0'' """,
    "pool": """
        proj.0 proj.1 proj.2 proj.3 proj.4 proj.5 norm.0 norm.2 proj.6 proj.7 norm.4 norm.6 """,
}


def order(engine):
    for word in ORDER[engine].split():
        kind, i = word.rstrip("'").split(".")
        yield kind, int(i), word.count("'")


def fills(*kinds):
    return [(k, i) for lag in range(3) for k, i, g in order("pe") if g == lag and k in kinds]


PROJ_ORDER = fills("proj", "v")
TRB_ORDER = fills("pt", "ot")


class Count:

    def __init__(self, sem, per):
        self.sem, self.per = sem, per

    def at(self, batch, n):
        return batch * self.per + n


def build(nc, x_in, w_in, w_out_in, Wqkv, q_scale, k_scale, Wo, ln_g, ln_b, W1, b1, W2, b2,
          rotary, masks, ident_in, pick_in, gather_in, seg_in, out):
    ctx = ExitStack()
    with ctx:
        def sb(name, shape, dt=F32):
            return ctx.enter_context(nc.sbuf_tensor(name, shape, dt))

        def ps(name, shape, dt=F32):
            return ctx.enter_context(nc.psum_tensor(name, shape, dt))

        def sem(name):
            return ctx.enter_context(nc.semaphore(name))

        counts = []

        def per_batch(name, per):
            counts.append(Count(sem(name), per))
            return counts[-1]

        X = sb("X", [P, NB * T])
        wqkv_raw = sb("wqkv_raw", [P, 3 * INNER])
        wo_raw = sb("wo_raw", [P, 2 * 4, D])
        w1_raw = sb("w1_raw", [P, 2 * FF])
        w2_raw = sb("w2_raw", [P, 3, D])
        vec_raw = sb("vec_raw", [P, 9])
        qks_raw = sb("qks_raw", [P, 2, DH])
        wqkv_hi = sb("wqkv_hi", [P, 3 * INNER], F32R)
        wqkv_lo = sb("wqkv_lo", [P, 3 * INNER], F32R)
        wo = sb("wo", [P, 8, D])
        w1 = sb("w1", [P, 2 * FF])
        w2 = sb("w2", [P, 3, D])
        vec = sb("vec", [P, 9])
        rot = sb("rot", [P, NT, 4, DH])
        rots = sb("rots", [P, NT, 4, DH])
        ident = sb("ident", [P, P])
        identb = sb("identb", [P, P], BF16)
        mask_f = sb("mask_f", [P, 2, 2 * WIN])
        maskb = sb("maskb", [P, 2, 2 * WIN], BF16)
        mean_w = sb("mean_w", [P, P])
        xraw = sb("xraw", [P, WIN + T])
        xs_hi = sb("xs_hi", [P, T], F32R)
        xs_lo = sb("xs_lo", [P, T], F32R)
        xw_hi = sb("xw_hi", [P, 4, 3 * DH], F32R)
        xw_lo = sb("xw_lo", [P, 4, 3 * DH], F32R)
        qraw = sb("qraw", [P, 3, 512])
        sq = sb("sq", [P, 2, 512])
        ropec = sb("ropec", [P, 2, 512])
        ropes = sb("ropes", [P, 2, 512])
        qn = sb("qn", [P, 8, 512])
        ss = sb("ss", [P, 64 + NT])
        rsq_i = sb("rsq_i", [P, 64 + NT], I32)
        rsq_t = sb("rsq_t", [P, 64 + NT])
        rinv = sb("rinv", [P, 64 + NT])
        qT = sb("qT", [P, 8, T])
        kT = sb("kT", [P, 8, WIN + T])
        V = sb("V", [P, 4, 2, 4, 2, DH + 1])
        mx = sb("mx", [P, 2, 8])
        Pr = sb("Pr", [P, 2, 512])
        PT = sb("PT", [P, 2, 512])
        rs = sb("rs", [P, 2, 4])
        On = sb("On", [P, 2, 512])
        OT = sb("OT", [P, 8, T])
        xres = sb("xres", [P, T])
        x1 = sb("x1", [P, T])
        xsf = sb("xsf", [P, T])
        dlt = sb("dlt", [P, T])
        dsq = sb("dsq", [P, T])
        lnt = sb("lnt", [P, T])
        xn = sb("xn", [P, T])
        gel = sb("gel", [P, 2, T])
        hm = sb("hm", [P, 3, T])
        x2 = sb("x2", [P, T])

        bank = [ps(f"bank{i}", [P, 512]) for i in range(6)]
        obank = ps("obank", [P, 2, 512])
        b_proj, b_trA, b_trB, b_sim, b_c = bank[0:2], bank[2], bank[3], bank[4], bank[5]

        qTf = qT[:].rearrange("p a b -> p (a b)")
        kTf = kT[:].rearrange("p a b -> p (a b)")
        Vf = V[:].rearrange("p a b c d e -> p (a b c d e)")
        pick = Vf[:, 0:1024].rearrange("p (m n) -> p m n", m=LH)
        gather = Vf[:, 1024:2048].rearrange("p (m n) -> p m n", m=LH)
        la_w = Vf[:, 2048:2048 + 4 * P].rearrange("p (m n) -> p m n", m=4)
        OTf = OT[:].rearrange("p a b -> p (a b)")
        la_x, la_q, la_kn, la_y = (qTf[:, i * 512:(i + 1) * 512] for i in range(4))
        la_k = [kTf[:, i * 512:(i + 1) * 512] for i in range(2)]
        la_v = [OTf[:, i * 512:(i + 1) * 512] for i in range(2)]
        la_qn = [OTf[:, 1024:1536], OTf[:, 1536:2048]]
        la_seg = kTf[:, 1024:1536]
        la_w_rows = Vf[:, 2560:2560 + 3 * P].rearrange("p (m n) -> p m n", m=3)
        X1 = qn[:].rearrange("p a b -> p (a b)").rearrange("p (t c) -> p t c", c=D)
        ln_tmp = Vf[:, 0:NB * NT * D].rearrange("p (t c) -> p t c", c=D)
        ln_sq = [b[:].rearrange("p a b -> p (a b)").rearrange("p (t c) -> p t c", c=D) for b in (sq, ropec)]
        st = sb("st", [P, 4, 64])

        start = sem("start")
        const_in = sem("const_in")
        x_in_sem = sem("x_in_sem")
        setup = sem("setup")
        ln_step = sem("ln_step")
        ln_sqd = sem("ln_sqd")
        ln_tr = sem("ln_tr")
        ln_cp = sem("ln_cp")
        la_wt = sem("la_wt")
        la_wc = sem("la_wc")
        la_step = per_batch("la_step", 9)
        la_pe = per_batch("la_pe", 4)
        la_act = per_batch("la_act", 3)
        la_yc = per_batch("la_yc", 1)
        la_po = per_batch("la_po", 1)
        la_xin = per_batch("la_xin", 16)
        la_vb = per_batch("la_vb", 8)
        la_kv = per_batch("la_kv", 8)
        la_sc = per_batch("la_sc", 8)
        la_z = per_batch("la_z", 8)
        la_ym = per_batch("la_ym", 8)
        la_out = per_batch("la_out", 1)
        la_const_in = sem("la_const_in")
        x1_saved = sem("x1_saved")
        x1_back = sem("x1_back")
        fin_tr = sem("fin_tr")
        fin_add = sem("fin_add")
        fin_dma = sem("fin_dma")

        w_in_sem = sem("w_in")
        w_hi = sem("w_hi")
        w_lo = sem("w_lo")
        w_c = sem("w_c")
        sp_held, pe_held = sem("sp_held"), sem("pe_held")
        x_loaded = per_batch("x_loaded", 32)
        xres_loaded = per_batch("xres_loaded", 16)
        x_stored = per_batch("x_stored", 16)
        xs_hi_done = per_batch("xs_hi_done", 1)
        xs_lo_done = per_batch("xs_lo_done", 1)
        proj_full = per_batch("proj_full", 16)
        raw_copied = per_batch("raw_copied", 8)
        squared = per_batch("squared", 8)
        roped = per_batch("roped", 8)
        ropes_done = per_batch("ropes_done", 8)
        ss_done = per_batch("ss_done", 8)
        rope_sum = per_batch("rope_sum", 8)
        rsq_step = per_batch("rsq_step", RSQ_STEPS)
        normed_p = per_batch("normed_p", 4)
        normed_v = per_batch("normed_v", 4)
        v_copied = per_batch("v_copied", 8)
        trA_full = per_batch("trA_full", 8)
        trA_copied = per_batch("trA_copied", 8)
        sim_full = per_batch("sim_full", 4)
        max_done = per_batch("max_done", 4)
        sim_shift = per_batch("sim_shift", 4)
        p_ready = per_batch("p_ready", 4)
        trB_full = per_batch("trB_full", 8)
        pt_copied = per_batch("pt_copied", 4)
        o_full = per_batch("o_full", 4)
        rs_done = per_batch("rs_done", 4)
        on_done = per_batch("on_done", 4)
        ot_copied = per_batch("ot_copied", 4)
        c_full = per_batch("c_full", 8)
        c_x1 = per_batch("c_x1", 1)
        c_xs = per_batch("c_xs", 1)
        c_d = per_batch("c_d", 1)
        c_dsq = per_batch("c_dsq", 1)
        c_var = per_batch("c_var", 1)
        c_ln = per_batch("c_ln", 2)
        c_gelu = per_batch("c_gelu", 3)
        c_h = per_batch("c_h", 3)
        c_x2 = per_batch("c_x2", 1)

        out_rows = out.rearrange("b (t p) c -> p (b t) c", p=P)
        block = ctx.enter_context(nc.Block())

        LA_STEPS = NB * T // GRP

        def la_pipeline(eng, head, channels):
            for piece in head(1, 1):
                piece()
            with eng.Fori(0, LA_STEPS // 2 - 1) as j:
                channels(2 * j + 1, 1, head(2 * j + 2, 0))
                channels(2 * j + 2, 0, head(2 * j + 3, 1))
            channels(LA_STEPS - 1, 1, head(LA_STEPS, 0))
            channels(LA_STEPS, 0, [])

        def pipeline(eng, body, conv_a=None, conv_c=None, loads=None):
            conv_a and conv_a(0)
            body(1, 0, (0,), 0)
            body(2, 1, (0, 1), None)
            conv_c and conv_c(0)
            with eng.Fori(0, DEPTH - 1) as l:
                loads and loads(l + 1)
                with eng.Fori(2, NB) as g:
                    body(l * NB + g + 1, g, (0, 1, 2), None)
                conv_a and conv_a(l + 1)
                body(l * NB + NB + 1, 0, (0, 1, 2), l + 1)
                body(l * NB + NB + 2, 1, (0, 1, 2), None)
                conv_c and conv_c(l + 1)
            last = (DEPTH - 1) * NB
            with eng.Fori(2, NB) as g:
                body(last + g + 1, g, (0, 1, 2), None)
            body(last + NB + 1, 0, (1, 2), None)
            body(last + NB + 2, 1, (2,), None)

        def run_slots(engine, n, g, lags, layer, steps):
            for kind, i, lag in order(engine):
                step = steps.get(kind)
                if step is None:
                    continue
                if kind == "rsqrt":
                    step(n, 0 in lags, 2 in lags)
                elif lag in lags:
                    if kind in ("proj", "v"):
                        step(n - lag, i, layer)
                    elif kind == "ln":
                        step(n - lag, n)
                    else:
                        step(n - lag, i)

        def chunk(c):
            return (c // 2) % 2, c % 2, c // 4

        def heads8(ap):
            return ap.rearrange("p (h d) -> p h d", h=8)

        def halves(ap):
            return ap.rearrange("p (h a d) -> p h a d", h=8, a=2)

        def ring3(c):
            return RING3[c]

        def table(t, i):
            return rots[:, t, i, :].rearrange("p (a d) -> p a d", a=2).unsqueeze(1).broadcast_to([P, 8, 2, DH // 2])

        def normalise(eng, c):
            return eng.tensor_tensor(heads8(qn[:, c, :]), heads8(qn[:, c, :]),
                                     rinv[:, 8 * c:8 * c + 8].unsqueeze(2).broadcast_to([P, 8, DH]), ALU.mult)

        RING3 = [0, 1, 2, 0, 1, 2, 0, 1]
        UNIT = [(u // 2, u % 2) for u in range(4)]

        def even_odd(ap, e):
            return ap.rearrange("p j (w e q) -> p j w e q", w=2, e=2)[:, :, :, e, :]

        def hold(eng, held, s, value):
            eng.wait_ge(s, value)
            eng.sem_inc(held, 1)

        def bank_free(eng, a, n):
            kind, i = PROJ_ORDER[n - 2]
            s = raw_copied if kind == "proj" else v_copied
            eng.wait_ge(s.sem, s.at(a if n >= 2 else a - 1, i + 1))

        def window_view(n):
            a = xraw[:, 0:T].rearrange("p (w c) -> p w c", w=4)
            return bass.AP(a.tensor, a.offset, [list(a.ap[0]), [2 * WIN, 4], [WIN, n], [1, DH]])

        W_DMAS = 20
        W_THIRD = INNER

        @block.sync
        def _(sp):
            for s in counts:
                sp.sem_inc(s.sem, s.per)
            sp.sem_inc(start, 1)
            for k in range(4):
                rows = slice(8 * k, 8 * k + 8)
                sp.dma_start(X1[:, rows, :], x_in.rearrange("b (t p) c -> p (b t) c", p=P)[:, rows, :]).then_inc(x_in_sem, 16)
            sp.dma_start(ident[:], ident_in).then_inc(const_in, 16)
            sp.dma_start(rot[:], rotary).then_inc(const_in, 16)
            sp.dma_start(mask_f[:], masks).then_inc(const_in, 16)

            def load_weights(layer):
                def col(name, i, src, n=P):
                    sp.dma_start(vec_raw[0:n, i:i + 1], src).then_inc(w_in_sem, 16)
                one = slice(layer, layer + 1) if isinstance(layer, int) else bass.ds(layer, 1)
                sp.dma_start(wqkv_raw[:], Wqkv[one].rearrange("l p n -> p (l n)")).then_inc(w_in_sem, 16)
                for slot in range(2):
                    for par in range(2):
                        src = Wo[one].rearrange("l (j s r p) n -> s r p (l j) n", j=4, s=2, r=2)[slot, par]
                        sp.dma_start(wo_raw[slot * 64:slot * 64 + 64, 4 * par:4 * par + 4, :], src).then_inc(w_in_sem, 16)
                sp.dma_start(w1_raw[:], W1[one].rearrange("l p n -> p (l n)")).then_inc(w_in_sem, 16)
                for j, (f0, n) in enumerate(FFB):
                    sp.dma_start(w2_raw[0:n, j, :], W2[one, f0:f0 + n].rearrange("l p n -> p (l n)")).then_inc(w_in_sem, 16)
                col("g", 0, ln_g[one].rearrange("l p -> p l"))
                col("b", 1, ln_b[one].rearrange("l p -> p l"))
                col("b2", 2, b2[one].rearrange("l p -> p l"))
                for j, (f0, n) in enumerate(FFB):
                    col("b1a", 3 + j, b1[one, f0:f0 + n].rearrange("l p -> p l"), n)
                    col("b1g", 6 + j, b1[one, FF + f0:FF + f0 + n].rearrange("l p -> p l"), n)
                sp.dma_start(qks_raw[:, 0, :], q_scale[one].broadcast_to([P, DH])).then_inc(w_in_sem, 16)
                sp.dma_start(qks_raw[:, 1, :], k_scale[one].broadcast_to([P, DH])).then_inc(w_in_sem, 16)

            load_weights(0)
            sp.wait_ge(ln_cp, 8)
            sp.dma_start(la_w_rows, w_in.rearrange("(m p) c -> p m c", p=P)).then_inc(la_const_in, 16)
            sp.dma_start(la_w[:, 3, :], w_out_in).then_inc(la_const_in, 16)
            sp.dma_start(pick, pick_in).then_inc(la_const_in, 16)
            sp.dma_start(gather, gather_in).then_inc(la_const_in, 16)
            sp.dma_start(la_seg, seg_in).then_inc(la_const_in, 16)
            with sp.Fori(0, NB * T // GRP) as i:
                sp.wait_ge(la_pe.sem, la_pe.at(i, 3))
                sp.dma_start(la_x, X[:, bass.ds(i * GRP, GRP)]).then_inc(la_xin.sem, 16)

            sp.wait_ge(la_out.sem, la_out.at(NB * T // GRP, 1))
            sp.dma_start(out_rows, X1).then_inc(x1_saved, 16)
            sp.wait_ge(ln_cp, 16)

            def place(g):
                return bass.ds(g * T, T)

            def load_x(g):
                sp.dma_start(xraw[0:64, WIN:WIN + T], X[0:64, place(g)]).then_inc(x_loaded.sem, 16)
                sp.dma_start(xraw[64:P, WIN + 1:WIN + T], X[64:P, bass.ds(g * T, T - 1)]).then_inc(x_loaded.sem, 16)

            def body(n, g, lags, layer):
                c = n - 2
                has_a, has_b, has_c = (lag in lags for lag in (0, 1, 2))
                if has_b:
                    if has_c:
                        sp.wait_ge(c_x1.sem, c_x1.at(c, 1))
                    sp.dma_start(xres[:], X[:, place(wrap(g - 1))]).then_inc(xres_loaded.sem, 16)
                if has_a:
                    sp.wait_ge(xs_lo_done.sem, xs_lo_done.at(n, 1))
                    load_x(wrap(g + 1))
                if has_c:
                    sp.wait_ge(c_x2.sem, c_x2.at(c, 1))
                    sp.dma_start(X[:, place(wrap(g - 2))], x2[:]).then_inc(x_stored.sem, 16)

            def wrap(g):
                if isinstance(g, int):
                    return g % NB
                return (g + NB) % NB

            def loads(layer):
                hold(sp, sp_held, w_lo, 3 * layer)
                hold(sp, sp_held, w_c, layer)
                load_weights(layer)

            load_x(0)
            pipeline(sp, body, loads=loads)
            sp.wait_ge(x_stored.sem, x_stored.at(DEPTH * NB, 16))
            sp.wait_ge(x_loaded.sem, x_loaded.at(DEPTH * NB + 1, 32))
            sp.wait_ge(trA_full.sem, trA_full.at(DEPTH * NB, 8))
            sp.wait_ge(x1_saved, 16)
            sp.dma_start(X1, out_rows).then_inc(x1_back, 16)
            for k in range(8):
                sp.wait_ge(fin_add, k + 1)
                rows = slice(4 * k, 4 * k + 4)
                sp.dma_start(out_rows[:, rows, :], X1[:, rows, :]).then_inc(fin_dma, 16)
            sp.wait_ge(fin_dma, 8 * 16)

        @block.tensor
        def _(pe):
            pe.wait_ge(start, 1)
            pe.wait_ge(const_in, 3 * 16)

            def rows_to_X(first, norm_steps):
                for k in range(8):
                    pe.wait_ge(ln_step, first + norm_steps[k // 2])
                    if first or k >= 2:
                        pe.wait_ge(ln_cp, (8 if first else 0) + k - 1 if not (first and k < 2) else 8)
                    for t in range(4):
                        mm = pe.transpose(b_proj[k % 2][:, t * P:(t + 1) * P], ln_tmp[:, 4 * k + t, :], ident[:])
                    mm.then_inc(ln_tr, 1)

            rows_to_X(0, LN_DONE)
            pe.wait_ge(la_const_in, 5 * 16)
            for m in range(3):
                mm = pe.transpose(b_sim[:, m * P:(m + 1) * P], la_w_rows[:, m, :], ident[:])
            mm.then_inc(la_wt, 1)
            pe.wait_ge(la_wc, 1)

            def la_head(i, b):
                def q():
                    pe.wait_ge(la_xin.sem, la_xin.at(i, 16))
                    pe.wait_ge(la_step.sem, la_step.at(i - 1, 2))
                    for t in range(4):
                        mm = pe.matmul(bank[0][:, t * P:(t + 1) * P], la_x[:, t * P:(t + 1) * P], la_w[:, 0, :], start=True, stop=True)
                    mm.then_inc(la_pe.sem, 1)

                def kv():
                    pe.wait_ge(la_act.sem, la_act.at(i - 1, 3))
                    pe.matmul(bank[1][:], la_w[:, 1, :], la_x, start=True, stop=True).then_inc(la_pe.sem, 1)
                    pe.matmul(bank[2][:], la_w[:, 2, :], la_x, start=True, stop=True).then_inc(la_pe.sem, 1)

                def q_columns():
                    pe.wait_ge(la_step.sem, la_step.at(i, 5))
                    pe.wait_ge(la_step.sem, la_step.at(i - 1, 9))
                    for t in range(4):
                        mm = pe.transpose(bank[3][:, t * P:(t + 1) * P], la_q[:, t * P:(t + 1) * P], ident[:])
                    mm.then_inc(la_pe.sem, 1)
                return [q, kv, q_columns]

            def la_channels(i, b, head):
                after = dict(zip((0, 1, 5), head))

                def vb(m):
                    if m == 0:
                        pe.wait_ge(la_act.sem, la_act.at(i, 3))
                    pe.wait_ge(la_kv.sem, la_kv.at(i - 1, m + 7) if m < 2 else la_kv.at(i, m - 1))
                    pe.matmul(bank[4 + m % 2][:], pick[:, m, :], la_v[b], start=True, stop=True).then_inc(la_vb.sem, 1)

                vb(0)
                vb(1)
                for m in range(LH):
                    m in after and after[m]()
                    if m + 2 < LH:
                        vb(m + 2)
                    pe.wait_ge(la_z.sem, la_z.at(i, m + 1))
                    if m == 0:
                        pe.wait_ge(la_yc.sem, la_yc.at(i - 1, 1))
                    pe.matmul(obank[:, 0, :], gather[:, m, :], Pr[:, m % 2, :], start=m == 0, stop=m == LH - 1).then_inc(la_ym.sem, 1)
                pe.wait_ge(la_yc.sem, la_yc.at(i, 1))
                pe.wait_ge(la_out.sem, la_out.at(i - 1, 1))
                for t in range(4):
                    mm = pe.matmul(obank[:, 1, t * P:(t + 1) * P], la_y[:, t * P:(t + 1) * P], la_w[:, 3, :], start=True, stop=True)
                mm.then_inc(la_po.sem, 1)

            la_pipeline(pe, la_head, la_channels)
            rows_to_X(LN_ALL, LN_DONE)

            def a_proj(a, c, layer):
                kind, hh, t = chunk(c)
                n = PROJ_ORDER.index(("proj", c))
                if layer is not None and c in (0, 2):
                    pe.wait_ge(w_lo, 3 * layer + c // 2 + 1)
                if c == 0:
                    pe.wait_ge(xs_lo_done.sem, xs_lo_done.at(a, 1))
                bank_free(pe, a, n)
                cols = slice(kind * INNER + hh * 512, kind * INNER + hh * 512 + 512)
                rows = slice(t * P, t * P + P)
                o = b_proj[n % 2][:]
                pe.matmul(o, xs_hi[:, rows], wqkv_hi[:, cols], start=True, stop=False)
                pe.matmul(o, xs_hi[:, rows], wqkv_lo[:, cols], start=False, stop=False)
                pe.matmul(o, xs_lo[:, rows], wqkv_hi[:, cols], start=False, stop=True).then_inc(proj_full.sem, 1)

            def a_v(a, n8, layer):
                wp, mo = n8 // 2, n8 % 2
                n = PROJ_ORDER.index(("v", n8))
                if layer is not None and n8 == 0:
                    pe.wait_ge(w_lo, 3 * layer + 3)
                bank_free(pe, a, n)
                keys = slice(DH * mo, DH * mo + P)
                def wv(w):
                    return w[:, 2 * INNER:3 * INNER].rearrange("p (i m c) -> p i m c", i=4, m=2)[:, :, mo, :]
                o = b_proj[n % 2][:].rearrange("p (i c) -> p i c", i=4)
                pe.matmul(o, xw_hi[:, wp, keys], wv(wqkv_hi), start=True, stop=False)
                pe.matmul(o, xw_hi[:, wp, keys], wv(wqkv_lo), start=False, stop=False)
                pe.matmul(o, xw_lo[:, wp, keys], wv(wqkv_hi), start=False, stop=True).then_inc(proj_full.sem, 1)

            def a_tr(a, c):
                s = (normed_p, normed_v)[c % 2]
                pe.wait_ge(s.sem, s.at(a, c // 2 + 1))
                pe.wait_ge(trA_copied.sem, trA_copied.at(a, c) if c else trA_copied.at(a - 1, 8))
                for j in range(4):
                    mm = pe.transpose(b_trA[:, j * P:(j + 1) * P], qn[:, c, j * P:(j + 1) * P], ident[:])
                mm.then_inc(trA_full.sem, 1)

            def b_qk(b, u):
                t, par = UNIT[u]
                if u == 0:
                    pe.wait_ge(trA_copied.sem, trA_copied.at(b, 8))
                pe.wait_ge(sim_shift.sem, sim_shift.at(b, u) if u else sim_shift.at(b - 1, 4))
                pe.matmul(b_sim[:], identb[:], maskb[:, 1 if t else 0, :].unsqueeze(1).broadcast_to([P, 8, 2 * WIN]),
                          start=True, stop=False, skip_group_check=True)
                for w in range(4):
                    for m in range(8):
                        slot = (m + w) % 2
                        col = (2 * (m // 2) + slot) * 2 * WIN
                        q0 = t * P + w * WIN
                        mm = pe.matmul(b_sim[w * WIN:(w + 1) * WIN, col:col + 2 * WIN],
                                       qT[64 * par:64 * par + 64, m, q0:q0 + WIN],
                                       kT[64 * par:64 * par + 64, m, q0:q0 + 2 * WIN],
                                       start=False, stop=w == 3 and m == 7, skip_group_check=True)
                mm.then_inc(sim_full.sem, 1)

            def b_pt(b, u):
                pe.wait_ge(p_ready.sem, p_ready.at(b, u + 1))
                trB_free(b, "pt", u)
                for j in range(4):
                    mm = pe.transpose(b_trB[:, j * P:(j + 1) * P], Pr[:, u % 2, j * P:(j + 1) * P], ident[:])
                mm.then_inc(trB_full.sem, 1)

            def trB_free(b, kind, u):
                at = TRB_ORDER.index((kind, u))
                k, n = TRB_ORDER[at - 1]
                batch = b if at else b - 1
                if k == "pt":
                    pe.wait_ge(pt_copied.sem, pt_copied.at(batch, n + 1))
                else:
                    pe.wait_ge(ot_copied.sem, ot_copied.at(batch, n + 1))

            def b_pv(b, u):
                t, par = UNIT[u]
                if u == 0:
                    hold(pe, pe_held, v_copied.sem, v_copied.at(b, 8))
                hold(pe, pe_held, on_done.sem, on_done.at(b, u) if u else on_done.at(b - 1, 4))
                hold(pe, pe_held, pt_copied.sem, pt_copied.at(b, u + 1))
                for w in range(4):
                    for slot in range(2):
                        for j in range(4):
                            rows = slice(64 * slot, 64 * slot + 64)
                            wg = 4 * t + w
                            mm = pe.matmul(obank[w * WIN:(w + 1) * WIN, slot, j * 65:j * 65 + 65],
                                           PT[rows, u % 2, j * P + w * WIN:j * P + (w + 1) * WIN],
                                           V[rows, wg // 2, (slot + w) % 2, j, par, :],
                                           start=True, stop=True, skip_group_check=True)
                mm.then_inc(o_full.sem, 1)

            def b_ot(b, u):
                pe.wait_ge(on_done.sem, on_done.at(b, u + 1))
                trB_free(b, "ot", u)
                for j in range(4):
                    mm = pe.transpose(b_trB[:, j * P:(j + 1) * P], On[:, u % 2, j * P:(j + 1) * P], ident[:])
                mm.then_inc(trB_full.sem, 1)

            def c_wo(c, _):
                pe.wait_ge(ot_copied.sem, ot_copied.at(c, 4))
                pe.wait_ge(c_x2.sem, c_x2.at(c - 1, 1))
                for i in range(8):
                    mm = pe.matmul(b_c[:, 0:T], wo[:, i, :], OT[:, i, :], start=i == 0, stop=i == 7)
                mm.then_inc(c_full.sem, 1)

            def c_mean(c, _):
                pe.wait_ge(c_x1.sem, c_x1.at(c, 1))
                pe.wait_ge(c_xs.sem, c_xs.at(c, 1))
                pe.matmul(b_c[:, 0:T], mean_w[:], xsf[:], start=True, stop=True).then_inc(c_full.sem, 1)

            def c_var_(c, _):
                pe.wait_ge(c_d.sem, c_d.at(c, 1))
                pe.wait_ge(c_dsq.sem, c_dsq.at(c, 1))
                for t in range(NT):
                    mm = pe.matmul(b_c[:, t:t + 1], dsq[:, t * P:(t + 1) * P], mean_w[:, 0:1], start=True, stop=True)
                mm.then_inc(c_full.sem, 1)

            def c_ln_(c, n):
                pe.wait_ge(rsq_step.sem, rsq_step.at(n, RSQ_STEPS))
                for t in range(NT):
                    mm = pe.matmul(b_c[:, t * P:(t + 1) * P], rinv[:, 64 + t:65 + t].broadcast_to([P, P]), ident[:],
                                   start=True, stop=True)
                mm.then_inc(c_full.sem, 1)

            def c_w1(c, j):
                f0, n = FFB[j]
                if j == 0:
                    pe.wait_ge(c_ln.sem, c_ln.at(c, 2))
                else:
                    pe.wait_ge(c_h.sem, c_h.at(c, j))
                for part in range(2):
                    cols = slice(part * FF + f0, part * FF + f0 + n)
                    mm = pe.matmul(b_c[0:n, part * T:(part + 1) * T], w1[:, cols], xn[:], start=True, stop=True)
                mm.then_inc(c_full.sem, 1)

            def c_w2(c, _):
                pe.wait_ge(c_h.sem, c_h.at(c, 3))
                for j, (f0, n) in enumerate(FFB):
                    mm = pe.matmul(b_c[:, 0:T], w2[0:n, j, :], hm[0:n, j, :], start=j == 0, stop=j == 2)
                mm.then_inc(c_full.sem, 1)

            steps = {"proj": a_proj, "v": a_v, "tr": a_tr, "qk": b_qk,
                     "pt": b_pt, "pv": b_pv, "ot": b_ot, "wo": c_wo,
                     "mean": c_mean, "var": c_var_, "ln": c_ln_, "w1": c_w1, "w2": c_w2}

            def conv_c(layer):
                pe.wait_ge(w_c, layer + 1)

            pipeline(pe, lambda *z: run_slots("pe", *z, steps), conv_c=conv_c)
            pe.wait_ge(x_stored.sem, x_stored.at(DEPTH * NB, 16))
            for k in range(8):
                if k >= 2:
                    pe.wait_ge(fin_add, k - 1)
                for t in range(4):
                    i = 4 * k + t
                    mm = pe.transpose(b_proj[k % 2][:, t * P:(t + 1) * P], X[:, i * P:(i + 1) * P], ident[:])
                mm.then_inc(fin_tr, 1)

        @block.scalar
        def _(act):
            act.wait_ge(start, 1)

            def row_norm(first, marks):
                for k in range(4):
                    act.wait_ge(ln_step, first + LN_SUB[k])
                    act.activation(ln_sq[k % 2], ln_tmp[:, 8 * k:8 * k + 8, :], ACT.Square).then_inc(ln_sqd, 1)
                for k in range(8):
                    act.wait_ge(ln_tr, (8 if first else 0) + k + 1)
                    act.activation(X[:, k * 512:(k + 1) * 512], b_proj[k % 2][:], ACT.Copy).then_inc(ln_cp, 1)

            row_norm(0, None)
            act.wait_ge(la_wt, 1)
            act.activation(la_w[:, 0:3, :], b_sim[:, 0:3 * P].rearrange("p (m n) -> p m n", m=3), ACT.Copy).then_inc(la_wc, 1)

            def la_head(i, b):
                def exp_q():
                    act.wait_ge(la_step.sem, la_step.at(i, 2))
                    act.activation(la_q, la_q, ACT.Exp, scale=LH ** -0.5).then_inc(la_act.sem, 1)

                def exp_k():
                    act.wait_ge(la_pe.sem, la_pe.at(i, 2))
                    act.wait_ge(la_kv.sem, la_kv.at(i - 1, 1))
                    act.activation(la_k[b], bank[1][:], ACT.Exp, scale=LH ** -0.5).then_inc(la_act.sem, 1)

                def v():
                    act.wait_ge(la_pe.sem, la_pe.at(i, 3))
                    act.wait_ge(la_vb.sem, la_vb.at(i - 1, 1))
                    act.activation(la_v[b], bank[2][:], ACT.Copy).then_inc(la_act.sem, 1)
                return [exp_q, exp_k, v]

            def la_channels(i, b, head):
                for piece in head:
                    piece()
                act.wait_ge(la_ym.sem, la_ym.at(i, 8))
                act.wait_ge(la_po.sem, la_po.at(i - 1, 1))
                act.activation(la_y, obank[:, 0, :], ACT.Copy).then_inc(la_yc.sem, 1)

            la_pipeline(act, la_head, la_channels)
            row_norm(LN_ALL, None)

            def a_xs(a, _):
                act.wait_ge(x_loaded.sem, x_loaded.at(a, 32))
                act.wait_ge(proj_full.sem, proj_full.at(a - 1, 16))
                act.activation(xs_hi[:], xraw[:, WIN:WIN + T], ACT.Copy)
                act.activation(xw_hi[:, :, 0:P].rearrange("p w (a c) -> p w a c", a=2), window_view(2), ACT.Copy)
                act.activation(xw_hi[:, :, P:3 * DH], xraw[:, 0:T].rearrange("p (w c) -> p w c", w=4), ACT.Copy).then_inc(xs_hi_done.sem, 1)

            def a_proj(a, c, layer):
                n = PROJ_ORDER.index(("proj", c))
                act.wait_ge(proj_full.sem, proj_full.at(a, n + 1))
                before = (a, c - 3) if c >= 3 else (a - 1, c + 5)
                act.wait_ge(roped.sem, roped.at(before[0], before[1] + 1))
                act.wait_ge(ropes_done.sem, ropes_done.at(before[0], before[1] + 1))
                act.wait_ge(squared.sem, squared.at(before[0], before[1] + 1))
                act.activation(qraw[:, ring3(c), :], b_proj[n % 2][:], ACT.Copy).then_inc(raw_copied.sem, 1)
                act.wait_ge(raw_copied.sem, raw_copied.at(a, c + 1))
                act.wait_ge(ss_done.sem, ss_done.at(a, c - 1) if c >= 2 else ss_done.at(a - 1, c + 7))
                act.activation(sq[:, c % 2, :], qraw[:, ring3(c), :], ACT.Square).then_inc(squared.sem, 1)

            def a_v(a, n8, layer):
                wp, mo = n8 // 2, n8 % 2
                n = PROJ_ORDER.index(("v", n8))
                act.wait_ge(proj_full.sem, proj_full.at(a, n + 1))
                act.wait_ge(o_full.sem, o_full.at(a - 1, 2 if wp < 2 else 4))
                act.activation(V[:, wp, mo, :, :, 0:DH], b_proj[n % 2][:].rearrange("p (i r c) -> p i r c", i=4, r=2),
                               ACT.Copy).then_inc(v_copied.sem, 1)

            def a_tr(a, c):
                kind, hh, t = chunk(c)
                act.wait_ge(trA_full.sem, trA_full.at(a, c + 1))
                if c == 0:
                    act.wait_ge(sim_full.sem, sim_full.at(a - 1, 4))
                pad = WIN if kind else 0
                dst = (kT if kind else qT)[:, 4 * hh:4 * hh + 4, pad + t * P:pad + (t + 1) * P]
                act.activation(dst, b_trA[:].rearrange("p (j q) -> p j q", j=4), ACT.Copy).then_inc(trA_copied.sem, 1)

            def b_qk(b, u):
                act.wait_ge(sim_shift.sem, sim_shift.at(b, u + 1))
                act.activation(Pr[:, u % 2, :], Pr[:, u % 2, :], ACT.Exp, scale=8.0).then_inc(p_ready.sem, 1)

            def b_pt(b, u):
                act.wait_ge(trB_full.sem, trB_full.at(b, TRB_ORDER.index(("pt", u)) + 1))
                act.wait_ge(o_full.sem, o_full.at(b, u - 1) if u >= 2 else o_full.at(b - 1, u + 3))
                act.activation(PT[:, u % 2, :], b_trB[:], ACT.Copy).then_inc(pt_copied.sem, 1)

            def b_ot(b, u):
                t, par = UNIT[u]
                act.wait_ge(trB_full.sem, trB_full.at(b, TRB_ORDER.index(("ot", u)) + 1))
                if u == 0:
                    act.wait_ge(c_full.sem, c_full.at(b - 1, 1))
                src = b_trB[:].rearrange("p (j q) -> p j q", j=4)
                dst = OT[:, 4 * par:4 * par + 4, t * P:(t + 1) * P]
                act.activation(even_odd(dst, 0), even_odd(src, 0), ACT.Copy)
                act.activation(even_odd(dst, 1)[0:64], even_odd(src, 1)[64:P], ACT.Copy)
                act.activation(even_odd(dst, 1)[64:P], even_odd(src, 1)[0:64], ACT.Copy).then_inc(ot_copied.sem, 1)

            def c_x1_(c, _):
                act.wait_ge(c_x1.sem, c_x1.at(c, 1))
                act.activation(xsf[0:64, :], x1[0:64, :], ACT.Copy)
                act.activation(xsf[64:P, 1:T], x1[64:P, 0:T - 1], ACT.Copy).then_inc(c_xs.sem, 1)

            def c_mean(c, _):
                act.wait_ge(c_d.sem, c_d.at(c, 1))
                act.activation(dsq[:], dlt[:], ACT.Square).then_inc(c_dsq.sem, 1)

            def c_w1(c, j):
                f0, n = FFB[j]
                act.wait_ge(c_full.sem, c_full.at(c, 5 + j))
                act.wait_ge(c_h.sem, c_h.at(c, j - 1) if j >= 2 else c_h.at(c - 1, 3))
                act.activation(gel[0:n, j % 2, :], b_c[0:n, T:2 * T], ACT.Gelu, bias=vec[0:n, 6 + j:7 + j]).then_inc(c_gelu.sem, 1)

            steps = {"xs": a_xs, "proj": a_proj, "v": a_v, "tr": a_tr, "qk": b_qk,
                     "pt": b_pt, "ot": b_ot, "x1": c_x1_, "mean": c_mean,
                     "w1": c_w1}

            def conv_a(layer):
                act.wait_ge(w_in_sem, (layer + 1) * (W_DMAS * 16))
                act.wait_ge(proj_full.sem, proj_full.at(layer * NB, 16))
                for k in range(3):
                    cols = slice(k * W_THIRD, (k + 1) * W_THIRD)
                    act.activation(wqkv_hi[:, cols], wqkv_raw[:, cols], ACT.Copy).then_inc(w_hi, 1)

            def conv_c(layer):
                act.wait_ge(c_x2.sem, c_x2.at(layer * NB, 1))
                f2 = FFB[2][1]
                act.activation(wo[:], wo_raw[:], ACT.Copy)
                act.activation(w1[:], w1_raw[:], ACT.Copy)
                act.activation(w2[:, 0:2, :], w2_raw[:, 0:2, :], ACT.Copy)
                act.activation(w2[0:f2, 2, :], w2_raw[0:f2, 2, :], ACT.Copy)
                act.activation(vec[:, 0:5], vec_raw[:, 0:5], ACT.Copy)
                act.activation(vec[0:f2, 5:6], vec_raw[0:f2, 5:6], ACT.Copy)
                act.activation(vec[:, 6:8], vec_raw[:, 6:8], ACT.Copy)
                act.activation(vec[0:f2, 8:9], vec_raw[0:f2, 8:9], ACT.Copy).then_inc(w_c, 1)
                act.wait_ge(w_c, layer + 1)

            pipeline(act, lambda *z: run_slots("act", *z, steps), conv_a, conv_c)

        @block.gpsimd
        def _(pool):
            pool.wait_ge(start, 1)

            def la_channels(i, b, _):
                for m in range(LH):
                    pool.wait_ge(la_sc.sem, la_sc.at(i, m + 1))
                    pool.wait_ge(la_ym.sem, la_ym.at(i, m - 1) if m >= 2 else la_ym.at(i - 1, m + 7))
                    pool.tensor_tensor(Pr[:, m % 2, :], PT[:, m % 2, :], la_qn[b], ALU.mult).then_inc(la_z.sem, 1)

            la_pipeline(pool, lambda i, b: [], la_channels)

            def a_proj(a, c, layer):
                if layer is not None and c == 0:
                    pool.wait_ge(w_lo, 3 * layer + 1)
                pool.wait_ge(raw_copied.sem, raw_copied.at(a, c + 1))
                if c:
                    pool.wait_ge(rope_sum.sem, rope_sum.at(a, c))
                kind, hh, t = chunk(c)
                pool.tensor_tensor(halves(ropes[:, c % 2, :]), halves(qraw[:, ring3(c), :])[:, :, ::-1, :],
                                   table(t, 2 * kind + 1), ALU.mult).then_inc(ropes_done.sem, 1)
                pool.wait_ge(ropes_done.sem, ropes_done.at(a, c + 1))
                pool.wait_ge(roped.sem, roped.at(a, c + 1))
                pool.wait_ge(trA_full.sem, trA_full.at(a - 1, c + 1))
                pool.tensor_tensor(qn[:, c, :], ropec[:, c % 2, :], ropes[:, c % 2, :], ALU.add).then_inc(rope_sum.sem, 1)

            def a_norm(a, c):
                if c % 2 == 0:
                    pool.wait_ge(rsq_step.sem, rsq_step.at(a, RSQ_STEPS))
                    pool.wait_ge(rope_sum.sem, rope_sum.at(a, c + 1))
                    normalise(pool, c).then_inc(normed_p.sem, 1)

            steps = {"proj": a_proj, "norm": a_norm}
            pool.wait_ge(x1_saved, 16)
            pipeline(pool, lambda *z: run_slots("pool", *z, steps))

        @block.vector
        def _(dve):
            dve.wait_ge(start, 1)
            dve.wait_ge(const_in, 3 * 16)
            dve.tensor_copy(identb[:], ident[:])
            dve.tensor_copy(maskb[:], mask_f[:])
            dve.memset(mean_w[:], 1.0 / D)
            dve.memset(xraw[:, 0:WIN + 1], 0.0)
            dve.memset(ss[:], 1.0)
            dve.memset(xsf[64:P, 0:1], 0.0).then_inc(setup, 1)

            n_ln = [0]

            def link(ins):
                n_ln[0] += 1
                ins.then_inc(ln_step, 1)
                dve.wait_ge(ln_step, n_ln[0])

            def rsqrt(step, wait, src, seed, tmp, dst):
                step(dve.tensor_scalar(seed, src.bitcast(I32), 1, None, ALU.logical_shift_right))
                wait()
                step(dve.tensor_scalar(dst.bitcast(I32), seed, -1.0, RSQRT_SEED, ALU.mult, ALU.add))
                for _ in range(NEWTON):
                    wait()
                    step(dve.scalar_tensor_tensor(tmp, dst, -0.5, dst, ALU.mult, ALU.mult))
                    wait()
                    step(dve.tensor_tensor(tmp, tmp, src, ALU.mult))
                    wait()
                    step(dve.scalar_tensor_tensor(dst, tmp, 1.5, dst, ALU.add, ALU.mult))

            def row_norm(first):
                for k in range(4):
                    t8 = slice(8 * k, 8 * k + 8)
                    s, v, r = (st[:, j, 0:8] for j in range(3))
                    i_ = rsq_i[:, 0:8]
                    if not first:
                        dve.wait_ge(x_in_sem, 16 * (k + 1))
                    elif k == 0:
                        dve.wait_ge(la_out.sem, la_out.at(NB * T // GRP, 1))
                    link(dve.tensor_reduce(s, X1[:, t8, :], AX.X, ALU.add))
                    link(dve.tensor_scalar(s, s, -1.0 / D, None, ALU.mult))
                    link(dve.tensor_tensor(ln_tmp[:, t8, :], X1[:, t8, :], s.unsqueeze(2).broadcast_to([P, 8, D]), ALU.add))
                    dve.wait_ge(ln_sqd, (4 if first else 0) + k + 1)
                    link(dve.tensor_reduce(v, ln_sq[k % 2], AX.X, ALU.add))
                    link(dve.tensor_scalar(v, v, 1.0 / D, EPS_LN, ALU.mult, ALU.add))
                    rsqrt(link, lambda: None, v, i_, s, r)
                    link(dve.tensor_tensor(ln_tmp[:, t8, :], ln_tmp[:, t8, :], r.unsqueeze(2).broadcast_to([P, 8, D]), ALU.mult))

            row_norm(0)
            assert n_ln[0] == LN_ALL
            dve.wait_ge(la_wc, 1)
            q3 = la_q.rearrange("p (h l) -> p h l", l=LH)
            m64, s64 = st[:, 0, :], st[:, 1, :]

            def la_head(i, b):
                def own(n):
                    dve.wait_ge(la_step.sem, la_step.at(i, n))

                b3 = bank[0][:].rearrange("p (h l) -> p h l", l=LH)

                def q_max():
                    dve.wait_ge(la_pe.sem, la_pe.at(i, 1))
                    dve.tensor_reduce(m64, b3, AX.X, ALU.max).then_inc(la_step.sem, 1)

                def q_shift():
                    own(1)
                    dve.wait_ge(la_pe.sem, la_pe.at(i - 1, 4))
                    dve.tensor_tensor(q3, b3, m64.unsqueeze(2).broadcast_to([P, 64, LH]), ALU.subtract).then_inc(la_step.sem, 1)

                def q_sum():
                    dve.wait_ge(la_act.sem, la_act.at(i, 1))
                    dve.tensor_reduce(s64, q3, AX.X, ALU.add).then_inc(la_step.sem, 1)
                    own(3)
                    dve.reciprocal(s64, s64).then_inc(la_step.sem, 1)

                def q_scale():
                    own(4)
                    dve.tensor_tensor(q3, q3, s64.unsqueeze(2).broadcast_to([P, 64, LH]), ALU.mult).then_inc(la_step.sem, 1)

                def k_eps():
                    dve.wait_ge(la_act.sem, la_act.at(i, 2))
                    dve.tensor_scalar(la_k[b], la_k[b], EPS_K, None, ALU.add).then_inc(la_step.sem, 1)

                def k_sums():
                    own(6)
                    dve.tensor_tensor_scan(la_kn, la_seg, la_k[b], 0.0, ALU.mult, ALU.add).then_inc(la_step.sem, 1)

                def k_recip():
                    own(7)
                    dve.reciprocal(la_kn, la_kn).then_inc(la_step.sem, 1)

                def q_over_k():
                    own(8)
                    dve.wait_ge(la_pe.sem, la_pe.at(i, 4))
                    dve.wait_ge(la_z.sem, la_z.at(i - 1, 1))
                    dve.tensor_tensor(la_qn[b], bank[3][:], la_kn, ALU.mult).then_inc(la_step.sem, 1)
                return [q_max, q_shift, q_sum, q_scale, k_eps, k_sums, k_recip, q_over_k]

            def la_channels(i, b, head):
                def product(m):
                    dve.wait_ge(la_vb.sem, la_vb.at(i, m + 1))
                    dve.wait_ge(la_sc.sem, la_sc.at(i, m - 1) if m >= 2 else la_sc.at(i - 1, m + 7))
                    dve.tensor_tensor(On[:, m % 2, :], bank[4 + m % 2][:], la_k[b], ALU.mult).then_inc(la_kv.sem, 1)

                product(0)
                for m in range(LH):
                    if m + 1 < LH:
                        product(m + 1)
                    dve.wait_ge(la_kv.sem, la_kv.at(i, m + 1))
                    dve.wait_ge(la_z.sem, la_z.at(i, m - 1) if m >= 2 else la_z.at(i - 1, m + 7))
                    dve.tensor_tensor_scan(PT[:, m % 2, :], la_seg, On[:, m % 2, :], 0.0, ALU.mult, ALU.add).then_inc(la_sc.sem, 1)
                    if m < len(head):
                        head[m]()
                dve.wait_ge(la_po.sem, la_po.at(i, 1))
                rows = X1[:, bass.ds((i - 1) * 4, 4), :]
                dve.tensor_tensor(rows, rows, obank[:, 1, :].rearrange("p (t c) -> p t c", c=D), ALU.add).then_inc(la_out.sem, 1)

            la_pipeline(dve, la_head, la_channels)
            row_norm(1)
            dve.wait_ge(ln_tr, 16)
            dve.memset(kT[:, :, 0:WIN], 0.0)
            dve.memset(V[:, :, :, :, :, DH:DH + 1], 1.0).then_inc(setup, 1)

            def a_xs(a, _):
                dve.wait_ge(xs_hi_done.sem, xs_hi_done.at(a, 1))
                dve.tensor_tensor(xs_lo[:], xraw[:, WIN:WIN + T], xs_hi[:].bitcast(F32), ALU.subtract)
                dve.tensor_tensor(xw_lo[:, :, 0:P].rearrange("p w (a c) -> p w a c", a=2), window_view(2),
                                  xw_hi[:, :, 0:P].bitcast(F32).rearrange("p w (a c) -> p w a c", a=2), ALU.subtract)
                dve.tensor_tensor(xw_lo[:, :, P:3 * DH], xraw[:, 0:T].rearrange("p (w c) -> p w c", w=4),
                                  xw_hi[:, :, P:3 * DH].bitcast(F32), ALU.subtract).then_inc(xs_lo_done.sem, 1)

            def a_proj(a, c, layer):
                kind, hh, t = chunk(c)
                dve.wait_ge(raw_copied.sem, raw_copied.at(a, c + 1))
                dve.wait_ge(rope_sum.sem, rope_sum.at(a, c - 1) if c >= 2 else rope_sum.at(a - 1, c + 7))
                dve.tensor_tensor(halves(ropec[:, c % 2, :]), halves(qraw[:, ring3(c), :]), table(t, 2 * kind),
                                  ALU.mult).then_inc(roped.sem, 1)

            def sum_squares(a, c):
                dve.wait_ge(squared.sem, squared.at(a, c + 1))
                if c == 0:
                    dve.wait_ge(rsq_step.sem, rsq_step.at(a - 1, RSQ_STEPS))
                dve.tensor_reduce(ss[:, 8 * c:8 * c + 8], heads8(sq[:, c % 2, :]), AX.X, ALU.add).then_inc(ss_done.sem, 1)

            def rsqrt_(n, has_a, has_c):
                k = [0]

                def step(ins):
                    k[0] += 1
                    ins.then_inc(rsq_step.sem, 1)

                def wait():
                    dve.wait_ge(rsq_step.sem, rsq_step.at(n, k[0]))
                if has_a:
                    dve.wait_ge(ss_done.sem, ss_done.at(n, 8))
                    dve.wait_ge(normed_p.sem, normed_p.at(n - 1, 4))
                    dve.wait_ge(normed_v.sem, normed_v.at(n - 1, 4))
                if has_c:
                    dve.wait_ge(c_var.sem, c_var.at(n - 2, 1))
                    dve.wait_ge(c_full.sem, c_full.at(n - 3, 4))
                else:
                    dve.wait_ge(rsq_step.sem, rsq_step.at(n - 1, RSQ_STEPS))
                step(dve.tensor_scalar(ss[:], ss[:], EPS_L2SQ, None, ALU.max))
                wait()
                rsqrt(step, wait, ss[:], rsq_i[:], rsq_t[:], rinv[:])
                assert k[0] == RSQ_STEPS

            def a_norm(a, c):
                if c % 2:
                    dve.wait_ge(rsq_step.sem, rsq_step.at(a, RSQ_STEPS))
                    dve.wait_ge(rope_sum.sem, rope_sum.at(a, c + 1))
                    normalise(dve, c).then_inc(normed_v.sem, 1)

            def b_qk(b, u):
                dve.wait_ge(sim_full.sem, sim_full.at(b, u + 1))
                s3 = heads8(b_sim[:])
                dve.tensor_reduce(mx[:, u % 2, :], s3, AX.X, ALU.max).then_inc(max_done.sem, 1)
                dve.wait_ge(max_done.sem, max_done.at(b, u + 1))
                dve.wait_ge(trB_full.sem, trB_full.at(b, TRB_ORDER.index(("pt", u - 2)) + 1) if u >= 2
                            else trB_full.at(b - 1, TRB_ORDER.index(("pt", u + 2)) + 1))
                dve.tensor_tensor(heads8(Pr[:, u % 2, :]), s3, mx[:, u % 2, :].unsqueeze(2).broadcast_to([P, 8, 2 * WIN]),
                                  ALU.subtract).then_inc(sim_shift.sem, 1)

            def b_pv(b, u):
                dve.wait_ge(o_full.sem, o_full.at(b, u + 1))
                o4 = obank[:, :, 0:4 * 65].rearrange("p s (j c) -> p s j c", j=4)
                dve.reciprocal(rs[:], o4[:, :, :, DH]).then_inc(rs_done.sem, 1)
                dve.wait_ge(rs_done.sem, rs_done.at(b, u + 1))
                dve.wait_ge(trB_full.sem, trB_full.at(b, TRB_ORDER.index(("ot", u - 2)) + 1) if u >= 2
                            else trB_full.at(b - 1, TRB_ORDER.index(("ot", u + 2)) + 1))
                dve.tensor_tensor(On[:, u % 2, :].rearrange("p (j s c) -> p s j c", j=4, s=2), o4[:, :, :, 0:DH],
                                  rs[:].unsqueeze(3).broadcast_to([P, 2, 4, DH]), ALU.mult).then_inc(on_done.sem, 1)

            def c_x1_(c, _):
                dve.wait_ge(c_full.sem, c_full.at(c, 1))
                dve.wait_ge(xres_loaded.sem, xres_loaded.at(c, 16))
                dve.wait_ge(c_x2.sem, c_x2.at(c - 1, 1))
                dve.tensor_tensor(x1[:], b_c[:, 0:T], xres[:], ALU.add).then_inc(c_x1.sem, 1)

            def c_mean(c, _):
                dve.wait_ge(c_full.sem, c_full.at(c, 2))
                dve.tensor_tensor(dlt[:], xsf[:], b_c[:, 0:T], ALU.subtract).then_inc(c_d.sem, 1)

            def c_var_(c, _):
                dve.wait_ge(c_full.sem, c_full.at(c, 3))
                dve.wait_ge(rsq_step.sem, rsq_step.at(c + 1, RSQ_STEPS))
                dve.tensor_scalar(ss[:, 64:64 + NT], b_c[:, 0:NT], EPS_LN, None, ALU.add).then_inc(c_var.sem, 1)

            def c_ln_(c, n):
                dve.wait_ge(c_full.sem, c_full.at(c, 4))
                dve.tensor_tensor(lnt[:], dlt[:], b_c[:, 0:T], ALU.mult).then_inc(c_ln.sem, 1)
                dve.wait_ge(c_ln.sem, c_ln.at(c, 1))
                dve.tensor_scalar(xn[:], lnt[:], vec[:, 0:1], vec[:, 1:2], ALU.mult, ALU.add).then_inc(c_ln.sem, 1)

            def c_w1(c, j):
                f0, n = FFB[j]
                dve.wait_ge(c_gelu.sem, c_gelu.at(c, j + 1))
                dve.scalar_tensor_tensor(hm[0:n, j, :], b_c[0:n, 0:T], vec[0:n, 3 + j:4 + j], gel[0:n, j % 2, :],
                                         ALU.add, ALU.mult).then_inc(c_h.sem, 1)

            def c_w2(c, _):
                dve.wait_ge(c_full.sem, c_full.at(c, 8))
                dve.wait_ge(x_stored.sem, x_stored.at(c - 1, 16))
                dve.scalar_tensor_tensor(x2[:], b_c[:, 0:T], vec[:, 2:3], x1[:], ALU.add, ALU.add).then_inc(c_x2.sem, 1)

            steps = {"xs": a_xs, "proj": a_proj, "sums": sum_squares, "rsqrt": rsqrt_, "norm": a_norm, "qk": b_qk,
                     "pv": b_pv, "x1": c_x1_, "mean": c_mean,
                     "var": c_var_, "ln": c_ln_, "w1": c_w1, "w2": c_w2}

            def conv_a(layer):
                dve.wait_ge(w_in_sem, (layer + 1) * (W_DMAS * 16))
                dve.wait_ge(ropes_done.sem, ropes_done.at(layer * NB, 8))
                dve.wait_ge(roped.sem, roped.at(layer * NB, 8))
                for kind in range(2):
                    sc = qks_raw[:, kind, :]
                    sw = sc.rearrange("p (a d) -> p a d", a=2)[:, ::-1, :].unsqueeze(1).broadcast_to([P, NT, 2, DH // 2])
                    dve.tensor_tensor(rots[:, :, 2 * kind, :], rot[:, :, 2 * kind, :], sc.unsqueeze(1).broadcast_to([P, NT, DH]), ALU.mult)
                    dve.tensor_tensor(rots[:, :, 2 * kind + 1, :].rearrange("p t (a d) -> p t a d", a=2),
                                      rot[:, :, 2 * kind + 1, :].rearrange("p t (a d) -> p t a d", a=2), sw, ALU.mult)
                for k in range(3):
                    cols = slice(k * W_THIRD, (k + 1) * W_THIRD)
                    dve.wait_ge(w_hi, 3 * layer + k + 1)
                    dve.wait_ge(proj_full.sem, proj_full.at(layer * NB, 16))
                    dve.tensor_tensor(wqkv_lo[:, cols], wqkv_raw[:, cols], wqkv_hi[:, cols].bitcast(F32), ALU.subtract).then_inc(w_lo, 1)
                dve.wait_ge(w_lo, 3 * layer + 1)

            def conv_c(layer):
                dve.wait_ge(w_c, layer + 1)

            pipeline(dve, lambda *z: run_slots("dve", *z, steps), conv_a, conv_c)
            dve.wait_ge(x1_back, 16)
            for k in range(8):
                dve.wait_ge(fin_tr, k + 1)
                rows = X1[:, 4 * k:4 * k + 4, :]
                dve.tensor_tensor(rows, rows, b_proj[k % 2][:].rearrange("p (t c) -> p t c", c=D), ALU.add).then_inc(fin_add, 1)


LN_PER = 5 + (2 + 3 * NEWTON) + 1
LN_ALL = 4 * LN_PER
LN_SUB = [LN_PER * k + 3 for k in range(4)]
LN_DONE = [LN_PER * (k + 1) for k in range(4)]


def shape_constants():
    f = np.float32
    half = np.arange(0, DH, 2, dtype=f)
    inv_freq = (f(1.0) / f(10000.0) ** (half / f(DH))).astype(f)
    t = np.arange(T, dtype=f)
    freqs = (t[:, None] * inv_freq[None, :]).astype(f)
    freqs = np.concatenate([freqs, freqs], -1).astype(np.float64)
    base = ((half + f(0.4 * DH)) / f(1.4 * DH)).astype(f)
    power = ((t - T // 2) / f(WIN // 2)).astype(f)
    scale = base[None, :].astype(np.float64) ** power[:, None].astype(np.float64)
    scale = np.concatenate([scale, scale], -1)
    sign = np.where(np.arange(DH) < DH // 2, -1.0, 1.0)[None, :]
    cos, sin = np.cos(freqs), np.sin(freqs) * sign
    tab = np.stack([cos * scale, sin * scale, cos / scale, sin / scale], 1)
    rotary = tab.reshape(NT, P, 4, DH).transpose(1, 0, 2, 3).astype(f)
    masks = np.zeros((P, 2, 2 * WIN), f)
    i = np.arange(P) % WIN
    j = np.arange(WIN)
    masks[:, :, WIN:] = np.where(j[None, :] > i[:, None], f(-1e30), f(0))[:, None, :]
    masks[:, :, :WIN] = np.where(j[None, :] < i[:, None], f(-1e30), f(0))[:, None, :]
    masks[0:WIN, 0, 0:WIN] = f(-1e30)
    ident = np.eye(P, dtype=f)
    pick = np.zeros((P, LH, P), f)
    for m in range(LH):
        for h in range(HEADS):
            pick[h * LH + m, m, h * LH:(h + 1) * LH] = 1
    gather = np.ascontiguousarray(pick.transpose(2, 1, 0))
    seg = np.ones((P, GRP), f)
    seg[:, ::T] = 0
    return {"c_rotary": rotary, "c_masks": masks, "c_ident": ident, "c_pick": pick, "c_gather": gather, "c_seg": seg}


_INS = ["L0_attn_x", "L0_attn_w", "L0_attn_w_out", "L0_ffn_Wqkv", "L0_ffn_q_scale", "L0_ffn_k_scale", "L0_ffn_Wo",
        "L0_ffn_ln_g", "L0_ffn_ln_b", "L0_ffn_W1", "L0_ffn_b1", "L0_ffn_W2", "L0_ffn_b2"]


def kernel(**inputs):
    import concourse.bacc as bacc
    from concourse.bass_utils import run_bass_kernel_spmd

    nc = bacc.Bacc("TRN2", target_bir_lowering=False, num_devices=1)
    arrays, args = {}, []
    for name, a in [(n, inputs[n]) for n in _INS] + list(shape_constants().items()):
        a = np.ascontiguousarray(a)
        arrays[name] = a
        args.append(nc.dram_tensor(name, a.shape, mybir.dt.from_np(a.dtype), kind="ExternalInput").ap())
    args.append(nc.dram_tensor("out", (NB, T, D), F32, kind="ExternalOutput").ap())
    build(nc, *args)
    r = run_bass_kernel_spmd(nc, [arrays], core_ids=[0])
    return r.results[0]["out"]
```

```python
from contextlib import ExitStack

import numpy as np

import concourse.bass as bass
from concourse import mybir
from concourse.alu_op_type import AluOpType as ALU

F32 = mybir.dt.float32
F32R = mybir.dt.float32r
BF16 = mybir.dt.bfloat16
I32 = mybir.dt.int32
ACT = mybir.ActivationFunctionType
AX = mybir.AxisListType

P = 128
NB, T, D = 16, 256, 128
NT = T // P
DEPTH, HEADS, DH, WIN = 6, 16, 64, 32
INNER = HEADS * DH
FF = int(D * 4 * 2 / 3)
FFB = [(0, 128), (128, 128), (256, FF - 256)]
LH = 8
EPS_LN, EPS_L2SQ, EPS_K = 1e-5, 1e-24, 1e-6
RSQRT_SEED = float(0x5F3759DF)
NEWTON = 3
RSQ_STEPS = 3 + 3 * NEWTON
AHEAD = 3
V_DMAS = 10
GRP = 2 * T

ORDER = {
    "pe": """
        qk.0' proj.0 proj.1 ot.3'' proj.2 qk.1' proj.3 wo.0'' proj.4 qk.2' pt.0' proj.5 mean.0'' proj.6 pv.0'
        proj.7 v.0 var.0'' ot.0' qk.3' pt.1' v.1 pv.1' v.2 ln.0'' ot.1' tr.0 pt.2' tr.1 w1.0'' v.3 tr.2 pv.2'
        tr.3 w1.1'' ot.2' tr.4 pt.3' tr.5 w1.2'' tr.6 pv.3' tr.7 w2.0'' """,
    "act": """
        tr.7' xs.0 wa.1 proj.0 ot.3'' proj.1 wa.2 proj.2 qk.0' proj.3 x1.0'' qk.1' proj.4 pt.0' proj.5 proj.6
        mean.0'' wc.0'' proj.7 qk.2' ot.0' pt.1' v.0 v.1 ot.1' tr.0 pt.2' tr.1 qk.3' w1.0'' tr.2 tr.3 w1.1''
        ot.2' tr.4 pt.3' tr.5 w1.2'' wc.1'' tr.6 v.2 v.3 wc.2'' """,
    "dve": """
        xs.0 wa.1 pv.3'' qk.0' proj.0 proj.1 wa.2 sums.0 qk.1' proj.2 sums.1 sums.2 x1.0'' proj.3 sums.3 qk.2'
        sums.4 proj.4 mean.0'' sums.5 pv.0' proj.5 sums.6 var.0'' sums.7 rsqrt.0 pv.1' ln.0'' norm.1 qk.3'
        norm.3 proj.6 w1.0'' pv.2' w1.1'' norm.5 proj.7 norm.7 w1.2'' w2.0'' """,
    "pool": """
        proj.0 proj.1 proj.2 proj.3 proj.4 norm.0 norm.2 proj.5 norm.4 proj.6 norm.6 proj.7 """,
}


def order(engine):
    for word in ORDER[engine].split():
        kind, i = word.rstrip("'").split(".")
        yield kind, int(i), word.count("'")


def fills(*kinds):
    return [(k, i) for lag in range(3) for k, i, g in order("pe") if g == lag and k in kinds]


PROJ_ORDER = fills("proj", "v")
TRB_ORDER = fills("pt", "ot")


class Count:

    def __init__(self, sem, per):
        self.sem, self.per = sem, per

    def at(self, batch, n):
        return batch * self.per + n


def build(nc, x_in, w_in, w_out_in, Wqkv, q_scale, k_scale, Wo, ln_g, ln_b, W1, b1, W2, b2,
          rotary, masks, ident_in, pick_in, gather_in, seg_in, out):
    ctx = ExitStack()
    with ctx:
        def sb(name, shape, dt=F32):
            return ctx.enter_context(nc.sbuf_tensor(name, shape, dt))

        def ps(name, shape, dt=F32):
            return ctx.enter_context(nc.psum_tensor(name, shape, dt))

        def sem(name):
            return ctx.enter_context(nc.semaphore(name))

        counts = []

        def per_batch(name, per):
            counts.append(Count(sem(name), per))
            return counts[-1]

        X = sb("X", [P, NB * T])
        wqkv_raw = sb("wqkv_raw", [P, 3 * INNER])
        wo_raw = sb("wo_raw", [P, 2 * 4, D])
        w1_raw = sb("w1_raw", [P, 2 * FF])
        w2_raw = sb("w2_raw", [P, 3, D])
        vec_raw = sb("vec_raw", [P, 9])
        qks_raw = sb("qks_raw", [P, 2, DH])
        wqkv_hi = sb("wqkv_hi", [P, 3 * INNER], F32R)
        wqkv_lo = sb("wqkv_lo", [P, 3 * INNER], F32R)
        wo = sb("wo", [P, 8, D])
        w1 = sb("w1", [P, 2 * FF])
        w2 = sb("w2", [P, 3, D])
        vec = sb("vec", [P, 9])
        rot = sb("rot", [P, NT, 4, DH])
        rots = sb("rots", [P, NT, 4, DH])
        ident = sb("ident", [P, P])
        identb = sb("identb", [P, P], BF16)
        mask_f = sb("mask_f", [P, 2, 2 * WIN])
        maskb = sb("maskb", [P, 2, 2 * WIN], BF16)
        mean_w = sb("mean_w", [P, P])
        xraw = sb("xraw", [P, T])
        xs_hi = sb("xs_hi", [P, T], F32R)
        xs_lo = sb("xs_lo", [P, T], F32R)
        qraw = sb("qraw", [P, 3, 512])
        sq = sb("sq", [P, 2, 512])
        ropec = sb("ropec", [P, 2, 512])
        ropes = sb("ropes", [P, 2, 512])
        qn = sb("qn", [P, 8, 512])
        ss = sb("ss", [P, 64 + NT])
        rsq_i = sb("rsq_i", [P, 64 + NT], I32)
        rsq_t = sb("rsq_t", [P, 64 + NT])
        rinv = sb("rinv", [P, 64 + NT])
        qT = sb("qT", [P, 8, T])
        kT = sb("kT", [P, 8, WIN + T])
        V = sb("V", [P, 4, 2, 4, 2, DH + 1])
        Vt = sb("Vt", [P, NT, 2, 4, 2, DH + 1])
        mx = sb("mx", [P, 2, 8])
        Pr = sb("Pr", [P, 2, 512])
        PT = sb("PT", [P, 2, 512])
        rs = sb("rs", [P, 2, 4])
        On = sb("On", [P, 2, 512])
        OT = sb("OT", [P, 8, T])
        xres = sb("xres", [P, T])
        x1 = sb("x1", [P, T])
        xsf = sb("xsf", [P, T])
        dlt = sb("dlt", [P, T])
        dsq = sb("dsq", [P, T])
        lnt = sb("lnt", [P, T])
        xn = sb("xn", [P, T])
        gel = sb("gel", [P, 2, T])
        hm = sb("hm", [P, 3, T])
        x2 = sb("x2", [P, T])

        bank = [ps(f"bank{i}", [P, 512]) for i in range(6)]
        obank = ps("obank", [P, 2, 512])
        b_proj, b_trA, b_trB, b_sim, b_c = bank[0:2], bank[2], bank[3], bank[4], bank[5]

        qTf = qT[:].rearrange("p a b -> p (a b)")
        kTf = kT[:].rearrange("p a b -> p (a b)")
        Vf = V[:].rearrange("p a b c d e -> p (a b c d e)")
        pick = wo[:]
        gather = ropes[:].rearrange("p a b -> p (a b)").rearrange("p (m n) -> p m n", m=LH)
        la_w = gel[:].rearrange("p a b -> p (a b)").rearrange("p (m n) -> p m n", m=4)
        OTf = OT[:].rearrange("p a b -> p (a b)")
        la_x, la_q, la_kn, la_y = (qTf[:, i * 512:(i + 1) * 512] for i in range(4))
        la_k = [kTf[:, i * 512:(i + 1) * 512] for i in range(2)]
        la_v = [OTf[:, i * 512:(i + 1) * 512] for i in range(2)]
        la_qn = [OTf[:, 1024:1536], OTf[:, 1536:2048]]
        la_seg = kTf[:, 1024:1536]
        la_w_rows = w2[:]
        X1 = qn[:].rearrange("p a b -> p (a b)").rearrange("p (t c) -> p t c", c=D)
        ln_tmp = Vf[:, 0:NB * NT * D].rearrange("p (t c) -> p t c", c=D)
        ln_sq = [b[:].rearrange("p a b -> p (a b)").rearrange("p (t c) -> p t c", c=D) for b in (sq, ropec)]
        st = sb("st", [P, 4, 64])

        start = sem("start")
        const_in = sem("const_in")
        x_in_sem = [sem(f"x_in_{k}") for k in range(4)]
        setup = sem("setup")
        ln_step = sem("ln_step")
        ln_sqd = sem("ln_sqd")
        ln_tr = sem("ln_tr")
        ln_cp = sem("ln_cp")
        la_wt = sem("la_wt")
        la_wc = sem("la_wc")
        la_step = per_batch("la_step", 9)
        la_pe = per_batch("la_pe", 4)
        la_act = per_batch("la_act", 3)
        la_yc = per_batch("la_yc", 1)
        la_po = per_batch("la_po", 1)
        la_xin = per_batch("la_xin", 16)
        la_vb = per_batch("la_vb", 8)
        la_kv = per_batch("la_kv", 8)
        la_sc = per_batch("la_sc", 8)
        la_z = per_batch("la_z", 8)
        la_ym = per_batch("la_ym", 8)
        la_out = per_batch("la_out", 1)
        la_const_in = sem("la_const_in")
        x1_saved = sem("x1_saved")
        x1_back = sem("x1_back")
        fin_tr = sem("fin_tr")
        fin_add = sem("fin_add")
        fin_dma = sem("fin_dma")

        w_in_sem = sem("w_in")
        w_hi = sem("w_hi")
        w_lo = sem("w_lo")
        w_c = sem("w_c")
        sp_held, pe_held = sem("sp_held"), sem("pe_held")
        x_loaded = per_batch("x_loaded", 32)
        xres_loaded = per_batch("xres_loaded", 16)
        x_stored = per_batch("x_stored", 16)
        xs_hi_done = per_batch("xs_hi_done", 1)
        xs_lo_done = per_batch("xs_lo_done", 1)
        proj_full = per_batch("proj_full", 12)
        raw_copied = per_batch("raw_copied", 8)
        squared = per_batch("squared", 8)
        roped = per_batch("roped", 8)
        ropes_done = per_batch("ropes_done", 8)
        ss_done = per_batch("ss_done", 8)
        rope_sum = per_batch("rope_sum", 8)
        rsq_step = per_batch("rsq_step", RSQ_STEPS)
        normed_p = per_batch("normed_p", 4)
        normed_v = per_batch("normed_v", 4)
        v_copied = per_batch("v_copied", 4)
        v_placed = per_batch("v_placed", 16 * V_DMAS)
        trA_full = per_batch("trA_full", 8)
        trA_copied = per_batch("trA_copied", 8)
        sim_full = per_batch("sim_full", 4)
        max_done = per_batch("max_done", 4)
        sim_shift = per_batch("sim_shift", 4)
        p_ready = per_batch("p_ready", 4)
        trB_full = per_batch("trB_full", 8)
        pt_copied = per_batch("pt_copied", 4)
        o_full = per_batch("o_full", 4)
        rs_done = per_batch("rs_done", 4)
        on_done = per_batch("on_done", 4)
        ot_copied = per_batch("ot_copied", 4)
        c_full = per_batch("c_full", 8)
        c_x1 = per_batch("c_x1", 1)
        c_xs = per_batch("c_xs", 1)
        c_d = per_batch("c_d", 1)
        c_dsq = per_batch("c_dsq", 1)
        c_var = per_batch("c_var", 1)
        c_ln = per_batch("c_ln", 2)
        c_gelu = per_batch("c_gelu", 3)
        c_h = per_batch("c_h", 3)
        c_x2 = per_batch("c_x2", 1)

        out_rows = out.rearrange("b (t p) c -> p (b t) c", p=P)
        vb_bank = [bank[2], bank[4], bank[5]]
        block = ctx.enter_context(nc.Block())

        LA_STEPS = NB * T // GRP

        def la_pipeline(eng, head, channels):
            for piece in head(1, 1):
                piece()
            channels(1, 1, head(2, 0), False)
            channels(2, 0, head(3, 1), True)
            with eng.Fori(1, LA_STEPS // 2 - 1) as j:
                channels(2 * j + 1, 1, head(2 * j + 2, 0), True)
                channels(2 * j + 2, 0, head(2 * j + 3, 1), True)
            channels(LA_STEPS - 1, 1, head(LA_STEPS, 0), True)
            channels(LA_STEPS, 0, [], True)

        def pipeline(eng, body, conv_a=None, loads=None):
            body(1, 0, (0,), 0, None)
            body(2, 1, (0, 1), None, None)
            with eng.Fori(0, DEPTH - 1) as l:
                loads and loads(l + 1)
                with eng.Fori(2, NB) as g:
                    body(l * NB + g + 1, g, (0, 1, 2), None, l)
                conv_a and conv_a(l + 1)
                body(l * NB + NB + 1, 0, (0, 1, 2), l + 1, l)
                body(l * NB + NB + 2, 1, (0, 1, 2), None, l, l + 1)
            last = (DEPTH - 1) * NB
            with eng.Fori(2, NB) as g:
                body(last + g + 1, g, (0, 1, 2), None, DEPTH - 1)
            body(last + NB + 1, 0, (1, 2), None, DEPTH - 1)
            body(last + NB + 2, 1, (2,), None, DEPTH - 1)

        def is_first(layer):
            return isinstance(layer, int) and layer == 0

        def run_slots(steps, engine, n, g, lags, layer, c_layer, next_c=None):
            for kind, i, lag in order(engine):
                step = steps.get(kind)
                if step is None:
                    continue
                if kind == "wa":
                    if layer is not None and not is_first(layer):
                        step(layer, i)
                    continue
                if kind == "wc":
                    if next_c is not None:
                        step(n - 2, next_c, i)
                    continue
                if kind == "rsqrt":
                    step(n, 0 in lags, 2 in lags)
                elif lag in lags:
                    if kind in ("proj", "v"):
                        step(n - lag, i, layer)
                    elif kind == "ln":
                        step(n - lag, n, c_layer)
                    elif kind in ("wo", "w1"):
                        step(n - lag, i, c_layer)
                    else:
                        step(n - lag, i)

        def chunk(c):
            return (c // 2) % 2, c % 2, c // 4

        def heads8(ap):
            return ap.rearrange("p (h d) -> p h d", h=8)

        def halves(ap):
            return ap.rearrange("p (h a d) -> p h a d", h=8, a=2)

        def table(t, i):
            return rots[:, t, i, :].rearrange("p (a d) -> p a d", a=2).unsqueeze(1).broadcast_to([P, 8, 2, DH // 2])

        def normalise(eng, c):
            return eng.tensor_tensor(heads8(qn[:, c, :]), heads8(qn[:, c, :]),
                                     rinv[:, 8 * c:8 * c + 8].unsqueeze(2).broadcast_to([P, 8, DH]), ALU.mult)

        RING3 = [0, 1, 2, 0, 1, 2, 0, 1]
        UNIT = [(u // 2, u % 2) for u in range(4)]

        def even_odd(ap, e):
            return ap.rearrange("p j (w e q) -> p j w e q", w=2, e=2)[:, :, :, e, :]

        def hold(eng, held, s, value):
            eng.wait_ge(s, value)
            eng.sem_inc(held, 1)

        def bank_free(eng, a, n):
            kind, i = PROJ_ORDER[n - 2]
            s = raw_copied if kind == "proj" else v_copied
            eng.wait_ge(s.sem, s.at(a if n >= 2 else a - 1, i + 1))

        W_DMAS = 20
        W_THIRD = INNER

        @block.sync
        def _(sp):
            for s in counts:
                sp.sem_inc(s.sem, s.per)
            sp.sem_inc(start, 1)
            for k in range(4):
                rows = slice(8 * k, 8 * k + 8)
                sp.dma_start(X1[:, rows, :], x_in.rearrange("b (t p) c -> p (b t) c", p=P)[:, rows, :]).then_inc(x_in_sem[k], 16)
            sp.dma_start(ident[:], ident_in).then_inc(const_in, 16)
            sp.dma_start(la_w_rows, w_in.rearrange("(m p) c -> p m c", p=P)).then_inc(la_const_in, 16)
            sp.dma_start(la_w[:, 3, :], w_out_in).then_inc(la_const_in, 16)
            sp.dma_start(pick, pick_in).then_inc(la_const_in, 16)
            sp.dma_start(gather, gather_in).then_inc(la_const_in, 16)
            sp.dma_start(la_seg, seg_in).then_inc(la_const_in, 16)
            sp.dma_start(rot[:], rotary).then_inc(const_in, 16)
            sp.dma_start(mask_f[:], masks).then_inc(const_in, 16)

            def load_weights(layer):
                def col(name, i, src, n=P):
                    sp.dma_start(vec_raw[0:n, i:i + 1], src).then_inc(w_in_sem, 16)
                one = slice(layer, layer + 1) if isinstance(layer, int) else bass.ds(layer, 1)
                sp.dma_start(wqkv_raw[:], Wqkv[one].rearrange("l p n -> p (l n)")).then_inc(w_in_sem, 16)
                for slot in range(2):
                    for par in range(2):
                        src = Wo[one].rearrange("l (j s r p) n -> s r p (l j) n", j=4, s=2, r=2)[slot, par]
                        sp.dma_start(wo_raw[slot * 64:slot * 64 + 64, 4 * par:4 * par + 4, :], src).then_inc(w_in_sem, 16)
                sp.dma_start(w1_raw[:], W1[one].rearrange("l p n -> p (l n)")).then_inc(w_in_sem, 16)
                for j, (f0, n) in enumerate(FFB):
                    sp.dma_start(w2_raw[0:n, j, :], W2[one, f0:f0 + n].rearrange("l p n -> p (l n)")).then_inc(w_in_sem, 16)
                col("g", 0, ln_g[one].rearrange("l p -> p l"))
                col("b", 1, ln_b[one].rearrange("l p -> p l"))
                col("b2", 2, b2[one].rearrange("l p -> p l"))
                for j, (f0, n) in enumerate(FFB):
                    col("b1a", 3 + j, b1[one, f0:f0 + n].rearrange("l p -> p l"), n)
                    col("b1g", 6 + j, b1[one, FF + f0:FF + f0 + n].rearrange("l p -> p l"), n)
                sp.dma_start(qks_raw[:, 0, :], q_scale[one].broadcast_to([P, DH])).then_inc(w_in_sem, 16)
                sp.dma_start(qks_raw[:, 1, :], k_scale[one].broadcast_to([P, DH])).then_inc(w_in_sem, 16)

            load_weights(0)
            sp.wait_ge(ln_cp, 8)
            with sp.Fori(0, NB * T // GRP) as i:
                sp.wait_ge(la_pe.sem, la_pe.at(i, 3))
                sp.dma_start(la_x, X[:, bass.ds(i * GRP, GRP)]).then_inc(la_xin.sem, 16)

            sp.wait_ge(la_out.sem, la_out.at(NB * T // GRP, 1))
            sp.dma_start(out_rows, X1).then_inc(x1_saved, 16)
            sp.wait_ge(ln_cp, 16)

            def place(g):
                return bass.ds(g * T, T)

            def load_x(g):
                sp.dma_start(xraw[0:64, :], X[0:64, place(g)]).then_inc(x_loaded.sem, 16)
                sp.dma_start(xraw[64:P, 1:T], X[64:P, bass.ds(g * T, T - 1)]).then_inc(x_loaded.sem, 16)

            def place_v(n):
                sp.wait_ge(v_copied.sem, v_copied.at(n, 4))
                sp.wait_ge(o_full.sem, o_full.at(n - 1, 4))
                for mo in range(2):
                    even, odd = 64 * mo, 64 * (1 - mo)

                    def move(dst, pair, src, tiles, rows):
                        d = V[dst:dst + rows].rearrange("p (t w) m j r c -> p t w m (j r c)", w=2)[:, tiles, pair, mo]
                        v = Vt[src:src + rows].rearrange("p t m j r c -> p t m (j r c)")
                        v = v[:, 0:1, mo] if tiles == slice(1, 2) and src == P - WIN else v[:, tiles, mo]
                        sp.dma_start(d, v).then_inc(v_placed.sem, 16)

                    both = slice(0, 2)
                    move(odd, 0, 0, both, 64)
                    move(odd, 1, 64, both, 64)
                    move(even, 1, WIN, both, 64)
                    move(even + WIN, 0, 0, both, WIN)
                    move(even, 0, P - WIN, slice(1, 2), WIN)

            def body(n, g, lags, layer, c_layer, next_c=None):
                c = n - 2
                has_a, has_b, has_c = (lag in lags for lag in (0, 1, 2))
                if has_b:
                    if has_c:
                        sp.wait_ge(c_x1.sem, c_x1.at(c, 1))
                    sp.dma_start(xres[:], X[:, place(wrap(g - 1))]).then_inc(xres_loaded.sem, 16)
                if has_a:
                    sp.wait_ge(xs_lo_done.sem, xs_lo_done.at(n, 1))
                    load_x(wrap(g + 1))
                if has_a:
                    place_v(n)
                if has_c:
                    sp.wait_ge(c_x2.sem, c_x2.at(c, 1))
                    sp.dma_start(X[:, place(wrap(g - 2))], x2[:]).then_inc(x_stored.sem, 16)

            def wrap(g):
                if isinstance(g, int):
                    return g % NB
                return (g + NB) % NB

            def loads(layer):
                hold(sp, sp_held, w_lo, 3 * layer)
                hold(sp, sp_held, w_c, 3 * layer)
                load_weights(layer)

            load_x(0)
            pipeline(sp, body, loads=loads)
            sp.wait_ge(x_stored.sem, x_stored.at(DEPTH * NB, 16))
            sp.wait_ge(x_loaded.sem, x_loaded.at(DEPTH * NB + 1, 32))
            sp.wait_ge(trA_full.sem, trA_full.at(DEPTH * NB, 8))
            sp.wait_ge(x1_saved, 16)
            sp.dma_start(X1, out_rows).then_inc(x1_back, 16)
            for k in range(8):
                sp.wait_ge(fin_add, k + 1)
                rows = slice(4 * k, 4 * k + 4)
                sp.dma_start(out_rows[:, rows, :], X1[:, rows, :]).then_inc(fin_dma, 16)
            sp.wait_ge(fin_dma, 8 * 16)

        @block.tensor
        def _(pe):
            pe.wait_ge(start, 1)
            pe.wait_ge(const_in, 3 * 16)

            def rows_to_X(first, norm_steps):
                for k in range(8):
                    pe.wait_ge(ln_step, first + norm_steps[k // 2])
                    if first or k >= 2:
                        pe.wait_ge(ln_cp, (8 if first else 0) + k - 1 if not (first and k < 2) else 8)
                    for t in range(4):
                        mm = pe.transpose(b_proj[k % 2][:, t * P:(t + 1) * P], ln_tmp[:, 4 * k + t, :], ident[:])
                    mm.then_inc(ln_tr, 1)

            rows_to_X(0, LN_DONE)
            pe.wait_ge(la_const_in, 5 * 16)
            for m in range(3):
                mm = pe.transpose(b_sim[:, m * P:(m + 1) * P], la_w_rows[:, m, :], ident[:])
            mm.then_inc(la_wt, 1)
            pe.wait_ge(la_wc, 1)

            def la_head(i, b):
                def q():
                    pe.wait_ge(la_xin.sem, la_xin.at(i, 16))
                    pe.wait_ge(la_step.sem, la_step.at(i - 1, 2))
                    for t in range(4):
                        mm = pe.matmul(bank[0][:, t * P:(t + 1) * P], la_x[:, t * P:(t + 1) * P], la_w[:, 0, :], start=True, stop=True)
                    mm.then_inc(la_pe.sem, 1)

                def k():
                    pe.wait_ge(la_act.sem, la_act.at(i - 1, 3))
                    pe.matmul(bank[1][:], la_w[:, 1, :], la_x, start=True, stop=True).then_inc(la_pe.sem, 1)

                def v():
                    pe.wait_ge(la_act.sem, la_act.at(i, 2))
                    pe.matmul(bank[1][:], la_w[:, 2, :], la_x, start=True, stop=True).then_inc(la_pe.sem, 1)

                def q_columns():
                    pe.wait_ge(la_step.sem, la_step.at(i, 5))
                    pe.wait_ge(la_step.sem, la_step.at(i - 1, 9))
                    for t in range(4):
                        mm = pe.transpose(bank[3][:, t * P:(t + 1) * P], la_q[:, t * P:(t + 1) * P], ident[:])
                    mm.then_inc(la_pe.sem, 1)
                return [q, k, v, q_columns]

            def la_spread(i, b, m):
                if m == 0:
                    pe.wait_ge(la_act.sem, la_act.at(i, 3))
                pe.wait_ge(la_kv.sem, la_kv.at(i - 1, (7, 8, 6)[m]) if m < 3 else la_kv.at(i, m - 2))
                pe.matmul(vb_bank[m % 3][:], pick[:, m, :], la_v[b], start=True, stop=True).then_inc(la_vb.sem, 1)

            def la_channels(i, b, head, has_out):
                after = dict(zip((0, 1, 4, 5), head))
                if not has_out:
                    for m in range(AHEAD):
                        la_spread(i, b, m)
                for m in range(LH):
                    m in after and after[m]()
                    if m + AHEAD < LH:
                        la_spread(i, b, m + AHEAD)
                    elif head:
                        la_spread(i + 1, 1 - b, m + AHEAD - LH)
                    if m == 2 and has_out:
                        la_output(i - 1)
                    pe.wait_ge(la_z.sem, la_z.at(i, m + 1))
                    if m == 0:
                        pe.wait_ge(la_yc.sem, la_yc.at(i - 1, 1))
                    pe.matmul(obank[:, 0, :], gather[:, m, :], Pr[:, m % 2, :], start=m == 0, stop=m == LH - 1).then_inc(la_ym.sem, 1)

            def la_output(i):
                pe.wait_ge(la_yc.sem, la_yc.at(i, 1))
                pe.wait_ge(la_out.sem, la_out.at(i - 1, 1))
                for t in range(4):
                    mm = pe.matmul(obank[:, 1, t * P:(t + 1) * P], la_y[:, t * P:(t + 1) * P], la_w[:, 3, :], start=True, stop=True)
                mm.then_inc(la_po.sem, 1)

            la_pipeline(pe, la_head, la_channels)
            la_output(LA_STEPS)
            rows_to_X(LN_ALL, LN_DONE)

            def a_proj(a, c, layer):
                kind, hh, t = chunk(c)
                n = PROJ_ORDER.index(("proj", c))
                if layer is not None and c in (0, 2):
                    pe.wait_ge(w_lo, 3 * layer + c // 2 + 1)
                if c == 0:
                    pe.wait_ge(xs_lo_done.sem, xs_lo_done.at(a, 1))
                bank_free(pe, a, n)
                cols = slice(kind * INNER + hh * 512, kind * INNER + hh * 512 + 512)
                rows = slice(t * P, t * P + P)
                o = b_proj[n % 2][:]
                pe.matmul(o, xs_hi[:, rows], wqkv_hi[:, cols], start=True, stop=False)
                pe.matmul(o, xs_hi[:, rows], wqkv_lo[:, cols], start=False, stop=False)
                pe.matmul(o, xs_lo[:, rows], wqkv_hi[:, cols], start=False, stop=True).then_inc(proj_full.sem, 1)

            def a_v(a, i, layer):
                t, mo = i // 2, i % 2
                n = PROJ_ORDER.index(("v", i))
                if layer is not None and i == 0:
                    pe.wait_ge(w_lo, 3 * layer + 3)
                bank_free(pe, a, n)
                rows = slice(t * P, t * P + P)
                def wv(w):
                    return w[:, 2 * INNER:3 * INNER].rearrange("p (i m c) -> p i m c", i=4, m=2)[:, :, mo, :]
                o = b_proj[n % 2][:].rearrange("p (i c) -> p i c", i=4)
                pe.matmul(o, xs_hi[:, rows], wv(wqkv_hi), start=True, stop=False)
                pe.matmul(o, xs_hi[:, rows], wv(wqkv_lo), start=False, stop=False)
                pe.matmul(o, xs_lo[:, rows], wv(wqkv_hi), start=False, stop=True).then_inc(proj_full.sem, 1)

            def a_tr(a, c):
                s = (normed_p, normed_v)[c % 2]
                pe.wait_ge(s.sem, s.at(a, c // 2 + 1))
                pe.wait_ge(trA_copied.sem, trA_copied.at(a, c) if c else trA_copied.at(a - 1, 8))
                for j in range(4):
                    mm = pe.transpose(b_trA[:, j * P:(j + 1) * P], qn[:, c, j * P:(j + 1) * P], ident[:])
                mm.then_inc(trA_full.sem, 1)

            def b_qk(b, u):
                t, par = UNIT[u]
                if u == 0:
                    pe.wait_ge(trA_copied.sem, trA_copied.at(b, 8))
                pe.wait_ge(sim_shift.sem, sim_shift.at(b, u) if u else sim_shift.at(b - 1, 4))
                pe.matmul(b_sim[:], identb[:], maskb[:, 1 if t else 0, :].unsqueeze(1).broadcast_to([P, 8, 2 * WIN]),
                          start=True, stop=False, skip_group_check=True)
                for w in range(4):
                    for m in range(8):
                        slot = (m + w) % 2
                        col = (2 * (m // 2) + slot) * 2 * WIN
                        q0 = t * P + w * WIN
                        mm = pe.matmul(b_sim[w * WIN:(w + 1) * WIN, col:col + 2 * WIN],
                                       qT[64 * par:64 * par + 64, m, q0:q0 + WIN],
                                       kT[64 * par:64 * par + 64, m, q0:q0 + 2 * WIN],
                                       start=False, stop=w == 3 and m == 7, skip_group_check=True)
                mm.then_inc(sim_full.sem, 1)

            def b_pt(b, u):
                pe.wait_ge(p_ready.sem, p_ready.at(b, u + 1))
                trB_free(b, "pt", u)
                for j in range(4):
                    mm = pe.transpose(b_trB[:, j * P:(j + 1) * P], Pr[:, u % 2, j * P:(j + 1) * P], ident[:])
                mm.then_inc(trB_full.sem, 1)

            def trB_free(b, kind, u):
                at = TRB_ORDER.index((kind, u))
                k, n = TRB_ORDER[at - 1]
                batch = b if at else b - 1
                if k == "pt":
                    pe.wait_ge(pt_copied.sem, pt_copied.at(batch, n + 1))
                else:
                    pe.wait_ge(ot_copied.sem, ot_copied.at(batch, n + 1))

            def b_pv(b, u):
                t, par = UNIT[u]
                if u == 0:
                    hold(pe, pe_held, v_placed.sem, v_placed.at(b, 16 * V_DMAS))
                hold(pe, pe_held, on_done.sem, on_done.at(b, u) if u else on_done.at(b - 1, 4))
                hold(pe, pe_held, pt_copied.sem, pt_copied.at(b, u + 1))
                for w in range(4):
                    for slot in range(2):
                        for j in range(4):
                            rows = slice(64 * slot, 64 * slot + 64)
                            wg = 4 * t + w
                            mm = pe.matmul(obank[w * WIN:(w + 1) * WIN, slot, j * 65:j * 65 + 65],
                                           PT[rows, u % 2, j * P + w * WIN:j * P + (w + 1) * WIN],
                                           V[rows, wg // 2, (slot + w) % 2, j, par, :],
                                           start=True, stop=True, skip_group_check=True)
                mm.then_inc(o_full.sem, 1)

            def b_ot(b, u):
                pe.wait_ge(on_done.sem, on_done.at(b, u + 1))
                trB_free(b, "ot", u)
                for j in range(4):
                    mm = pe.transpose(b_trB[:, j * P:(j + 1) * P], On[:, u % 2, j * P:(j + 1) * P], ident[:])
                mm.then_inc(trB_full.sem, 1)

            def c_wo(c, _, layer):
                pe.wait_ge(w_c, 3 * layer + 1)
                pe.wait_ge(ot_copied.sem, ot_copied.at(c, 4))
                pe.wait_ge(c_x2.sem, c_x2.at(c - 1, 1))
                for i in range(8):
                    mm = pe.matmul(b_c[:, 0:T], wo[:, i, :], OT[:, i, :], start=i == 0, stop=i == 7)
                mm.then_inc(c_full.sem, 1)

            def c_mean(c, _):
                pe.wait_ge(c_x1.sem, c_x1.at(c, 1))
                pe.wait_ge(c_xs.sem, c_xs.at(c, 1))
                pe.matmul(b_c[:, 0:T], mean_w[:], xsf[:], start=True, stop=True).then_inc(c_full.sem, 1)

            def c_var_(c, _):
                pe.wait_ge(c_d.sem, c_d.at(c, 1))
                pe.wait_ge(c_dsq.sem, c_dsq.at(c, 1))
                for t in range(NT):
                    mm = pe.matmul(b_c[:, t:t + 1], dsq[:, t * P:(t + 1) * P], mean_w[:, 0:1], start=True, stop=True)
                mm.then_inc(c_full.sem, 1)

            def c_ln_(c, n, layer):
                pe.wait_ge(rsq_step.sem, rsq_step.at(n, RSQ_STEPS))
                for t in range(NT):
                    mm = pe.matmul(b_c[:, t * P:(t + 1) * P], rinv[:, 64 + t:65 + t].broadcast_to([P, P]), ident[:],
                                   start=True, stop=True)
                mm.then_inc(c_full.sem, 1)

            def c_w1(c, j, layer):
                f0, n = FFB[j]
                if j == 0:
                    pe.wait_ge(w_c, 3 * layer + 3)
                    pe.wait_ge(c_ln.sem, c_ln.at(c, 2))
                else:
                    pe.wait_ge(c_h.sem, c_h.at(c, j))
                for part in range(2):
                    cols = slice(part * FF + f0, part * FF + f0 + n)
                    mm = pe.matmul(b_c[0:n, part * T:(part + 1) * T], w1[:, cols], xn[:], start=True, stop=True)
                mm.then_inc(c_full.sem, 1)

            def c_w2(c, _):
                pe.wait_ge(c_h.sem, c_h.at(c, 3))
                for j, (f0, n) in enumerate(FFB):
                    mm = pe.matmul(b_c[:, 0:T], w2[0:n, j, :], hm[0:n, j, :], start=j == 0, stop=j == 2)
                mm.then_inc(c_full.sem, 1)

            steps = {"proj": a_proj, "v": a_v, "tr": a_tr, "qk": b_qk,
                     "pt": b_pt, "pv": b_pv, "ot": b_ot, "wo": c_wo,
                     "mean": c_mean, "var": c_var_, "ln": c_ln_, "w1": c_w1, "w2": c_w2}

            pipeline(pe, lambda *z: run_slots(steps, "pe", *z))
            pe.wait_ge(x_stored.sem, x_stored.at(DEPTH * NB, 16))
            for k in range(8):
                if k >= 2:
                    pe.wait_ge(fin_add, k - 1)
                for t in range(4):
                    i = 4 * k + t
                    mm = pe.transpose(b_proj[k % 2][:, t * P:(t + 1) * P], X[:, i * P:(i + 1) * P], ident[:])
                mm.then_inc(fin_tr, 1)

        @block.scalar
        def _(act):
            act.wait_ge(start, 1)

            def conv_a(layer):
                act.wait_ge(w_in_sem, (layer + 1) * (W_DMAS * 16))
                act.wait_ge(proj_full.sem, proj_full.at(layer * NB, 12))
                w_a(layer, 0)

            def w_a(layer, k):
                cols = slice(k * W_THIRD, (k + 1) * W_THIRD)
                act.activation(wqkv_hi[:, cols], wqkv_raw[:, cols], ACT.Copy).then_inc(w_hi, 1)

            def row_norm(first):
                for k in range(4):
                    act.wait_ge(ln_step, first + LN_SUB[k])
                    act.activation(ln_sq[k % 2], ln_tmp[:, 8 * k:8 * k + 8, :], ACT.Square).then_inc(ln_sqd, 1)
                if not first:
                    conv_a(0)
                    w_a(0, 1)
                    w_a(0, 2)
                for k in range(8):
                    act.wait_ge(ln_tr, (8 if first else 0) + k + 1)
                    act.activation(X[:, k * 512:(k + 1) * 512], b_proj[k % 2][:], ACT.Copy).then_inc(ln_cp, 1)

            row_norm(0)
            act.wait_ge(la_wt, 1)
            act.activation(la_w[:, 0:3, :], b_sim[:, 0:3 * P].rearrange("p (m n) -> p m n", m=3), ACT.Copy).then_inc(la_wc, 1)

            def la_head(i, b):
                def exp_q():
                    act.wait_ge(la_step.sem, la_step.at(i, 2))
                    act.activation(la_q, la_q, ACT.Exp, scale=LH ** -0.5).then_inc(la_act.sem, 1)

                def exp_k():
                    act.wait_ge(la_pe.sem, la_pe.at(i, 2))
                    act.wait_ge(la_kv.sem, la_kv.at(i - 1, 1))
                    act.activation(la_k[b], bank[1][:], ACT.Exp, scale=LH ** -0.5).then_inc(la_act.sem, 1)

                def v():
                    act.wait_ge(la_pe.sem, la_pe.at(i, 3))
                    act.wait_ge(la_vb.sem, la_vb.at(i - 1, 1))
                    act.activation(la_v[b], bank[1][:], ACT.Copy).then_inc(la_act.sem, 1)
                return [exp_q, exp_k, v]

            def la_channels(i, b, head, has_out):
                for piece in head:
                    piece()
                act.wait_ge(la_ym.sem, la_ym.at(i, 8))
                act.wait_ge(la_po.sem, la_po.at(i - 1, 1))
                act.activation(la_y, obank[:, 0, :], ACT.Copy).then_inc(la_yc.sem, 1)

            la_pipeline(act, la_head, la_channels)
            row_norm(LN_ALL)

            def a_xs(a, _):
                act.wait_ge(x_loaded.sem, x_loaded.at(a, 32))
                act.wait_ge(proj_full.sem, proj_full.at(a - 1, 12))
                act.activation(xs_hi[:], xraw[:], ACT.Copy).then_inc(xs_hi_done.sem, 1)

            def a_proj(a, c, layer):
                n = PROJ_ORDER.index(("proj", c))
                act.wait_ge(proj_full.sem, proj_full.at(a, n + 1))
                before = (a, c - 3) if c >= 3 else (a - 1, (6, 7, 5)[c])
                act.wait_ge(roped.sem, roped.at(before[0], before[1] + 1))
                act.wait_ge(ropes_done.sem, ropes_done.at(before[0], before[1] + 1))
                act.wait_ge(squared.sem, squared.at(before[0], before[1] + 1))
                act.activation(qraw[:, RING3[c], :], b_proj[n % 2][:], ACT.Copy).then_inc(raw_copied.sem, 1)
                act.wait_ge(raw_copied.sem, raw_copied.at(a, c + 1))
                act.wait_ge(ss_done.sem, ss_done.at(a, c - 1) if c >= 2 else ss_done.at(a - 1, c + 7))
                act.activation(sq[:, c % 2, :], qraw[:, RING3[c], :], ACT.Square).then_inc(squared.sem, 1)

            def a_v(a, i, layer):
                n = PROJ_ORDER.index(("v", i))
                act.wait_ge(proj_full.sem, proj_full.at(a, n + 1))
                act.wait_ge(v_placed.sem, v_placed.at(a - 1, 16 * V_DMAS))
                act.activation(Vt[:, i // 2, i % 2, :, :, 0:DH], b_proj[n % 2][:].rearrange("p (i r c) -> p i r c", i=4, r=2),
                               ACT.Copy).then_inc(v_copied.sem, 1)

            def a_tr(a, c):
                kind, hh, t = chunk(c)
                act.wait_ge(trA_full.sem, trA_full.at(a, c + 1))
                if c == 0:
                    act.wait_ge(sim_full.sem, sim_full.at(a - 1, 4))
                pad = WIN if kind else 0
                dst = (kT if kind else qT)[:, 4 * hh:4 * hh + 4, pad + t * P:pad + (t + 1) * P]
                act.activation(dst, b_trA[:].rearrange("p (j q) -> p j q", j=4), ACT.Copy).then_inc(trA_copied.sem, 1)

            def b_qk(b, u):
                act.wait_ge(sim_shift.sem, sim_shift.at(b, u + 1))
                act.activation(Pr[:, u % 2, :], Pr[:, u % 2, :], ACT.Exp, scale=8.0).then_inc(p_ready.sem, 1)

            def b_pt(b, u):
                act.wait_ge(trB_full.sem, trB_full.at(b, TRB_ORDER.index(("pt", u)) + 1))
                act.wait_ge(o_full.sem, o_full.at(b, u - 1) if u >= 2 else o_full.at(b - 1, u + 3))
                act.activation(PT[:, u % 2, :], b_trB[:], ACT.Copy).then_inc(pt_copied.sem, 1)

            def b_ot(b, u):
                t, par = UNIT[u]
                act.wait_ge(trB_full.sem, trB_full.at(b, TRB_ORDER.index(("ot", u)) + 1))
                if u == 0:
                    act.wait_ge(c_full.sem, c_full.at(b - 1, 1))
                src = b_trB[:].rearrange("p (j q) -> p j q", j=4)
                dst = OT[:, 4 * par:4 * par + 4, t * P:(t + 1) * P]
                act.activation(even_odd(dst, 0), even_odd(src, 0), ACT.Copy)
                act.activation(even_odd(dst, 1)[0:64], even_odd(src, 1)[64:P], ACT.Copy)
                act.activation(even_odd(dst, 1)[64:P], even_odd(src, 1)[0:64], ACT.Copy).then_inc(ot_copied.sem, 1)

            def c_x1_(c, _):
                act.wait_ge(c_x1.sem, c_x1.at(c, 1))
                act.activation(xsf[0:64, :], x1[0:64, :], ACT.Copy)
                act.activation(xsf[64:P, 1:T], x1[64:P, 0:T - 1], ACT.Copy).then_inc(c_xs.sem, 1)

            def c_mean(c, _):
                act.wait_ge(c_d.sem, c_d.at(c, 1))
                act.activation(dsq[:], dlt[:], ACT.Square).then_inc(c_dsq.sem, 1)

            def c_w1(c, j, layer):
                f0, n = FFB[j]
                if j == 0:
                    act.wait_ge(w_c, 3 * layer + 3)
                act.wait_ge(c_full.sem, c_full.at(c, 5 + j))
                act.wait_ge(c_h.sem, c_h.at(c, j - 1) if j >= 2 else c_h.at(c - 1, 3))
                act.activation(gel[0:n, j % 2, :], b_c[0:n, T:2 * T], ACT.Gelu, bias=vec[0:n, 6 + j:7 + j]).then_inc(c_gelu.sem, 1)

            steps = {"xs": a_xs, "proj": a_proj, "v": a_v, "tr": a_tr, "qk": b_qk,
                     "pt": b_pt, "ot": b_ot, "x1": c_x1_, "mean": c_mean,
                     "w1": c_w1}

            def w_cs(c, layer, k):
                f2 = FFB[2][1]
                if k == 0:
                    act.wait_ge(w_in_sem, (layer + 1) * (W_DMAS * 16))
                    act.wait_ge(c_full.sem, c_full.at(c, 1))
                    act.activation(wo[:], wo_raw[:], ACT.Copy).then_inc(w_c, 1)
                elif k == 1:
                    act.wait_ge(c_full.sem, c_full.at(c, 7))
                    act.activation(w1[:], w1_raw[:], ACT.Copy).then_inc(w_c, 1)
                else:
                    act.wait_ge(c_x2.sem, c_x2.at(c, 1))
                    act.activation(w2[:, 0:2, :], w2_raw[:, 0:2, :], ACT.Copy)
                    act.activation(w2[0:f2, 2, :], w2_raw[0:f2, 2, :], ACT.Copy)
                    act.activation(vec[:, 0:5], vec_raw[:, 0:5], ACT.Copy)
                    act.activation(vec[0:f2, 5:6], vec_raw[0:f2, 5:6], ACT.Copy)
                    act.activation(vec[:, 6:8], vec_raw[:, 6:8], ACT.Copy)
                    act.activation(vec[0:f2, 8:9], vec_raw[0:f2, 8:9], ACT.Copy).then_inc(w_c, 1)

            for k in range(3):
                w_cs(0, 0, k)
            steps.update({"wa": w_a, "wc": w_cs})
            pipeline(act, lambda *z: run_slots(steps, "act", *z), conv_a)

        @block.gpsimd
        def _(pool):
            pool.wait_ge(start, 1)

            def la_channels(i, b, _, __):
                for m in range(LH):
                    pool.wait_ge(la_sc.sem, la_sc.at(i, m + 1))
                    pool.wait_ge(la_ym.sem, la_ym.at(i, m - 1) if m >= 2 else la_ym.at(i - 1, m + 7))
                    pool.tensor_tensor(Pr[:, m % 2, :], PT[:, m % 2, :], la_qn[b], ALU.mult).then_inc(la_z.sem, 1)

            la_pipeline(pool, lambda i, b: [], la_channels)

            def a_proj(a, c, layer):
                if layer is not None and c == 0:
                    pool.wait_ge(w_lo, 3 * layer + 1)
                pool.wait_ge(raw_copied.sem, raw_copied.at(a, c + 1))
                if c:
                    pool.wait_ge(rope_sum.sem, rope_sum.at(a, c))
                kind, hh, t = chunk(c)
                pool.tensor_tensor(halves(ropes[:, c % 2, :]), halves(qraw[:, RING3[c], :])[:, :, ::-1, :],
                                   table(t, 2 * kind + 1), ALU.mult).then_inc(ropes_done.sem, 1)
                pool.wait_ge(ropes_done.sem, ropes_done.at(a, c + 1))
                pool.wait_ge(roped.sem, roped.at(a, c + 1))
                pool.wait_ge(trA_full.sem, trA_full.at(a - 1, c + 1))
                pool.tensor_tensor(qn[:, c, :], ropec[:, c % 2, :], ropes[:, c % 2, :], ALU.add).then_inc(rope_sum.sem, 1)

            def a_norm(a, c):
                if c % 2 == 0:
                    pool.wait_ge(rsq_step.sem, rsq_step.at(a, RSQ_STEPS))
                    pool.wait_ge(rope_sum.sem, rope_sum.at(a, c + 1))
                    normalise(pool, c).then_inc(normed_p.sem, 1)

            steps = {"proj": a_proj, "norm": a_norm}
            pool.wait_ge(x1_saved, 16)
            pipeline(pool, lambda *z: run_slots(steps, "pool", *z))

        @block.vector
        def _(dve):
            dve.wait_ge(start, 1)
            dve.memset(mean_w[:], 1.0 / D)
            dve.memset(xraw[64:P, 0:1], 0.0)
            dve.memset(Vt[:], 1.0)
            dve.memset(ss[:], 1.0)
            dve.memset(xsf[64:P, 0:1], 0.0).then_inc(setup, 1)

            n_ln = [0]

            def link(ins):
                n_ln[0] += 1
                ins.then_inc(ln_step, 1)
                dve.wait_ge(ln_step, n_ln[0])

            def rsqrt(step, wait, src, seed, tmp, dst):
                step(dve.tensor_scalar(seed, src.bitcast(I32), 1, None, ALU.logical_shift_right))
                wait()
                step(dve.tensor_scalar(dst.bitcast(I32), seed, -1.0, RSQRT_SEED, ALU.mult, ALU.add))
                for _ in range(NEWTON):
                    wait()
                    step(dve.scalar_tensor_tensor(tmp, dst, -0.5, dst, ALU.mult, ALU.mult))
                    wait()
                    step(dve.tensor_tensor(tmp, tmp, src, ALU.mult))
                    wait()
                    step(dve.scalar_tensor_tensor(dst, tmp, 1.5, dst, ALU.add, ALU.mult))

            def row_norm(first):
                n = NB * NT
                s, v, r = (st[:, j, 0:n] for j in range(3))

                def tiles(k):
                    return slice(8 * k, 8 * k + 8)

                def wide(a, k):
                    return a[:, tiles(k)].unsqueeze(2).broadcast_to([P, 8, D])

                def variance(k):
                    dve.wait_ge(ln_sqd, (4 if first else 0) + k + 1)
                    link(dve.tensor_reduce(v[:, tiles(k)], ln_sq[k % 2], AX.X, ALU.add))

                for k in range(4):
                    if not first:
                        dve.wait_ge(x_in_sem[k], 16)
                    elif k == 0:
                        dve.wait_ge(la_out.sem, la_out.at(NB * T // GRP, 1))
                    link(dve.tensor_reduce(s[:, tiles(k)], X1[:, tiles(k), :], AX.X, ALU.add))
                    link(dve.tensor_scalar(s[:, tiles(k)], s[:, tiles(k)], -1.0 / D, None, ALU.mult))
                    link(dve.tensor_tensor(ln_tmp[:, tiles(k), :], X1[:, tiles(k), :], wide(s, k), ALU.add))
                    if k:
                        variance(k - 1)
                variance(3)
                link(dve.tensor_scalar(v, v, 1.0 / D, EPS_LN, ALU.mult, ALU.add))
                rsqrt(link, lambda: None, v, rsq_i[:, 0:n], s, r)
                for k in range(4):
                    link(dve.tensor_tensor(ln_tmp[:, tiles(k), :], ln_tmp[:, tiles(k), :], wide(r, k), ALU.mult))

            def conv_a(layer):
                dve.wait_ge(w_in_sem, (layer + 1) * (W_DMAS * 16))
                dve.wait_ge(ropes_done.sem, ropes_done.at(layer * NB, 8))
                dve.wait_ge(roped.sem, roped.at(layer * NB, 8))
                for kind in range(2):
                    sc = qks_raw[:, kind, :]
                    sw = sc.rearrange("p (a d) -> p a d", a=2)[:, ::-1, :].unsqueeze(1).broadcast_to([P, NT, 2, DH // 2])
                    dve.tensor_tensor(rots[:, :, 2 * kind, :], rot[:, :, 2 * kind, :], sc.unsqueeze(1).broadcast_to([P, NT, DH]), ALU.mult)
                    dve.tensor_tensor(rots[:, :, 2 * kind + 1, :].rearrange("p t (a d) -> p t a d", a=2),
                                      rot[:, :, 2 * kind + 1, :].rearrange("p t (a d) -> p t a d", a=2), sw, ALU.mult)
                w_a(layer, 0)
                dve.wait_ge(w_lo, 3 * layer + 1)

            def w_a(layer, k):
                cols = slice(k * W_THIRD, (k + 1) * W_THIRD)
                dve.wait_ge(w_hi, 3 * layer + k + 1)
                dve.wait_ge(proj_full.sem, proj_full.at(layer * NB, 12))
                dve.tensor_tensor(wqkv_lo[:, cols], wqkv_raw[:, cols], wqkv_hi[:, cols].bitcast(F32), ALU.subtract).then_inc(w_lo, 1)

            row_norm(0)
            assert n_ln[0] == LN_ALL
            dve.wait_ge(const_in, 3 * 16)
            dve.tensor_copy(identb[:], ident[:])
            dve.tensor_copy(maskb[:], mask_f[:]).then_inc(setup, 1)
            conv_a(0)
            w_a(0, 1)
            w_a(0, 2)
            dve.wait_ge(la_wc, 1)
            q3 = la_q.rearrange("p (h l) -> p h l", l=LH)
            m64, s64 = st[:, 0, :], st[:, 1, :]

            def la_head(i, b):
                def own(n):
                    dve.wait_ge(la_step.sem, la_step.at(i, n))

                b3 = bank[0][:].rearrange("p (h l) -> p h l", l=LH)

                def q_max():
                    dve.wait_ge(la_pe.sem, la_pe.at(i, 1))
                    dve.tensor_reduce(m64, b3, AX.X, ALU.max).then_inc(la_step.sem, 1)

                def q_shift():
                    own(1)
                    dve.wait_ge(la_pe.sem, la_pe.at(i - 1, 4))
                    dve.tensor_tensor(q3, b3, m64.unsqueeze(2).broadcast_to([P, 64, LH]), ALU.subtract).then_inc(la_step.sem, 1)

                def q_sum():
                    dve.wait_ge(la_act.sem, la_act.at(i, 1))
                    dve.tensor_reduce(s64, q3, AX.X, ALU.add).then_inc(la_step.sem, 1)
                    own(3)
                    dve.reciprocal(s64, s64).then_inc(la_step.sem, 1)

                def q_scale():
                    own(4)
                    dve.tensor_tensor(q3, q3, s64.unsqueeze(2).broadcast_to([P, 64, LH]), ALU.mult).then_inc(la_step.sem, 1)

                def k_eps():
                    dve.wait_ge(la_act.sem, la_act.at(i, 2))
                    dve.tensor_scalar(la_k[b], la_k[b], EPS_K, None, ALU.add).then_inc(la_step.sem, 1)

                def k_sums():
                    own(6)
                    dve.tensor_tensor_scan(la_kn, la_seg, la_k[b], 0.0, ALU.mult, ALU.add).then_inc(la_step.sem, 1)

                def k_recip():
                    own(7)
                    dve.reciprocal(la_kn, la_kn).then_inc(la_step.sem, 1)

                def q_over_k():
                    own(8)
                    dve.wait_ge(la_pe.sem, la_pe.at(i, 4))
                    dve.wait_ge(la_z.sem, la_z.at(i - 1, 1))
                    dve.tensor_tensor(la_qn[b], bank[3][:], la_kn, ALU.mult).then_inc(la_step.sem, 1)
                return [q_max, q_shift, q_sum, q_scale, k_eps, k_sums, k_recip, q_over_k]

            def la_channels(i, b, head, has_out):
                def product(m):
                    dve.wait_ge(la_vb.sem, la_vb.at(i, m + 1))
                    dve.wait_ge(la_sc.sem, la_sc.at(i, m - 1) if m >= 2 else la_sc.at(i - 1, m + 7))
                    dve.tensor_tensor(On[:, m % 2, :], vb_bank[m % 3][:], la_k[b], ALU.mult).then_inc(la_kv.sem, 1)

                product(0)
                for m in range(LH):
                    if m + 1 < LH:
                        product(m + 1)
                    dve.wait_ge(la_kv.sem, la_kv.at(i, m + 1))
                    dve.wait_ge(la_z.sem, la_z.at(i, m - 1) if m >= 2 else la_z.at(i - 1, m + 7))
                    dve.tensor_tensor_scan(PT[:, m % 2, :], la_seg, On[:, m % 2, :], 0.0, ALU.mult, ALU.add).then_inc(la_sc.sem, 1)
                    if m < len(head):
                        head[m]()
                    if m == 3 and has_out:
                        la_residual(i - 1)

            def la_residual(i):
                dve.wait_ge(la_po.sem, la_po.at(i, 1))
                rows = X1[:, bass.ds((i - 1) * 4, 4), :]
                dve.tensor_tensor(rows, rows, obank[:, 1, :].rearrange("p (t c) -> p t c", c=D), ALU.add).then_inc(la_out.sem, 1)

            la_pipeline(dve, la_head, la_channels)
            la_residual(LA_STEPS)
            row_norm(1)
            dve.wait_ge(ln_tr, 16)
            dve.memset(kT[:, :, 0:WIN], 0.0)
            dve.memset(V[0:WIN, 0, 0], 0.0)
            dve.memset(V[64:64 + WIN, 0, 1], 0.0).then_inc(setup, 1)

            def a_xs(a, _):
                dve.wait_ge(xs_hi_done.sem, xs_hi_done.at(a, 1))
                dve.tensor_tensor(xs_lo[:], xraw[:], xs_hi[:].bitcast(F32), ALU.subtract).then_inc(xs_lo_done.sem, 1)

            def a_proj(a, c, layer):
                kind, hh, t = chunk(c)
                dve.wait_ge(raw_copied.sem, raw_copied.at(a, c + 1))
                dve.wait_ge(rope_sum.sem, rope_sum.at(a, c - 1) if c >= 2 else rope_sum.at(a - 1, c + 7))
                dve.tensor_tensor(halves(ropec[:, c % 2, :]), halves(qraw[:, RING3[c], :]), table(t, 2 * kind),
                                  ALU.mult).then_inc(roped.sem, 1)

            def sum_squares(a, c):
                dve.wait_ge(squared.sem, squared.at(a, c + 1))
                if c == 0:
                    dve.wait_ge(rsq_step.sem, rsq_step.at(a - 1, RSQ_STEPS))
                dve.tensor_reduce(ss[:, 8 * c:8 * c + 8], heads8(sq[:, c % 2, :]), AX.X, ALU.add).then_inc(ss_done.sem, 1)

            def rsqrt_(n, has_a, has_c):
                k = [0]

                def step(ins):
                    k[0] += 1
                    ins.then_inc(rsq_step.sem, 1)

                def wait():
                    dve.wait_ge(rsq_step.sem, rsq_step.at(n, k[0]))
                if has_a:
                    dve.wait_ge(ss_done.sem, ss_done.at(n, 8))
                    dve.wait_ge(normed_p.sem, normed_p.at(n - 1, 4))
                    dve.wait_ge(normed_v.sem, normed_v.at(n - 1, 4))
                if has_c:
                    dve.wait_ge(c_var.sem, c_var.at(n - 2, 1))
                    dve.wait_ge(c_full.sem, c_full.at(n - 3, 4))
                else:
                    dve.wait_ge(rsq_step.sem, rsq_step.at(n - 1, RSQ_STEPS))
                step(dve.tensor_scalar(ss[:], ss[:], EPS_L2SQ, None, ALU.max))
                wait()
                rsqrt(step, wait, ss[:], rsq_i[:], rsq_t[:], rinv[:])
                assert k[0] == RSQ_STEPS

            def a_norm(a, c):
                if c % 2:
                    dve.wait_ge(rsq_step.sem, rsq_step.at(a, RSQ_STEPS))
                    dve.wait_ge(rope_sum.sem, rope_sum.at(a, c + 1))
                    normalise(dve, c).then_inc(normed_v.sem, 1)

            def b_qk(b, u):
                dve.wait_ge(sim_full.sem, sim_full.at(b, u + 1))
                s3 = heads8(b_sim[:])
                dve.tensor_reduce(mx[:, u % 2, :], s3, AX.X, ALU.max).then_inc(max_done.sem, 1)
                dve.wait_ge(max_done.sem, max_done.at(b, u + 1))
                dve.wait_ge(trB_full.sem, trB_full.at(b, TRB_ORDER.index(("pt", u - 2)) + 1) if u >= 2
                            else trB_full.at(b - 1, TRB_ORDER.index(("pt", u + 2)) + 1))
                dve.tensor_tensor(heads8(Pr[:, u % 2, :]), s3, mx[:, u % 2, :].unsqueeze(2).broadcast_to([P, 8, 2 * WIN]),
                                  ALU.subtract).then_inc(sim_shift.sem, 1)

            def b_pv(b, u):
                dve.wait_ge(o_full.sem, o_full.at(b, u + 1))
                o4 = obank[:, :, 0:4 * 65].rearrange("p s (j c) -> p s j c", j=4)
                dve.reciprocal(rs[:], o4[:, :, :, DH]).then_inc(rs_done.sem, 1)
                dve.wait_ge(rs_done.sem, rs_done.at(b, u + 1))
                dve.wait_ge(trB_full.sem, trB_full.at(b, TRB_ORDER.index(("ot", u - 2)) + 1) if u >= 2
                            else trB_full.at(b - 1, TRB_ORDER.index(("ot", u + 2)) + 1))
                dve.tensor_tensor(On[:, u % 2, :].rearrange("p (j s c) -> p s j c", j=4, s=2), o4[:, :, :, 0:DH],
                                  rs[:].unsqueeze(3).broadcast_to([P, 2, 4, DH]), ALU.mult).then_inc(on_done.sem, 1)

            def c_x1_(c, _):
                dve.wait_ge(c_full.sem, c_full.at(c, 1))
                dve.wait_ge(xres_loaded.sem, xres_loaded.at(c, 16))
                dve.wait_ge(c_x2.sem, c_x2.at(c - 1, 1))
                dve.tensor_tensor(x1[:], b_c[:, 0:T], xres[:], ALU.add).then_inc(c_x1.sem, 1)

            def c_mean(c, _):
                dve.wait_ge(c_full.sem, c_full.at(c, 2))
                dve.tensor_tensor(dlt[:], xsf[:], b_c[:, 0:T], ALU.subtract).then_inc(c_d.sem, 1)

            def c_var_(c, _):
                dve.wait_ge(c_full.sem, c_full.at(c, 3))
                dve.wait_ge(rsq_step.sem, rsq_step.at(c + 1, RSQ_STEPS))
                dve.tensor_scalar(ss[:, 64:64 + NT], b_c[:, 0:NT], EPS_LN, None, ALU.add).then_inc(c_var.sem, 1)

            def c_ln_(c, n, layer):
                dve.wait_ge(w_c, 3 * layer + 3)
                dve.wait_ge(c_full.sem, c_full.at(c, 4))
                dve.tensor_tensor(lnt[:], dlt[:], b_c[:, 0:T], ALU.mult).then_inc(c_ln.sem, 1)
                dve.wait_ge(c_ln.sem, c_ln.at(c, 1))
                dve.tensor_scalar(xn[:], lnt[:], vec[:, 0:1], vec[:, 1:2], ALU.mult, ALU.add).then_inc(c_ln.sem, 1)

            def c_w1(c, j, layer):
                f0, n = FFB[j]
                dve.wait_ge(c_gelu.sem, c_gelu.at(c, j + 1))
                dve.scalar_tensor_tensor(hm[0:n, j, :], b_c[0:n, 0:T], vec[0:n, 3 + j:4 + j], gel[0:n, j % 2, :],
                                         ALU.add, ALU.mult).then_inc(c_h.sem, 1)

            def c_w2(c, _):
                dve.wait_ge(c_full.sem, c_full.at(c, 8))
                dve.wait_ge(x_stored.sem, x_stored.at(c - 1, 16))
                dve.scalar_tensor_tensor(x2[:], b_c[:, 0:T], vec[:, 2:3], x1[:], ALU.add, ALU.add).then_inc(c_x2.sem, 1)

            steps = {"xs": a_xs, "proj": a_proj, "sums": sum_squares, "rsqrt": rsqrt_, "norm": a_norm, "qk": b_qk,
                     "pv": b_pv, "x1": c_x1_, "mean": c_mean,
                     "var": c_var_, "ln": c_ln_, "w1": c_w1, "w2": c_w2}

            steps["wa"] = w_a
            pipeline(dve, lambda *z: run_slots(steps, "dve", *z), conv_a)
            dve.wait_ge(x1_back, 16)
            for k in range(8):
                dve.wait_ge(fin_tr, k + 1)
                rows = X1[:, 4 * k:4 * k + 4, :]
                dve.tensor_tensor(rows, rows, b_proj[k % 2][:].rearrange("p (t c) -> p t c", c=D), ALU.add).then_inc(fin_add, 1)


LN_SUB = [3, 6, 10, 14]
LN_DONE = [16 + 1 + (2 + 3 * NEWTON) + k + 1 for k in range(4)]
LN_ALL = LN_DONE[3]


def shape_constants():
    f = np.float32
    half = np.arange(0, DH, 2, dtype=f)
    inv_freq = (f(1.0) / f(10000.0) ** (half / f(DH))).astype(f)
    t = np.arange(T, dtype=f)
    freqs = (t[:, None] * inv_freq[None, :]).astype(f)
    freqs = np.concatenate([freqs, freqs], -1).astype(np.float64)
    base = ((half + f(0.4 * DH)) / f(1.4 * DH)).astype(f)
    power = ((t - T // 2) / f(WIN // 2)).astype(f)
    scale = base[None, :].astype(np.float64) ** power[:, None].astype(np.float64)
    scale = np.concatenate([scale, scale], -1)
    sign = np.where(np.arange(DH) < DH // 2, -1.0, 1.0)[None, :]
    cos, sin = np.cos(freqs), np.sin(freqs) * sign
    tab = np.stack([cos * scale, sin * scale, cos / scale, sin / scale], 1)
    rotary = tab.reshape(NT, P, 4, DH).transpose(1, 0, 2, 3).astype(f)
    masks = np.zeros((P, 2, 2 * WIN), f)
    i = np.arange(P) % WIN
    j = np.arange(WIN)
    masks[:, :, WIN:] = np.where(j[None, :] > i[:, None], f(-1e30), f(0))[:, None, :]
    masks[:, :, :WIN] = np.where(j[None, :] < i[:, None], f(-1e30), f(0))[:, None, :]
    masks[0:WIN, 0, 0:WIN] = f(-1e30)
    ident = np.eye(P, dtype=f)
    pick = np.zeros((P, LH, P), f)
    for m in range(LH):
        for h in range(HEADS):
            pick[h * LH + m, m, h * LH:(h + 1) * LH] = 1
    gather = np.ascontiguousarray(pick.transpose(2, 1, 0))
    seg = np.ones((P, GRP), f)
    seg[:, ::T] = 0
    return {"c_rotary": rotary, "c_masks": masks, "c_ident": ident, "c_pick": pick, "c_gather": gather, "c_seg": seg}


_INS = ["L0_attn_x", "L0_attn_w", "L0_attn_w_out", "L0_ffn_Wqkv", "L0_ffn_q_scale", "L0_ffn_k_scale", "L0_ffn_Wo",
        "L0_ffn_ln_g", "L0_ffn_ln_b", "L0_ffn_W1", "L0_ffn_b1", "L0_ffn_W2", "L0_ffn_b2"]


def kernel(**inputs):
    import concourse.bacc as bacc
    from concourse.bass_utils import run_bass_kernel_spmd

    nc = bacc.Bacc("TRN2", target_bir_lowering=False, num_devices=1)
    arrays, args = {}, []
    for name, a in [(n, inputs[n]) for n in _INS] + list(shape_constants().items()):
        a = np.ascontiguousarray(a)
        arrays[name] = a
        args.append(nc.dram_tensor(name, a.shape, mybir.dt.from_np(a.dtype), kind="ExternalInput").ap())
    args.append(nc.dram_tensor("out", (NB, T, D), F32, kind="ExternalOutput").ap())
    build(nc, *args)
    r = run_bass_kernel_spmd(nc, [arrays], core_ids=[0])
    return r.results[0]["out"]
```
